# Optimizing a Trainium2 kernel written in Bass

```python
import numpy as np
import jax
import jax.numpy as jnp

def _softmax(x, axis=-1):
    return jax.nn.softmax(x, axis=axis)

def _gelu(x):
    return jax.nn.gelu(x, approximate=True)

def _silu(x):
    return jax.nn.silu(x)

def _sigmoid(x):
    return jax.nn.sigmoid(x)

def _layernorm(x, axis=-1, eps=1e-05):
    m = jnp.mean(x, axis=axis, keepdims=True)
    v = jnp.var(x, axis=axis, keepdims=True)
    return (x - m) / jnp.sqrt(v + eps)

def _scatter_add(tgt, idx, src, axis=0):
    return tgt.at[idx].add(src)

def _segment_sum(src, seg, n):
    return jax.ops.segment_sum(src, seg, n)
kernel_name = 'mk_sandwich_d2_jaxref_r8_40e147'

def setup_inputs(seed: int=0):
    np.random.seed(seed)
    _w = jnp.asarray

    def _L0_attn_setup():
        import jax, jax.numpy as jnp
        import numpy as np
        B, T, C = (8, 512, 128)
        LN_EPS = 1e-05
        NEG_INF = -1e+38

        def _ln(x, g, b):
            mu = jnp.mean(x, axis=-1, keepdims=True)
            var = jnp.mean(jnp.square(x - mu), axis=-1, keepdims=True)
            return (x - mu) * jax.lax.rsqrt(var + LN_EPS) * g + b

        def _shift(x):
            return jnp.concatenate([jnp.zeros_like(x[:, :1]), x[:, :-1]], axis=1)

        def _wkv(w, u, k, v):
            kt = jnp.moveaxis(k, 1, 0)
            vt = jnp.moveaxis(v, 1, 0)
            aa = jnp.zeros(k.shape[::2], k.dtype)
            bb = jnp.zeros(k.shape[::2], k.dtype)
            pp = jnp.full(k.shape[::2], NEG_INF, k.dtype)

            def step(carry, kv):
                aa, bb, pp = carry
                kk, vv = kv
                p = jnp.maximum(pp, u + kk)
                e1 = jnp.exp(pp - p)
                e2 = jnp.exp(u + kk - p)
                y = (e1 * aa + e2 * vv) / (e1 + e2)
                p2 = jnp.maximum(pp + w, w + kk)
                e1u = jnp.exp(pp + w - p2)
                e2u = jnp.exp(w + kk - p2)
                aa = e1u * aa + e2u * vv
                bb = e1u + e2u
                pp = p2 + jnp.log(bb)
                return ((aa, bb, pp), y)
            _, ys = jax.lax.scan(step, (aa, bb, pp), (kt, vt))
            return jnp.moveaxis(ys, 0, 1)
        key = jax.random.key(seed)
        ks = jax.random.split(key, 20)
        n = lambda i, sh, s=1.0: jax.random.normal(ks[i], sh, jnp.float32) * s
        un = lambda i, sh: jax.random.uniform(ks[i], sh, jnp.float32)
        return {'x': n(0, (B, T, C)), 'w': n(1, (C,), 0.01), 'u': n(2, (C,), 0.01), 'rk': un(3, (C,)), 'rv': un(4, (C,)), 'rr': un(5, (C,)), 'crk': un(6, (C,)), 'crr': un(7, (C,)), 'Wk': n(8, (C, C), 0.02), 'Wv': n(9, (C, C), 0.02), 'Wr': n(10, (C, C), 0.02), 'Wck': n(11, (4 * C, C), 0.02), 'Wcv': n(12, (C, 4 * C), 0.02), 'Wcr': n(13, (C, C), 0.02), 'ln1_g': jnp.ones((C,)), 'ln1_b': jnp.zeros((C,)), 'ln2_g': jnp.ones((C,)), 'ln2_b': jnp.zeros((C,))}
    _L0_attn_in = _L0_attn_setup()

    def _L0_ffn_setup():
        import jax, jax.numpy as jnp
        import numpy as np
        from jax import lax
        T, B, I, M, O = (32, 64, 128, 128, 128)

        def _xavier(key, shape):
            fan_out, fan_in = shape
            limit = float(np.sqrt(6.0 / (fan_in + fan_out)))
            return jax.random.uniform(key, shape, jnp.float32, -limit, limit)
        key = jax.random.key(seed)
        ks = jax.random.split(key, 9)
        x = jax.random.normal(ks[0], (T, B, I), jnp.float32)
        return {'x': x, 'wf': _xavier(ks[1], (M, I)), 'uf': _xavier(ks[2], (M, M)), 'bf': jnp.zeros((M,), jnp.float32), 'wi': _xavier(ks[3], (M, I)), 'ui': _xavier(ks[4], (M, M)), 'bi': jnp.zeros((M,), jnp.float32), 'wc': _xavier(ks[5], (M, I)), 'uc': _xavier(ks[6], (M, M)), 'bc': jnp.zeros((M,), jnp.float32), 'wo': _xavier(ks[7], (O, I)), 'uo': _xavier(ks[8], (O, M)), 'bo': jnp.zeros((O,), jnp.float32), 'in_c': jnp.zeros((M,), jnp.float32)}
    _L0_ffn_in = _L0_ffn_setup()

    def _L1_attn_setup():
        import jax, jax.numpy as jnp
        import numpy as np
        D_MODEL = 128
        NHEAD = 16
        HEAD_DIM = D_MODEL // NHEAD
        MAX_POS = 256

        def _rope_tables(seq_len, dim):
            inv_freq = 1.0 / 10000.0 ** (jnp.arange(0, dim, 2, dtype=jnp.float32) / dim)
            t = jnp.arange(seq_len, dtype=jnp.float32)[:, None]
            freqs = t * inv_freq[None, :]
            emb = jnp.concatenate([freqs, freqs], axis=-1)
            return (jnp.cos(emb), jnp.sin(emb))

        def _rotate_half(x):
            x1, x2 = jnp.split(x, 2, axis=-1)
            return jnp.concatenate([-x2, x1], axis=-1)

        def _apply_rope(x, cos, sin):
            c = cos[None, :, None, :]
            s = sin[None, :, None, :]
            return x * c + _rotate_half(x) * s
        key = jax.random.key(seed)
        ks = jax.random.split(key, 9)
        B, L, D = (4, 256, D_MODEL)
        lim = 1.0 / np.sqrt(D)

        def lin(k):
            kw, kb = jax.random.split(k)
            W = jax.random.uniform(kw, (D, D), jnp.float32, -lim, lim)
            b = jax.random.uniform(kb, (D,), jnp.float32, -lim, lim)
            return (W, b)
        Wq, bq = lin(ks[0])
        Wk, bk = lin(ks[1])
        Wv, bv = lin(ks[2])
        Wo, bo = lin(ks[3])
        x = jax.random.normal(ks[4], (B, L, D), jnp.float32)
        return {'x': x, 'Wq': Wq, 'bq': bq, 'Wk': Wk, 'bk': bk, 'Wv': Wv, 'bv': bv, 'Wo': Wo, 'bo': bo}
    _L1_attn_in = _L1_attn_setup()

    def _L1_ffn_setup():
        import jax, jax.numpy as jnp
        import numpy as np
        TOP_K = 2
        key = jax.random.key(seed)
        k0, k1, k2, k3, k4 = jax.random.split(key, 5)
        B, S, H, I, E = (4, 256, 128, 352, 8)
        s_h = 1.0 / np.sqrt(H)
        s_i = 1.0 / np.sqrt(I)
        return {'x': jax.random.normal(k0, (B, S, H), jnp.float32), 'w_router': jax.random.normal(k1, (E, H), jnp.float32) * s_h, 'w_gate': jax.random.normal(k2, (E, I, H), jnp.float32) * s_h, 'w_up': jax.random.normal(k3, (E, I, H), jnp.float32) * s_h, 'w_down': jax.random.normal(k4, (E, H, I), jnp.float32) * s_i}
    _L1_ffn_in = _L1_ffn_setup()
    _d = {'L0_attn_x': _L0_attn_in['x'], 'L0_attn_w': _L0_attn_in['w'], 'L0_attn_u': _L0_attn_in['u'], 'L0_attn_rk': _L0_attn_in['rk'], 'L0_attn_rv': _L0_attn_in['rv'], 'L0_attn_rr': _L0_attn_in['rr'], 'L0_attn_crk': _L0_attn_in['crk'], 'L0_attn_crr': _L0_attn_in['crr'], 'L0_attn_Wk': _L0_attn_in['Wk'], 'L0_attn_Wv': _L0_attn_in['Wv'], 'L0_attn_Wr': _L0_attn_in['Wr'], 'L0_attn_Wck': _L0_attn_in['Wck'], 'L0_attn_Wcv': _L0_attn_in['Wcv'], 'L0_attn_Wcr': _L0_attn_in['Wcr'], 'L0_attn_ln1_g': _L0_attn_in['ln1_g'], 'L0_attn_ln1_b': _L0_attn_in['ln1_b'], 'L0_attn_ln2_g': _L0_attn_in['ln2_g'], 'L0_attn_ln2_b': _L0_attn_in['ln2_b'], 'L0_ffn_wf': _L0_ffn_in['wf'], 'L0_ffn_uf': _L0_ffn_in['uf'], 'L0_ffn_bf': _L0_ffn_in['bf'], 'L0_ffn_wi': _L0_ffn_in['wi'], 'L0_ffn_ui': _L0_ffn_in['ui'], 'L0_ffn_bi': _L0_ffn_in['bi'], 'L0_ffn_wc': _L0_ffn_in['wc'], 'L0_ffn_uc': _L0_ffn_in['uc'], 'L0_ffn_bc': _L0_ffn_in['bc'], 'L0_ffn_wo': _L0_ffn_in['wo'], 'L0_ffn_uo': _L0_ffn_in['uo'], 'L0_ffn_bo': _L0_ffn_in['bo'], 'L0_ffn_in_c': _L0_ffn_in['in_c'], 'L1_attn_Wq': _L1_attn_in['Wq'], 'L1_attn_bq': _L1_attn_in['bq'], 'L1_attn_Wk': _L1_attn_in['Wk'], 'L1_attn_bk': _L1_attn_in['bk'], 'L1_attn_Wv': _L1_attn_in['Wv'], 'L1_attn_bv': _L1_attn_in['bv'], 'L1_attn_Wo': _L1_attn_in['Wo'], 'L1_attn_bo': _L1_attn_in['bo'], 'L1_ffn_w_router': _L1_ffn_in['w_router'], 'L1_ffn_w_gate': _L1_ffn_in['w_gate'], 'L1_ffn_w_up': _L1_ffn_in['w_up'], 'L1_ffn_w_down': _L1_ffn_in['w_down']}
    _x0 = _d['L0_attn_x']
    _d['L0_attn_x'] = jax.random.normal(jax.random.fold_in(jax.random.key(seed), 1), (2, 1024, 128), dtype=_x0.dtype)
    del _x0
    return _d

def reference(L0_attn_x, L0_attn_w, L0_attn_u, L0_attn_rk, L0_attn_rv, L0_attn_rr, L0_attn_crk, L0_attn_crr, L0_attn_Wk, L0_attn_Wv, L0_attn_Wr, L0_attn_Wck, L0_attn_Wcv, L0_attn_Wcr, L0_attn_ln1_g, L0_attn_ln1_b, L0_attn_ln2_g, L0_attn_ln2_b, L0_ffn_wf, L0_ffn_uf, L0_ffn_bf, L0_ffn_wi, L0_ffn_ui, L0_ffn_bi, L0_ffn_wc, L0_ffn_uc, L0_ffn_bc, L0_ffn_wo, L0_ffn_uo, L0_ffn_bo, L0_ffn_in_c, L1_attn_Wq, L1_attn_bq, L1_attn_Wk, L1_attn_bk, L1_attn_Wv, L1_attn_bv, L1_attn_Wo, L1_attn_bo, L1_ffn_w_router, L1_ffn_w_gate, L1_ffn_w_up, L1_ffn_w_down):

    def _L0_attn_ref(x, w, u, rk, rv, rr, crk, crr, Wk, Wv, Wr, Wck, Wcv, Wcr, ln1_g, ln1_b, ln2_g, ln2_b):
        import jax, jax.numpy as jnp
        import numpy as np
        B, T, C = (8, 512, 128)
        LN_EPS = 1e-05
        NEG_INF = -1e+38

        def _ln(x, g, b):
            mu = jnp.mean(x, axis=-1, keepdims=True)
            var = jnp.mean(jnp.square(x - mu), axis=-1, keepdims=True)
            return (x - mu) * jax.lax.rsqrt(var + LN_EPS) * g + b

        def _shift(x):
            return jnp.concatenate([jnp.zeros_like(x[:, :1]), x[:, :-1]], axis=1)

        def _wkv(w, u, k, v):
            kt = jnp.moveaxis(k, 1, 0)
            vt = jnp.moveaxis(v, 1, 0)
            aa = jnp.zeros(k.shape[::2], k.dtype)
            bb = jnp.zeros(k.shape[::2], k.dtype)
            pp = jnp.full(k.shape[::2], NEG_INF, k.dtype)

            def step(carry, kv):
                aa, bb, pp = carry
                kk, vv = kv
                p = jnp.maximum(pp, u + kk)
                e1 = jnp.exp(pp - p)
                e2 = jnp.exp(u + kk - p)
                y = (e1 * aa + e2 * vv) / (e1 + e2)
                p2 = jnp.maximum(pp + w, w + kk)
                e1u = jnp.exp(pp + w - p2)
                e2u = jnp.exp(w + kk - p2)
                aa = e1u * aa + e2u * vv
                bb = e1u + e2u
                pp = p2 + jnp.log(bb)
                return ((aa, bb, pp), y)
            _, ys = jax.lax.scan(step, (aa, bb, pp), (kt, vt))
            return jnp.moveaxis(ys, 0, 1)
        xa = _ln(x, ln1_g, ln1_b)
        xp = _shift(xa)
        xk = xa * rk + xp * (1.0 - rk)
        xv = xa * rv + xp * (1.0 - rv)
        xr = xa * rr + xp * (1.0 - rr)
        k = jnp.einsum('btc,dc->btd', xk, Wk)
        v = jnp.einsum('btc,dc->btd', xv, Wv)
        r = jnp.einsum('btc,dc->btd', xr, Wr)
        wkv = _wkv(w, u, k, v)
        x1 = x + jax.nn.sigmoid(r) * wkv
        xb = _ln(x1, ln2_g, ln2_b)
        xpb = _shift(xb)
        xck = xb * crk + xpb * (1.0 - crk)
        xcr = xb * crr + xpb * (1.0 - crr)
        kc = jnp.square(jax.nn.relu(jnp.einsum('btc,dc->btd', xck, Wck)))
        vc = jnp.einsum('bth,dh->btd', kc, Wcv)
        out = x1 + jax.nn.sigmoid(jnp.einsum('btc,dc->btd', xcr, Wcr)) * vc
        return out

    def _L0_ffn_ref(x, wf, uf, bf, wi, ui, bi, wc, uc, bc, wo, uo, bo, in_c):
        import jax, jax.numpy as jnp
        import numpy as np
        from jax import lax
        T, B, I, M, O = (32, 64, 128, 128, 128)

        def _xavier(key, shape):
            fan_out, fan_in = shape
            limit = float(np.sqrt(6.0 / (fan_in + fan_out)))
            return jax.random.uniform(key, shape, jnp.float32, -limit, limit)
        batch = x.shape[1]
        c0 = jnp.broadcast_to(in_c, (batch, in_c.shape[0]))

        def step(c, xt):
            ft = jax.nn.sigmoid(xt @ wf.T + c @ uf.T + bf)
            it = jax.nn.sigmoid(xt @ wi.T + c @ ui.T + bi)
            gt = jnp.tanh(xt @ wc.T + c @ uc.T + bc)
            c = ft * c + it * gt
            return (c, None)
        c_final, _ = lax.scan(step, c0, x)
        h = jnp.tanh(jnp.einsum('tbi,oi->tbo', x, wo) + c_final @ uo.T + bo)
        return h

    def _L1_attn_ref(x, Wq, bq, Wk, bk, Wv, bv, Wo, bo):
        import jax, jax.numpy as jnp
        import numpy as np
        D_MODEL = 128
        NHEAD = 16
        HEAD_DIM = D_MODEL // NHEAD
        MAX_POS = 256

        def _rope_tables(seq_len, dim):
            inv_freq = 1.0 / 10000.0 ** (jnp.arange(0, dim, 2, dtype=jnp.float32) / dim)
            t = jnp.arange(seq_len, dtype=jnp.float32)[:, None]
            freqs = t * inv_freq[None, :]
            emb = jnp.concatenate([freqs, freqs], axis=-1)
            return (jnp.cos(emb), jnp.sin(emb))

        def _rotate_half(x):
            x1, x2 = jnp.split(x, 2, axis=-1)
            return jnp.concatenate([-x2, x1], axis=-1)

        def _apply_rope(x, cos, sin):
            c = cos[None, :, None, :]
            s = sin[None, :, None, :]
            return x * c + _rotate_half(x) * s
        B, L, D = x.shape
        H, hd = (NHEAD, HEAD_DIM)
        q = (x @ Wq.T + bq).reshape(B, L, H, hd)
        k = (x @ Wk.T + bk).reshape(B, L, H, hd)
        v = (x @ Wv.T + bv).reshape(B, L, H, hd)
        cos, sin = _rope_tables(L, hd)
        q = _apply_rope(q, cos, sin)
        k = _apply_rope(k, cos, sin)
        scores = jnp.einsum('bqhd,bkhd->bhqk', q, k) / np.sqrt(hd).astype(np.float32)
        attn = jax.nn.softmax(scores, axis=-1)
        out = jnp.einsum('bhqk,bkhd->bqhd', attn, v).reshape(B, L, D)
        return out @ Wo.T + bo

    def _L1_ffn_ref(x, w_router, w_gate, w_up, w_down):
        import jax, jax.numpy as jnp
        import numpy as np
        TOP_K = 2
        B, S, H = x.shape
        E = w_router.shape[0]
        xf = x.reshape(-1, H)
        logits = jnp.einsum('th,eh->te', xf, w_router)
        probs = jax.nn.softmax(logits, axis=-1)
        topw, topi = jax.lax.top_k(probs, TOP_K)
        topw = topw / jnp.sum(topw, axis=-1, keepdims=True)
        onehot = (topi[..., None] == jnp.arange(E)).astype(x.dtype)
        combine = jnp.einsum('tk,tke->te', topw, onehot)
        gate = jax.nn.silu(jnp.einsum('th,eih->eti', xf, w_gate))
        up = jnp.einsum('th,eih->eti', xf, w_up)
        down = jnp.einsum('eti,ehi->eth', gate * up, w_down)
        out = jnp.einsum('eth,te->th', down, combine)
        return out.reshape(B, S, H)
    x = L0_attn_x
    x = x + _layernorm(_L0_attn_ref(_layernorm(x, axis=-1), L0_attn_w, L0_attn_u, L0_attn_rk, L0_attn_rv, L0_attn_rr, L0_attn_crk, L0_attn_crr, L0_attn_Wk, L0_attn_Wv, L0_attn_Wr, L0_attn_Wck, L0_attn_Wcv, L0_attn_Wcr, L0_attn_ln1_g, L0_attn_ln1_b, L0_attn_ln2_g, L0_attn_ln2_b), axis=-1)
    x = x + _layernorm(_L0_ffn_ref(_layernorm(x, axis=-1), L0_ffn_wf, L0_ffn_uf, L0_ffn_bf, L0_ffn_wi, L0_ffn_ui, L0_ffn_bi, L0_ffn_wc, L0_ffn_uc, L0_ffn_bc, L0_ffn_wo, L0_ffn_uo, L0_ffn_bo, L0_ffn_in_c), axis=-1)
    x = x + _layernorm(_L1_attn_ref(_layernorm(x, axis=-1), L1_attn_Wq, L1_attn_bq, L1_attn_Wk, L1_attn_bk, L1_attn_Wv, L1_attn_bv, L1_attn_Wo, L1_attn_bo), axis=-1)
    x = x + _layernorm(_L1_ffn_ref(_layernorm(x, axis=-1), L1_ffn_w_router, L1_ffn_w_gate, L1_ffn_w_up, L1_ffn_w_down), axis=-1)
    return x

_drawn_inputs = setup_inputs


def setup_inputs(seed=0):
    import zlib

    import numpy as np

    out = dict(_drawn_inputs(seed))
    spreads = {'L0_attn_ln1_g': (1.0, 0.2),
     'L0_attn_ln1_b': (0.0, 0.1),
     'L0_attn_ln2_g': (1.0, 0.6),
     'L0_attn_ln2_b': (0.0, 0.466),
     'L0_ffn_bf': (0.0, 0.508),
     'L0_ffn_bi': (0.0, 0.32),
     'L0_ffn_bc': (0.0, 0.1),
     'L0_ffn_bo': (0.0, 0.1),
     'L0_ffn_in_c': (0.0, 0.1)}
    factors = {'L0_attn_u': 200.0,
     'L0_attn_rr': 3.283,
     'L0_attn_crk': 3.259,
     'L0_attn_crr': 5.829,
     'L0_attn_Wcr': 4.539,
     'L1_attn_bq': 2.95,
     'L1_attn_bk': 4.766}
    for name, (base, spread) in spreads.items():
        noise = np.random.default_rng([zlib.crc32(name.encode()), seed]).standard_normal(out[name].shape)
        drawn = base * np.exp(spread * noise) if base else spread * noise
        out[name] = jnp.asarray(drawn.astype(out[name].dtype))
    for name, factor in factors.items():
        out[name] = (out[name] * factor).astype(out[name].dtype)
    return out
```

```python
from contextlib import ExitStack

import concourse.bass as bass
from concourse import mybir

ALU = mybir.AluOpType
ACT = mybir.ActivationFunctionType
AXX = mybir.AxisListType.X
F32 = mybir.dt.float32
BF16 = mybir.dt.bfloat16
I32 = mybir.dt.int32
U32 = mybir.dt.uint32

B, T, C = 2, 1024, 128
P = 128
NT = B * T // P
TB = T // P
CH = 512
NCH = B * T // CH
QPB = T // CH
TPC = CH // P
H, D = 16, 8
HG = 4
NG = H // HG
E, FI = 8, 352
FIP = 384
NF = FIP // P
LN_EPS = 1e-5
NEG = -1e38
SCALE = float(D) ** -0.5

BLOCKS = ["wk", "wv", "wr", "wcr", "wck0", "wck1", "wck2", "wck3", "wcv0", "wcv1", "wcv2", "wcv3", "ident",
          "wf", "wi", "wc", "uf", "ui", "uc", "wo", "uo", "aq", "aqr", "ak", "akr", "av", "ao", "row0"]
VECS = ["w", "u", "rk", "rv", "rr", "crk", "crr", "g1", "b1", "g2", "b2", "bf", "bi", "bc", "in_c",
        "bq", "bqr", "bk", "bkr"] + [f"n{k}" for k in range(8)]
ROWS = ["bo", "bv", "bao"]
Q_PART = (0, 0, 0, 1, 1, 2)
K_PART = (0, 1, 2, 0, 1, 0)
NP6 = len(Q_PART)
STK = D * NP6
NPT = 8
GROUPS = B * NG
UNITS = TB * HG
MROW = 96


def sandwich_kernel(nc, x_in, wt_in, vec_in, rows_in, cos_in, sin_in, wg_in, wu_in, wd_in, wrt_in, out):
    ctx = ExitStack()
    with ctx:
        def sb(name, shape, dt=F32):
            return ctx.enter_context(nc.sbuf_tensor(name, shape, dt))

        sems = {}

        def S(name):
            if name not in sems:
                sems[name] = ctx.enter_context(nc.semaphore(name))
            return sems[name]

        X = sb("X", [P, NT, C])
        XN = sb("XN", [P, NT, C])
        TM = sb("TM", [P, NT, C])
        CT = sb("CT", [P, B * T])
        XS = sb("XS", [P, B, T + 1])
        WT = sb("WT", [P, len(BLOCKS) * P])
        VEC = sb("VEC", [P, len(VECS)])
        ROW = sb("ROW", [P, len(ROWS) * P])
        OMV = sb("OMV", [P, 8])
        WMA = sb("WMA", [P, 8 * P])
        WMB = sb("WMB", [P, 8 * P])
        COS = sb("COS", [P, T])
        SIN = sb("SIN", [P, T])
        WG = sb("WG", [P, E, FI])
        WU = sb("WU", [P, E, FI])
        WD = sb("WD", [P, E, NF, C])
        WRT = sb("WRT", [P, E])
        ST = sb("ST", [P, NT, 6])
        MV = sb("MV", [P, NT, 2])
        RS = sb("RS", [P, NT])
        RS2 = sb("RS2", [P, NT])
        NV = sb("NV", [P, NT])
        NI = sb("NI", [P, NT], I32)
        ND = sb("ND", [P, NT])
        GB0 = sb("GB0", [P, 4])
        ARENA = sb("ARENA", [P, 96 * 256])

        ps01 = [ctx.enter_context(nc.psum_tensor(f"bank{i}", [P, CH], F32)) for i in range(2)]
        PSP = [ctx.enter_context(nc.psum_tensor(f"banks{2 + 2 * i}", [P, 2 * CH], F32)) for i in range(2)]
        ps67 = [ctx.enter_context(nc.psum_tensor(f"bank{6 + i}", [P, CH], F32)) for i in range(2)]
        PS = [p[:, :] for p in PSP]
        bank = [ps01[0][:, :], ps01[1][:, :], PSP[0][:, 0:CH], PSP[0][:, CH:], PSP[1][:, 0:CH], PSP[1][:, CH:],
                ps67[0][:, :], ps67[1][:, :]]

        def blk(name):
            k = BLOCKS.index(name)
            return WT[:, k * P:(k + 1) * P]

        def vec(name):
            k = VECS.index(name)
            return VEC[:, k:k + 1]

        def row(name):
            k = ROWS.index(name)
            return ROW[:, k * P:(k + 1) * P]

        ident = blk("ident")

        def arena(kib, n, dt=F32):
            v = ARENA[:, kib * 256:kib * 256 + n]
            return v

        Kc = [arena(0 + 4 * b, T) for b in range(B)]
        Vc = [arena(8 + 4 * b, T) for b in range(B)]
        SR = [arena(16 + 4 * b, T) for b in range(B)]
        DD = [arena(24 + 4 * b, T) for b in range(B)]
        EA = [arena(32 + 4 * b, T) for b in range(B)]
        EB = [arena(40 + 4 * b, T) for b in range(B)]
        MM = [arena(48 + 5 * b, T + 1) for b in range(B)]
        SS = [arena(58 + 5 * b, T + 1) for b in range(B)]
        AA = [arena(68 + 5 * b, T + 1) for b in range(B)]
        SG = [arena(78 + 4 * b, T) for b in range(B)]
        RL = [arena(86 + 2 * k, CH) for k in range(4)]
        KC = [arena(2 * k, CH) for k in range(8)]
        SCR = [arena(24 + 2 * k, CH) for k in range(2)]
        OUT1 = arena(32, B * T).rearrange("p (i c) -> p i c", c=C)
        FG = [arena(0 + 2 * k, CH) for k in range(4)]
        IGT = [arena(8 + 2 * k, CH) for k in range(4)]
        GG = [arena(16 + 2 * k, CH) for k in range(4)]
        CST = [arena(24 + 4 * k, T) for k in range(2)]
        HH = arena(40, B * T).rearrange("p (i c) -> p i c", c=C)

        VS = ARENA[:, 0:32 * 256].rearrange("p (i h e) -> p i h e", h=H, e=32)
        PT = [arena(32 + 4 * k, T) for k in range(NPT)]
        RT1 = [arena(48 + 2 * k, CH) for k in range(2)]
        RT2 = [arena(52 + 2 * k, CH) for k in range(2)]
        PARTS = [ARENA[:, (56 + 3 * k) * 256:(59 + 3 * k) * 256].bitcast(BF16).rearrange("p (s t) -> p s t", s=3)
                 for k in range(2)]
        QS = ARENA[:, 64 * 256:80 * 256].bitcast(BF16).rearrange("p (s h t) -> p s h t", s=2, h=HG)
        KS = ARENA[:, 80 * 256:96 * 256].bitcast(BF16).rearrange("p (s h t) -> p s h t", s=2, h=HG)
        OT = XN
        OE = XS[:, :, :].rearrange("p b t -> p (b t)")[:, 0:T]
        IDB = sb("IDB", [P, P], BF16)
        MX = sb("MX", [P, HG * TB, QPB])
        MQ = sb("MQ", [P, HG * TB])
        MR = sb("MR", [P, HG * TB])
        M3 = sb("M3", [P, 3, HG * TB], BF16)
        M3T = sb("M3T", [3 * HG * TB, P], BF16)
        RDEN = sb("RDEN", [P, QPB, TPC, HG])
        QD = nc.dram_tensor("q_stacks", (P, NP6, B * T), BF16, kind="Internal").ap()
        KD = nc.dram_tensor("k_stacks", (P, NP6, B * T), BF16, kind="Internal").ap()
        SL = [arena(0 + 2 * k, FI) for k in range(2)]
        HB = [arena(4 + 2 * k, FIP) for k in range(2)]
        HT = [arena(8 + 2 * k, FIP) for k in range(2)]
        YO = arena(12, B * T).rearrange("p (i c) -> p i c", c=C)
        LG = sb("LG", [P, NT, E])
        TOP = sb("TOP", [P, NT, 8])
        TIX = sb("TIX", [P, NT, 8], U32)
        TIF = sb("TIF", [P, NT, 2])
        W12 = sb("W12", [P, NT, 2])
        CMB = sb("CMB", [P, NT, E])
        CM2 = sb("CM2", [P, NT, E])

        def side_work(g):
            at = [[] for _ in range(UNITS)]
            if g + 1 < GROUPS:
                todo = [("scores", g + 1, j, qt, kk) for j in range(HG) for qt in range(TB) for kk in range(QPB)]
                last = 26
                for k, op in enumerate(todo):
                    at[k * last // len(todo)].append(op)
                at[29].append(("maxima", g + 1))
            if g >= 1:
                at[9].append(("output", g - 1, 0))
                at[10].append(("output", g - 1, 1))
            return at

        FIRST_SIDE = [("scores", 0, j, qt, kk) for j in range(HG) for qt in range(TB) for kk in range(QPB)]
        FIRST_SIDE += [("maxima", 0)]
        LAST_SIDE = [("output", GROUPS - 1, 0), ("output", GROUPS - 1, 1)]
        every = FIRST_SIDE + [op for g in range(GROUPS) for ops in side_work(g) for op in ops] + LAST_SIDE
        side_at = {op: k for k, op in enumerate(every)}

        block = ctx.enter_context(nc.Block())

        class Steps:

            def __init__(self, eng, name):
                self.eng, self.sem, self.n = eng, S(name), 0

            def __call__(self, ins):
                ins.then_inc(self.sem, 1)
                self.n += 1

            def sync(self):
                self.eng.wait_ge(self.sem, self.n)

        @block.sync
        def _(sp):
            xv = x_in.rearrange("b (i p) c -> b p i c", p=P)
            n0 = BLOCKS.index("wf") * P
            sp.dma_start(X[:, 0:TB, :], xv[0]).then_inc(S("x_loaded0"), 16)
            sp.dma_start(VEC[:, :], vec_in).then_inc(S("vec_loaded"), 16)
            sp.dma_start(WT[:, 0:n0], wt_in[:, 0:n0]).then_inc(S("w1_loaded"), 16)
            sp.dma_start(X[:, TB:NT, :], xv[1]).then_inc(S("x_loaded1"), 16)
            sp.dma_start(WT[:, n0:], wt_in[:, n0:]).then_inc(S("w2_loaded"), 16)
            sp.dma_start(ROW[:, :], rows_in).then_inc(S("w2_loaded"), 16)
            sp.dma_start(COS[:, :], cos_in).then_inc(S("rope_loaded"), 16)
            sp.dma_start(SIN[:, :], sin_in).then_inc(S("rope_loaded"), 16)
            sp.dma_start(WG[:, :, :], wg_in).then_inc(S("moe_loaded"), 16)
            sp.dma_start(WU[:, :, :], wu_in).then_inc(S("moe_loaded"), 16)
            sp.dma_start(WD[:, :, :, :], wd_in).then_inc(S("moe_loaded"), 16)
            sp.dma_start(WRT[:, :], wrt_in).then_inc(S("moe_loaded"), 16)
            for n in range(2 * NCH):
                c, side = n // 2, n % 2
                sp.wait_ge(S("parts_ready"), n + 1)
                ts = slice(c * CH, (c + 1) * CH)
                src, dst = PARTS[n % 2], (QD, KD)[side]
                at = 0
                for k in (3, 2, 1):
                    if side == 0:
                        s1 = src[:, 3 - k:4 - k, :].to_broadcast([P, k, CH])
                    else:
                        s1 = src[:, 0:k, :]
                    sp.dma_start(dst[:, at:at + k, ts], s1).then_inc(S(f"parts_stored{n % 2}"), 16)
                    at += k

            def load_stacks(g):
                b, h0, slot = g // NG, g % NG * HG, g % 2
                ts = slice(b * T, (b + 1) * T)
                for dst, src in ((QS, QD), (KS, KD)):
                    v = src.rearrange("(h d) s t -> h (d s) t", d=D)[h0:h0 + HG, :, ts].rearrange("h r t -> r h t")
                    sp.dma_start(dst[0:STK, slot, :, :], v).then_inc(S(f"stacks_loaded{slot}"), 16)

            def place_maxima(g):
                sp.wait_ge(S("side_used"), side_at[("maxima", g)] + 1)
                for k in range(3):
                    dst = QS[MROW + k:MROW + k + 1, g % 2, :, :].rearrange("p h (t q) -> p (h t) q", q=P)
                    sp.dma_start(dst, M3T[k * HG * TB:(k + 1) * HG * TB, :]).then_inc(S("maxima_placed"), 16)

            sp.wait_ge(S("stacks_cleared"), 1)
            for k in range(2):
                sp.wait_ge(S(f"parts_stored{k}"), 48 * NCH)
            load_stacks(0)
            load_stacks(1)
            place_maxima(0)
            for g in range(GROUPS):
                if g + 1 < GROUPS:
                    place_maxima(g + 1)
                if g + 2 < GROUPS:
                    sp.wait_ge(S("scores_filled"), UNITS * (g + 1))
                    load_stacks(g + 2)
            ov = out.rearrange("b (i p) c -> b p i c", p=P)
            for b in range(B):
                sp.wait_ge(S(f"x_done{b}"), 1)
                sp.dma_start(ov[b], X[:, b * TB:(b + 1) * TB, :]).then_inc(S("out_stored"), 16)
            sp.wait_ge(S("out_stored"), 32)

        @block.gpsimd
        def _(pool):
            st = Steps(pool, "pool_steps")
            st(pool.memset(XS[:, :, 0:1], 0.0))
            for b in range(B):
                st(pool.memset(MM[b][:, 0:1], NEG))
                st(pool.memset(SS[b][:, 0:1], 1.0))
                last = pool.memset(AA[b][:, 0:1], 0.0)
                if b == B - 1:
                    last.then_inc(S("scan_starts_set"), 1)
                else:
                    st(last)
            pool.wait_ge(S("vec_loaded"), 16)
            pool.wait_ge(S("w1_loaded"), 16)
            for k, name in enumerate(("rk", "rv", "rr", "crr", "crk")):
                st(pool.tensor_scalar(OMV[:, k:k + 1], vec(name), -1.0, 1.0, ALU.mult, ALU.add))
            st.sync()
            for k, name in enumerate(("rk", "rv", "rr", "crr")):
                pool.tensor_scalar(WMA[:, k * P:(k + 1) * P], WT[:, k * P:(k + 1) * P], vec(name), None, ALU.mult)
                pool.tensor_scalar(WMB[:, k * P:(k + 1) * P], WT[:, k * P:(k + 1) * P], OMV[:, k:k + 1], None,
                                   ALU.mult).then_inc(S("mix_scaled"), 1)
            pool.tensor_scalar(WMA[:, 4 * P:8 * P], WT[:, 4 * P:8 * P], vec("crk"), None, ALU.mult)
            pool.tensor_scalar(WMB[:, 4 * P:8 * P], WT[:, 4 * P:8 * P], OMV[:, 4:5], None,
                               ALU.mult).then_inc(S("mix_scaled"), 1)
            pool.wait_ge(S("w1_loaded"), 16)
            pool.tensor_copy(IDB[:, :], ident).then_inc(S("ident_bf16"), 1)
            pool.wait_ge(S("kc_ready"), 4 * NCH)
            st(pool.memset(ARENA[:, 64 * 256:96 * 256], 0.0))
            st.sync()
            pool.memset(KS[MROW:MROW + 3, :, :, :], 1.0).then_inc(S("stacks_cleared"), 1)
            pool.wait_ge(S("stacks_cleared"), 1)
            pool.wait_ge(S("h_filled"), NCH)
            st(pool.memset(ARENA[:, 0:32 * 256], 0.0))
            st.sync()
            pool.memset(VS[:, :, :, D:D + 1], 1.0).then_inc(S("v_cleared"), 1)

        @block.vector
        def _(dve):
            st = Steps(dve, "dve_steps")

            def stats(tiles, src):
                for i in tiles:
                    st(dve.bn_stats(ST[:, i, :], src(i)))
                st.sync()
                for i in tiles:
                    st(dve.bn_aggr(MV[:, i, :], ST[:, i, :]))
                st.sync()

            def rsqrt(dst, var, tiles):
                lo, hi = tiles[0], tiles[-1] + 1
                v, g, d, y = NV[:, lo:hi], NI[:, lo:hi], ND[:, lo:hi], dst[:, lo:hi]
                st(dve.tensor_scalar(v, var, LN_EPS, None, ALU.add))
                st.sync()
                st(dve.tensor_scalar(g, v.bitcast(I32), 1, None, ALU.logical_shift_right))
                st.sync()
                st(dve.tensor_scalar(y.bitcast(I32), g, -1.0, float(0x5F3759DF), ALU.mult, ALU.add))
                st.sync()
                for _ in range(3):
                    st(dve.tensor_tensor(d, y, y, ALU.mult))
                    st.sync()
                    st(dve.scalar_tensor_tensor(out=d, in0=d, scalar=-0.5, in1=v, op0=ALU.mult, op1=ALU.mult))
                    st.sync()
                    st(dve.scalar_tensor_tensor(out=y, in0=d, scalar=1.5, in1=y, op0=ALU.add, op1=ALU.mult))
                    st.sync()

            def var_of(tiles):
                return MV[:, tiles[0]:tiles[-1] + 1, 1]

            def scaled(tiles, dst, src, r, sem=None):
                for i in tiles:
                    ins = dve.tensor_scalar(dst(i), src(i), MV[:, i, 0:1], r[:, i:i + 1], ALU.subtract, ALU.mult)
                    if sem and i == tiles[-1]:
                        ins.then_inc(S(sem), 1)
                    else:
                        st(ins)

            def tm(i):
                return TM[:, i, :]

            def xt(i):
                return X[:, i, :]

            def add_ln(b, src, nxt):
                tiles = range(b * TB, (b + 1) * TB)
                stats(tiles, src)
                rsqrt(RS, var_of(tiles), tiles)
                scaled(tiles, tm, src, RS)
                st.sync()
                ins = dve.tensor_tensor(X[:, tiles[0]:tiles[-1] + 1, :], X[:, tiles[0]:tiles[-1] + 1, :],
                                        TM[:, tiles[0]:tiles[-1] + 1, :], ALU.add)
                if nxt is None:
                    ins.then_inc(S(f"x_done{b}"), 1)
                    return
                st(ins)
                st.sync()
                stats(tiles, xt)
                rsqrt(RS, var_of(tiles), tiles)
                scaled(tiles, tm, xt, RS, nxt)

            for b in range(B):
                tiles = range(b * TB, (b + 1) * TB)
                dve.wait_ge(S(f"x_loaded{b}"), 16)
                stats(tiles, xt)
                rsqrt(RS, var_of(tiles), tiles)
                r1, r2 = RS[:, tiles[0]:tiles[-1] + 1], RS2[:, tiles[0]:tiles[-1] + 1]
                nd = ND[:, tiles[0]:tiles[-1] + 1]
                st(dve.tensor_tensor(nd, r1, r1, ALU.mult))
                st.sync()
                st(dve.tensor_tensor(nd, nd, var_of(tiles), ALU.mult))
                st.sync()
                rsqrt(RS2, nd, tiles)
                st(dve.tensor_tensor(r2, r2, r1, ALU.mult))
                st.sync()
                scaled(tiles, tm, xt, RS2, f"xa_ready{b}")
                scaled(tiles, lambda i: XN[:, i, :], xt, RS)

            dve.wait_ge(S("scan_starts_set"), 1)
            for b in range(B):
                dve.wait_ge(S("kvr_evacuated"), 6 * b + 2)
                st(dve.tensor_tensor_scan(MM[b][:, 1:], Kc[b], VEC[:, 0:1].to_broadcast([P, T]), NEG,
                                          ALU.max, ALU.add))
                st.sync()
                st(dve.tensor_tensor(DD[b], MM[b][:, 0:T], Kc[b], ALU.subtract))
                st.sync()
                st(dve.tensor_scalar(EA[b], DD[b], 0.0, None, ALU.min))
                dve.tensor_scalar(EB[b], DD[b], 0.0, None, ALU.max).then_inc(S(f"d_ready{b}"), 1)
            for b in range(B):
                dve.wait_ge(S(f"ab_exp{b}"), 1)
                dve.tensor_tensor_scan(SS[b][:, 1:], EA[b], EB[b], 1.0, ALU.mult, ALU.add)\
                   .then_inc(S(f"s_ready{b}"), 1)
            for b in range(B):
                dve.wait_ge(S(f"log_s{b}"), 1)
                st(dve.tensor_tensor(DD[b], DD[b], Kc[b], ALU.add))
                st.sync()
                st(dve.tensor_scalar(EA[b], DD[b], 0.0, None, ALU.min))
                dve.tensor_scalar(EB[b], DD[b], 0.0, None, ALU.max).then_inc(S(f"z_ready{b}"), 1)
            for b in range(B):
                dve.wait_ge(S(f"e_exp{b}"), 1)
                dve.wait_ge(S("kvr_evacuated"), 6 * b + 4)
                st(dve.tensor_tensor(EB[b], EB[b], Vc[b], ALU.mult))
                st.sync()
                st(dve.tensor_tensor_scan(AA[b][:, 1:], EA[b], EB[b], 0.0, ALU.mult, ALU.add))
                st.sync()
                st(dve.tensor_tensor(EA[b], AA[b][:, 0:T], Vc[b], ALU.subtract))
            for b in range(B):
                dve.wait_ge(S(f"sig_z{b}"), 1)
                dve.wait_ge(S("kvr_evacuated"), 6 * b + 6)
                st.sync()
                st(dve.tensor_tensor(EA[b], EA[b], SG[b], ALU.mult))
                st.sync()
                st(dve.tensor_tensor(EA[b], EA[b], Vc[b], ALU.add))
                st.sync()
                dve.tensor_tensor(EB[b], EA[b], SR[b], ALU.mult).then_inc(S(f"y_ready{b}"), 1)

            for b in range(B):
                tiles = range(b * TB, (b + 1) * TB)
                for q in range(QPB):
                    c = QPB * b + q
                    dve.wait_ge(S("y_transposed"), c + 1)
                    v = XN[:, c * TPC:(c + 1) * TPC, :]
                    st(dve.tensor_tensor(v, v, bank[c][:, :].rearrange("p (i c) -> p i c", c=C), ALU.add))
                st.sync()
                stats(tiles, lambda i: XN[:, i, :])
                rsqrt(RS, var_of(tiles), tiles)
                scaled(tiles, tm, lambda i: XN[:, i, :], RS, f"xb_ready{b}")

            def mix_out(c):
                dve.wait_ge(S("cr_sigmoid"), c + 1)
                dve.wait_ge(S("vc_ready"), c + 1)
                o = OUT1[:, c * TPC:(c + 1) * TPC, :]
                dve.tensor_tensor(o, SCR[c % 2].rearrange("p (i c) -> p i c", c=C),
                                  bank[4 + c % 2][:, :].rearrange("p (i c) -> p i c", c=C), ALU.mult)\
                   .then_inc(S("vc_used"), 1)
                dve.wait_ge(S("vc_used"), c + 1)
                st(dve.tensor_tensor(o, o, XN[:, c * TPC:(c + 1) * TPC, :], ALU.add))

            for c in range(NCH + 1):
                if c < NCH:
                    for j in range(4):
                        m = 4 * c + j
                        dve.wait_ge(S("relu_done"), m + 1)
                        if m >= 8:
                            dve.wait_ge(S("vc_ready"), c - 1)
                        dve.tensor_tensor(KC[m % 8], RL[m % 4], RL[m % 4], ALU.mult).then_inc(S("kc_ready"), 1)
                if c >= 1:
                    mix_out(c - 1)
                if c in (QPB, 2 * QPB):
                    st.sync()
                    add_ln(c // QPB - 1, lambda i: OUT1[:, i, :], f"l_in_ready{c // QPB - 1}")

            dve.wait_ge(S("uc0_ready"), 1)
            dve.tensor_tensor(GB0[:, 0:3], bank[7][:, 0:3], VEC[:, VECS.index("bf"):VECS.index("bf") + 3],
                              ALU.add).then_inc(S("gate_bias_ready"), 1)
            for t in range(B):
                for q in range(QPB):
                    k = QPB * t + q
                    dve.wait_ge(S("gates_done"), 3 * k + 3)
                    st(dve.tensor_tensor(IGT[k], IGT[k], GG[k], ALU.mult))
                    new = CST[t][:, q * CH:(q + 1) * CH]
                    if t == 0:
                        st.sync()
                        dve.scalar_tensor_tensor(out=new, in0=FG[k], scalar=vec("in_c"), in1=IGT[k], op0=ALU.mult,
                                                 op1=ALU.add).then_inc(S("cell_ready"), 1)
                    else:
                        st(dve.tensor_tensor(FG[k], FG[k], CST[0][:, q * CH:(q + 1) * CH], ALU.mult))
                        st.sync()
                        dve.tensor_tensor(new, FG[k], IGT[k], ALU.add).then_inc(S("cell_ready"), 1)
            for b in range(B):
                dve.wait_ge(S("h_ready"), QPB * (b + 1))
                add_ln(b, lambda i: HH[:, i, :], f"a_in_ready{b}")
            dve.wait_ge(S("rope_loaded"), 32)
            for c in range(NCH):
                cs = slice(c % QPB * CH, (c % QPB + 1) * CH)
                for side in range(2):
                    n = 2 * c + side
                    names = (("bq", "bqr"), ("bk", "bkr"))[side]
                    t1, t2, parts = RT1[n % 2], RT2[n % 2], PARTS[n % 2]
                    for k, (dst, tab) in enumerate(((t1, COS), (t2, SIN))):
                        m = 2 * n + k
                        dve.wait_ge(S("qk_filled"), m + 1)
                        dve.scalar_tensor_tensor(out=dst, in0=bank[m % 8][:, :], scalar=vec(names[k]),
                                                 in1=tab[:, cs], op0=ALU.add, op1=ALU.mult)\
                           .then_inc(S("qk_used"), 1)
                    dve.wait_ge(S("qk_used"), 2 * n + 2)
                    dve.tensor_tensor(t1, t1, t2, ALU.add).then_inc(S("roped"), 1)
                    dve.wait_ge(S("part0_ready"), n + 1)
                    dve.tensor_tensor(t2, t1, parts[:, 0, :], ALU.subtract).then_inc(S("rest_ready"), 1)
                    dve.wait_ge(S("part1_ready"), n + 1)
                    dve.tensor_tensor(parts[:, 2, :], t2, parts[:, 1, :], ALU.subtract)\
                       .then_inc(S("parts_ready"), 1)

            def side(op):
                n = side_at[op]
                dve.wait_ge(S("side_filled"), n + 1)
                o = bank[n % 2]
                if op[0] == "scores":
                    _, g, j, qt, kk = op
                    dve.tensor_reduce(MX[:, j * TB + qt, kk:kk + 1], o[:, :], AXX, ALU.max)\
                       .then_inc(S("side_used"), 1)
                    if (j, qt, kk) == (HG - 1, TB - 1, QPB - 1):
                        dve.wait_ge(S("side_used"), n + 1)
                        st(dve.tensor_tensor(MQ[:, :], MX[:, :, 0], MX[:, :, 1], ALU.max))
                        st.sync()
                        st(dve.tensor_scalar(M3[:, 0, :], MQ[:, :], -1.0, None, ALU.mult))
                        st.sync()
                        st(dve.scalar_tensor_tensor(out=MR[:, :], in0=MQ[:, :], scalar=-1.0, in1=M3[:, 0, :],
                                                    op0=ALU.mult, op1=ALU.subtract))
                        st.sync()
                        st(dve.tensor_copy(M3[:, 1, :], MR[:, :]))
                        st.sync()
                        dve.tensor_tensor(M3[:, 2, :], MR[:, :], M3[:, 1, :], ALU.subtract)\
                           .then_inc(S("maxima_ready"), 1)
                elif op[0] == "maxima":
                    if op[1] >= 1:
                        dve.wait_ge(S("maxima_placed"), 48 * op[1])
                    dve.tensor_copy(M3T[:, :], o[:, :].bitcast(BF16)[0:3 * HG * TB, 0:P]).then_inc(S("side_used"), 1)
                else:
                    _, g, half = op
                    b, h0 = g // NG, g % NG * HG
                    v = o[:, :].rearrange("p (t j e) -> p t j e", j=HG, e=32)
                    st(dve.reciprocal(RDEN[:, half, :, :], v[:, :, :, D]))
                    st.sync()
                    i0 = b * TB + half * TPC
                    dst = OT[:, i0:i0 + TPC, h0 * D:(h0 + HG) * D].rearrange("p t (j d) -> p t j d", d=D)
                    dve.tensor_tensor(dst, v[:, :, :, 0:D], RDEN[:, half, :, :].unsqueeze(3).to_broadcast([P, TPC, HG, D]),
                                      ALU.mult).then_inc(S("side_used"), 1)

            for op in FIRST_SIDE:
                side(op)
            for g in range(GROUPS):
                for ops in side_work(g):
                    for op in ops:
                        side(op)
            for op in LAST_SIDE:
                side(op)

            for b in range(B):
                dve.wait_ge(S("proj_filled"), QPB * (b + 1))
                add_ln(b, lambda i: bank[4 + i // TPC][:, i % TPC * P:(i % TPC + 1) * P], f"m_in_ready{b}")

            for b in range(B):
                ts = slice(b * TB, (b + 1) * TB)
                dve.wait_ge(S("router_filled"), b + 1)
                st(dve.tensor_copy(LG[:, ts, :], bank[b][:, 0:TB * E].rearrange("p (i e) -> p i e", e=E)))
                st.sync()
                for i in range(b * TB, (b + 1) * TB):
                    st(dve.max(TOP[:, i, :], LG[:, i, :]))
                st.sync()
                for i in range(b * TB, (b + 1) * TB):
                    st(dve.max_index(TIX[:, i, :], TOP[:, i, :], LG[:, i, :]))
                st.sync()
                st(dve.tensor_copy(TIF[:, ts, :], TIX[:, ts, 0:2]))
                dve.tensor_tensor(W12[:, ts, 1], TOP[:, ts, 1], TOP[:, ts, 0], ALU.subtract)\
                   .then_inc(S("logit_gap"), 1)
                dve.wait_ge(S("gap_exp"), b + 1)
                st(dve.tensor_scalar(W12[:, ts, 0], W12[:, ts, 1], 1.0, None, ALU.add))
                st.sync()
                st(dve.reciprocal(W12[:, ts, 0], W12[:, ts, 0]))
                st.sync()
                st(dve.tensor_tensor(W12[:, ts, 1], W12[:, ts, 1], W12[:, ts, 0], ALU.mult))
                n0 = VECS.index("n0")
                for k, dst in ((0, CMB), (1, CM2)):
                    num = VEC[:, n0:n0 + E].unsqueeze(1).to_broadcast([P, TB, E])
                    st(dve.tensor_tensor(dst[:, ts, :], num, TIF[:, ts, k:k + 1].to_broadcast([P, TB, E]),
                                         ALU.is_equal))
                    st.sync()
                    st(dve.tensor_tensor(dst[:, ts, :], dst[:, ts, :],
                                         W12[:, ts, k:k + 1].to_broadcast([P, TB, E]), ALU.mult))
                st.sync()
                st(dve.tensor_tensor(CMB[:, ts, :], CMB[:, ts, :], CM2[:, ts, :], ALU.add))
            st.sync()
            for k in range(2):
                st(dve.memset(HB[k][:, FI:FIP], 0.0))

            for s in range(NT * E + 2):
                if s < NT * E:
                    i, e = s // E, s % E
                    dve.wait_ge(S("silu_done"), s + 1)
                    dve.wait_ge(S("up_filled"), s + 1)
                    if s >= 2:
                        dve.wait_ge(S("h_turned"), s - 1)
                    dve.scalar_tensor_tensor(out=HB[s % 2][:, 0:FI], in0=SL[s % 2], scalar=CMB[:, i, e:e + 1],
                                             in1=bank[2 + s % 2][:, 0:FI], op0=ALU.mult, op1=ALU.mult)\
                       .then_inc(S("hidden_ready"), 1)
                if s >= E + 1 and (s - 1) % E == 0:
                    i = (s - 1) // E - 1
                    dve.wait_ge(S("down_done"), E * (i + 1))
                    dve.tensor_copy(YO[:, i, :], bank[6 + i % 2][:, 0:P]).then_inc(S("tile_copied"), 1)
                    if (i + 1) % TB == 0:
                        dve.wait_ge(S("tile_copied"), i + 1)
                        add_ln(i // TB, lambda i: YO[:, i, :], None)

        @block.scalar
        def _(act):
            for c in range(NCH):
                b, q = c // QPB, c % QPB
                act.wait_ge(S("xa_transposed"), c + 1)
                if c == 0:
                    act.wait_ge(S("vec_loaded"), 16)
                act.activation(XS[:, b, 1 + q * CH:1 + (q + 1) * CH], bank[c][:, :], ACT.Identity,
                               bias=vec("b1"), scale=vec("g1")).then_inc(S("xa_evacuated"), 1)
            for n in range(12):
                b, kind, q = n // 6, n % 6 // 2, n % 2
                act.wait_ge(S("kvr_filled"), n + 1)
                dst = (Kc, Vc, SR)[kind][b][:, q * CH:(q + 1) * CH]
                act.activation(dst, bank[(4 + n) % 8][:, :], ACT.Sigmoid if kind == 2 else ACT.Identity)\
                   .then_inc(S("kvr_evacuated"), 1)
            for b in range(B):
                act.wait_ge(S(f"d_ready{b}"), 1)
                act.activation(EA[b], EA[b], ACT.Exp)
                act.activation(EB[b], EB[b], ACT.Exp, scale=-1.0).then_inc(S(f"ab_exp{b}"), 1)
            for b in range(B):
                act.wait_ge(S(f"s_ready{b}"), 1)
                act.activation(Kc[b], SS[b][:, 0:T], ACT.Ln).then_inc(S(f"log_s{b}"), 1)
            for b in range(B):
                act.wait_ge(S(f"z_ready{b}"), 1)
                act.activation(EA[b], EA[b], ACT.Exp)
                act.activation(EB[b], EB[b], ACT.Exp, scale=-1.0).then_inc(S(f"e_exp{b}"), 1)
            act.mul(OMV[:, 5:6], vec("u"), -1.0).then_inc(S("minus_u"), 1)
            act.wait_ge(S("minus_u"), 1)
            for b in range(B):
                act.activation(SG[b], DD[b], ACT.Sigmoid, bias=OMV[:, 5:6]).then_inc(S(f"sig_z{b}"), 1)
            for c in range(NCH):
                b, q = c // QPB, c % QPB
                act.wait_ge(S("xb_transposed"), c + 1)
                act.activation(XS[:, b, 1 + q * CH:1 + (q + 1) * CH], bank[4 + c][:, :], ACT.Identity,
                               bias=vec("b2"), scale=vec("g2")).then_inc(S("xb_evacuated"), 1)
            for c in range(NCH):
                for j in range(4):
                    m = 4 * c + j
                    act.wait_ge(S("kc_filled"), m + 1)
                    if m >= 4:
                        act.wait_ge(S("kc_ready"), m - 3)
                    act.activation(RL[m % 4], bank[m % 4][:, :], ACT.Relu).then_inc(S("relu_done"), 1)
                act.wait_ge(S("cr_filled"), c + 1)
                if c >= 2:
                    act.wait_ge(S("vc_used"), c - 1)
                act.activation(SCR[c % 2], bank[6 + c % 2][:, :], ACT.Sigmoid).then_inc(S("cr_sigmoid"), 1)
            act.wait_ge(S("gate_bias_ready"), 1)
            for b in range(B):
                for q in range(QPB):
                    c = QPB * b + q
                    act.wait_ge(S("l_transposed"), c + 1)
                    act.activation(CT[:, c * CH:(c + 1) * CH], bank[c][:, :], ACT.Identity)\
                       .then_inc(S("l_evacuated"), 1)
                for q in range(QPB):
                    for g in range(3):
                        n = 6 * b + 3 * q + g
                        act.wait_ge(S("gates_filled"), n + 1)
                        dst = (FG, IGT, GG)[g][QPB * b + q]
                        bias = GB0[:, g:g + 1] if b == 0 else vec(("bf", "bi", "bc")[g])
                        act.activation(dst, bank[4 + n % 4][:, :], ACT.Tanh if g == 2 else ACT.Sigmoid, bias=bias)\
                           .then_inc(S("gates_done"), 1)
            for c in range(NCH):
                act.wait_ge(S("h_filled"), c + 1)
                act.activation(HH[:, c * TPC:(c + 1) * TPC, :].rearrange("p i c -> p (i c)"), bank[c][:, :],
                               ACT.Tanh).then_inc(S("h_ready"), 1)
            for c in range(NCH):
                act.wait_ge(S("a_transposed"), c + 1)
                act.activation(CT[:, c * CH:(c + 1) * CH], bank[4 + c][:, :], ACT.Identity)\
                   .then_inc(S("a_evacuated"), 1)
                if c % QPB == QPB - 1:
                    for n in range(2 * (c - 1), 2 * (c + 1)):
                        t1, t2, parts = RT1[n % 2], RT2[n % 2], PARTS[n % 2]
                        act.wait_ge(S("roped"), n + 1)
                        if n >= 2:
                            act.wait_ge(S(f"parts_stored{n % 2}"), 48 * (n // 2))
                        act.activation(parts[:, 0, :], t1, ACT.Identity).then_inc(S("part0_ready"), 1)
                        act.wait_ge(S("rest_ready"), n + 1)
                        act.activation(parts[:, 1, :], t2, ACT.Identity).then_inc(S("part1_ready"), 1)
            act.wait_ge(S("v_cleared"), 1)
            for c in range(NCH):
                act.wait_ge(S("v_filled"), c + 1)
                act.activation(VS[:, c * TPC:(c + 1) * TPC, :, 0:D],
                               bank[c][:, :].rearrange("p (t h d) -> p t h d", h=H, d=D), ACT.Identity)\
                   .then_inc(S("v_ready"), 1)
            for k in range(2):
                act.wait_ge(S(f"parts_stored{k}"), 48 * NCH)
            for u in range(GROUPS * UNITS + 1):
                g = u // UNITS
                if u < GROUPS * UNITS:
                    act.wait_ge(S("scores_filled"), u + 1)
                    if u >= NPT:
                        act.wait_ge(S("av_steps"), (u - NPT) // HG + 1)
                    for q in range(1):
                        act.activation(PT[u % NPT], PS[u % 2], ACT.Exp, scale=SCALE).then_inc(S("exp_done"), 1)
                if (u % UNITS == 4 and g >= 1) or u == GROUPS * UNITS:
                    act.wait_ge(S("av_steps"), TB * g)
                    if g >= 2:
                        act.wait_ge(S("side_filled"), side_at[("output", g - 2, 1)] + 1)
                    for q in range(QPB):
                        act.activation(OE[:, q * CH:(q + 1) * CH], bank[6 + q][:, :], ACT.Identity)\
                           .then_inc(S("o_evacuated"), 1)
            for c in range(NCH):
                act.wait_ge(S("o_transposed"), c + 1)
                act.activation(CT[:, c * CH:(c + 1) * CH], bank[c][:, :], ACT.Identity).then_inc(S("ot_evacuated"), 1)
            for c in range(NCH):
                act.wait_ge(S("m_transposed"), c + 1)
                act.activation(CT[:, c * CH:(c + 1) * CH], bank[c][:, :], ACT.Identity).then_inc(S("m_evacuated"), 1)
            for b in range(B):
                act.wait_ge(S("logit_gap"), b + 1)
                ts = slice(b * TB, (b + 1) * TB)
                act.activation(W12[:, ts, 1], W12[:, ts, 1], ACT.Exp).then_inc(S("gap_exp"), 1)
            for s in range(NT * E + 1):
                if s < NT * E:
                    act.wait_ge(S("gate_filled"), s + 1)
                    if s >= 2:
                        act.wait_ge(S("hidden_ready"), s - 1)
                    act.activation(SL[s % 2], bank[s % 2][:, 0:FI], ACT.Silu).then_inc(S("silu_done"), 1)
                if s >= 1:
                    act.wait_ge(S("h_turned"), s)
                    if s >= 3:
                        act.wait_ge(S("down_done"), s - 2)
                    act.activation(HT[(s - 1) % 2], bank[4 + (s - 1) % 2][:, 0:FIP], ACT.Identity)\
                       .then_inc(S("ht_ready"), 1)

        @block.tensor
        def _(pe):
            def transposes(src, c, dst, sem):
                for j in range(TPC):
                    ins = pe.transpose(dst[:, j * P:(j + 1) * P], src(c * TPC + j), ident)
                ins.then_inc(S(sem), 1)

            def tm(i):
                return TM[:, i, :]

            pe.wait_ge(S("w1_loaded"), 16)
            n = 0
            for b in range(B):
                pe.wait_ge(S(f"xa_ready{b}"), 1)
                for q in range(QPB):
                    transposes(tm, QPB * b + q, bank[QPB * b + q], "xa_transposed")
                for kind in range(3):
                    pe.wait_ge(S("mix_scaled"), kind + 1)
                    for q in range(QPB):
                        pe.wait_ge(S("xa_evacuated"), QPB * b + q + 1)
                        if n >= 8:
                            pe.wait_ge(S("kvr_evacuated"), n - 7)
                        o = bank[(4 + n) % 8][:, :]
                        pe.matmul(o, WMA[:, kind * P:(kind + 1) * P], XS[:, b, 1 + q * CH:1 + (q + 1) * CH],
                                  start=True, stop=False)
                        pe.matmul(o, WMB[:, kind * P:(kind + 1) * P], XS[:, b, q * CH:(q + 1) * CH],
                                  start=False, stop=True).then_inc(S("kvr_filled"), 1)
                        n += 1
            for b in range(B):
                pe.wait_ge(S(f"y_ready{b}"), 1)
                if b == 0:
                    pe.wait_ge(S("kvr_evacuated"), 12)
                for q in range(QPB):
                    transposes(lambda i: EB[b][:, (i - b * TB) * P:(i - b * TB + 1) * P], QPB * b + q,
                               bank[QPB * b + q], "y_transposed")
            for b in range(B):
                pe.wait_ge(S(f"xb_ready{b}"), 1)
                for q in range(QPB):
                    transposes(tm, QPB * b + q, bank[4 + QPB * b + q], "xb_transposed")

            def kc_in(c):
                b, q = c // QPB, c % QPB
                pe.wait_ge(S("xb_evacuated"), c + 1)
                for j in range(4):
                    m = 4 * c + j
                    if m == 0:
                        pe.wait_ge(S("mix_scaled"), 5)
                    if m >= 4:
                        pe.wait_ge(S("relu_done"), m - 3)
                    k = 4 + j
                    pe.matmul(bank[m % 4][:, :], WMA[:, k * P:(k + 1) * P], XS[:, b, 1 + q * CH:1 + (q + 1) * CH],
                              start=True, stop=False)
                    pe.matmul(bank[m % 4][:, :], WMB[:, k * P:(k + 1) * P], XS[:, b, q * CH:(q + 1) * CH],
                              start=False, stop=True).then_inc(S("kc_filled"), 1)
                if c == 0:
                    pe.wait_ge(S("xb_evacuated"), NCH)
                if c >= 2:
                    pe.wait_ge(S("cr_sigmoid"), c - 1)
                for i in range(TPC):
                    o = bank[6 + c % 2][:, i * P:(i + 1) * P]
                    at = q * CH + i * P
                    pe.matmul(o, XS[:, b, 1 + at:1 + at + P], WMA[:, 3 * P:4 * P], start=True, stop=False)
                    ins = pe.matmul(o, XS[:, b, at:at + P], WMB[:, 3 * P:4 * P], start=False, stop=True)
                ins.then_inc(S("cr_filled"), 1)

            def kc_out(c):
                pe.wait_ge(S("kc_ready"), 4 * c + 4)
                if c >= 2:
                    pe.wait_ge(S("vc_used"), c - 1)
                for i in range(TPC):
                    for j in range(4):
                        ins = pe.matmul(bank[4 + c % 2][:, i * P:(i + 1) * P], KC[(4 * c + j) % 8][:, i * P:(i + 1) * P],
                                        blk(f"wcv{j}"), start=j == 0, stop=j == 3)
                ins.then_inc(S("vc_ready"), 1)

            for c in range(NCH + 1):
                if c < NCH:
                    kc_in(c)
                if c >= 1:
                    kc_out(c - 1)

            pe.wait_ge(S("w2_loaded"), 32)
            pe.wait_ge(S("cr_sigmoid"), NCH)
            for g, name in enumerate(("uf", "ui", "uc")):
                ins = pe.matmul(bank[7][:, g:g + 1], blk(name), vec("in_c"), start=True, stop=True)
            ins.then_inc(S("uc0_ready"), 1)
            pe.wait_ge(S("relu_done"), 4 * NCH)
            pe.wait_ge(S("vc_used"), NCH)
            pe.wait_ge(S("gate_bias_ready"), 1)
            for b in range(B):
                pe.wait_ge(S(f"l_in_ready{b}"), 1)
                for q in range(QPB):
                    transposes(tm, QPB * b + q, bank[QPB * b + q], "l_transposed")
                for q in range(QPB):
                    c = QPB * b + q
                    pe.wait_ge(S("l_evacuated"), c + 1)
                    if b == 1:
                        pe.wait_ge(S("cell_ready"), q + 1)
                    for g, (wn, un) in enumerate((("wf", "uf"), ("wi", "ui"), ("wc", "uc"))):
                        n = 6 * b + 3 * q + g
                        if n >= 4:
                            pe.wait_ge(S("gates_done"), n - 3)
                        o = bank[4 + n % 4][:, :]
                        ins = pe.matmul(o, blk(wn), CT[:, c * CH:(c + 1) * CH], start=True, stop=b == 0)
                        if b == 1:
                            ins = pe.matmul(o, blk(un), CST[0][:, q * CH:(q + 1) * CH], start=False, stop=True)
                        ins.then_inc(S("gates_filled"), 1)
            for c in range(NCH):
                q = c % QPB
                pe.wait_ge(S("cell_ready"), QPB + q + 1)
                for i in range(TPC):
                    o = bank[c][:, i * P:(i + 1) * P]
                    at = q * CH + i * P
                    pe.matmul(o, blk("row0"), row("bo"), start=True, stop=False)
                    pe.matmul(o, CT[:, c * CH + i * P:c * CH + (i + 1) * P], blk("wo"), start=False, stop=False)
                    ins = pe.matmul(o, CST[1][:, at:at + P], blk("uo"), start=False, stop=True)
                ins.then_inc(S("h_filled"), 1)
            def qk_in(c):
                pe.wait_ge(S("a_evacuated"), c + 1)
                for k, name in enumerate(("aq", "aqr", "ak", "akr")):
                    m = 4 * c + k
                    if m >= 8:
                        pe.wait_ge(S("qk_used"), m - 7)
                    pe.matmul(bank[m % 8][:, :], blk(name), CT[:, c * CH:(c + 1) * CH], start=True, stop=True)\
                      .then_inc(S("qk_filled"), 1)

            for b in range(B):
                pe.wait_ge(S(f"a_in_ready{b}"), 1)
                if b == 1:
                    pe.wait_ge(S("qk_used"), 8)
                for q in range(QPB):
                    transposes(tm, QPB * b + q, bank[4 + QPB * b + q], "a_transposed")
                for q in range(QPB):
                    if QPB * b + q == 1:
                        pe.wait_ge(S("a_evacuated"), 2)
                    qk_in(QPB * b + q)
            for c in range(NCH):
                pe.wait_ge(S("qk_used"), 8 + c + 1)
                for i in range(TPC):
                    o = bank[c][:, i * P:(i + 1) * P]
                    pe.matmul(o, blk("row0"), row("bv"), start=True, stop=False)
                    ins = pe.matmul(o, CT[:, c * CH + i * P:c * CH + (i + 1) * P], blk("av"), start=False, stop=True)
                ins.then_inc(S("v_filled"), 1)
            pe.wait_ge(S("qk_used"), 4 * NCH)
            pe.wait_ge(S("v_ready"), NCH)
            pe.wait_ge(S("ident_bf16"), 1)

            def side(op):
                n = side_at[op]
                if n >= 2:
                    pe.wait_ge(S("side_used"), n - 1)
                o = bank[n % 2]
                if op[0] == "scores":
                    _, g, j, qt, kk = op
                    if (j, qt, kk) == (0, 0, 0):
                        pe.wait_ge(S(f"stacks_loaded{g % 2}"), 32 * (g // 2 + 1))
                    ins = pe.matmul(o[:, :], QS[0:MROW, g % 2, j, qt * P:(qt + 1) * P],
                                    KS[0:MROW, g % 2, j, kk * CH:(kk + 1) * CH], start=True, stop=True)
                elif op[0] == "maxima":
                    pe.wait_ge(S("maxima_ready"), op[1] + 1)
                    ins = pe.transpose(o[:, :].bitcast(BF16)[0:3 * HG * TB, 0:P],
                                       M3[:, :, :].rearrange("p s m -> p (s m)"), IDB[:, :])
                else:
                    _, g, half = op
                    pe.wait_ge(S("o_evacuated"), QPB * g + half + 1)
                    for t in range(TPC):
                        at = half * CH + t * P
                        ins = pe.transpose(o[:, t * P:(t + 1) * P], OE[:, at:at + P], ident)
                ins.then_inc(S("side_filled"), 1)

            def scores(u):
                g, kt, j = u // UNITS, u % UNITS // HG, u % HG
                if u % UNITS == 0:
                    pe.wait_ge(S("maxima_placed"), 48 * (g + 1))
                if u >= 2:
                    pe.wait_ge(S("exp_done"), u - 1)
                for q in range(QPB):
                    ins = pe.matmul(PS[u % 2][:, q * CH:(q + 1) * CH], KS[:, g % 2, j, kt * P:(kt + 1) * P],
                                    QS[:, g % 2, j, q * CH:(q + 1) * CH], start=True, stop=True)
                ins.then_inc(S("scores_filled"), 1)

            def weigh(k):
                g, kt = k // TB, k % TB
                pe.wait_ge(S("exp_done"), HG * (k + 1))
                if kt == 0 and g >= 1:
                    pe.wait_ge(S("o_evacuated"), QPB * g)
                for q in range(QPB):
                    for j in range(HG):
                        ins = pe.matmul(bank[6 + q][32 * j:32 * (j + 1), :],
                                        VS[:, g // NG * TB + kt, g % NG * HG + j, :],
                                        PT[(HG * k + j) % NPT][:, q * CH:(q + 1) * CH],
                                        start=kt == 0, stop=kt == TB - 1)
                ins.then_inc(S("av_steps"), 1)

            for op in FIRST_SIDE:
                side(op)
            for g in range(GROUPS):
                work = side_work(g)
                for v in range(UNITS):
                    u = g * UNITS + v
                    scores(u)
                    for op in work[v]:
                        side(op)
                    if u % HG == HG - 1 and u >= HG:
                        weigh(u // HG - 1)
            weigh(GROUPS * TB - 1)
            for op in LAST_SIDE:
                side(op)

            pe.wait_ge(S("side_used"), len(every))
            pe.wait_ge(S("exp_done"), GROUPS * UNITS)
            for c in range(NCH):
                transposes(lambda i: OT[:, i, :], c, bank[c], "o_transposed")
            for c in range(NCH):
                pe.wait_ge(S("ot_evacuated"), c + 1)
                for i in range(TPC):
                    o = bank[4 + c][:, i * P:(i + 1) * P]
                    pe.matmul(o, blk("row0"), row("bao"), start=True, stop=False)
                    ins = pe.matmul(o, CT[:, c * CH + i * P:c * CH + (i + 1) * P], blk("ao"), start=False, stop=True)
                ins.then_inc(S("proj_filled"), 1)
            pe.wait_ge(S("moe_loaded"), 64)
            for b in range(B):
                pe.wait_ge(S(f"m_in_ready{b}"), 1)
                for q in range(QPB):
                    transposes(tm, QPB * b + q, bank[QPB * b + q], "m_transposed")
            for b in range(B):
                pe.wait_ge(S("m_evacuated"), NCH)
                for i in range(b * TB, (b + 1) * TB):
                    ins = pe.matmul(bank[b][:, (i % TB) * E:(i % TB + 1) * E], CT[:, i * P:(i + 1) * P], WRT[:, :],
                                    start=True, stop=True)
                ins.then_inc(S("router_filled"), 1)
            pe.wait_ge(S("logit_gap"), B)
            for s in range(NT * E + 2):
                if s < NT * E:
                    i, e = s // E, s % E
                    if s >= 2:
                        pe.wait_ge(S("silu_done"), s - 1)
                    pe.matmul(bank[s % 2][:, 0:FI], CT[:, i * P:(i + 1) * P], WG[:, e, :], start=True, stop=True)\
                      .then_inc(S("gate_filled"), 1)
                    if s >= 2:
                        pe.wait_ge(S("hidden_ready"), s - 1)
                    pe.matmul(bank[2 + s % 2][:, 0:FI], CT[:, i * P:(i + 1) * P], WU[:, e, :], start=True, stop=True)\
                      .then_inc(S("up_filled"), 1)
                if 1 <= s <= NT * E:
                    k = s - 1
                    pe.wait_ge(S("hidden_ready"), k + 1)
                    if k >= 2:
                        pe.wait_ge(S("ht_ready"), k - 1)
                    for j in range(NF):
                        ins = pe.transpose(bank[4 + k % 2][:, j * P:(j + 1) * P], HB[k % 2][:, j * P:(j + 1) * P],
                                           ident)
                    ins.then_inc(S("h_turned"), 1)
                if s >= 2:
                    k = s - 2
                    i, e = k // E, k % E
                    pe.wait_ge(S("ht_ready"), k + 1)
                    if e == 0 and i >= 2:
                        pe.wait_ge(S("tile_copied"), i - 1)
                    for j in range(NF):
                        ins = pe.matmul(bank[6 + i % 2][:, 0:P], HT[k % 2][:, j * P:(j + 1) * P], WD[:, e, j, :],
                                        start=e == 0 and j == 0, stop=e == E - 1 and j == NF - 1)
                    ins.then_inc(S("down_done"), 1)


_N_OUT = (B, T, C)


def _laid_out(f):
    import numpy as np

    f = {k: np.asarray(v, np.float32) for k, v in f.items()}
    a, l, n = "L0_attn_", "L0_ffn_", "L1_attn_"
    turn = (np.arange(C) // D) * D + (np.arange(C) % D + D // 2) % D
    w = {"wk": f[a + "Wk"].T, "wv": f[a + "Wv"].T, "wr": f[a + "Wr"].T, "wcr": f[a + "Wcr"].T,
         "wf": f[l + "wf"].T, "wi": f[l + "wi"].T, "wc": f[l + "wc"].T, "uf": f[l + "uf"].T, "ui": f[l + "ui"].T,
         "uc": f[l + "uc"].T, "wo": f[l + "wo"].T, "uo": f[l + "uo"].T, "aq": f[n + "Wq"].T, "aqr": f[n + "Wq"][turn].T,
         "ak": f[n + "Wk"].T, "akr": f[n + "Wk"][turn].T, "av": f[n + "Wv"].T, "ao": f[n + "Wo"].T,
         "ident": np.eye(C, dtype=np.float32)}
    for j in range(4):
        w[f"wck{j}"] = f[a + "Wck"].T[:, j * C:(j + 1) * C]
        w[f"wcv{j}"] = f[a + "Wcv"].T[j * C:(j + 1) * C]
    w["row0"] = np.zeros((C, C), np.float32)
    w["row0"][0] = 1.0
    v = {"w": f[a + "w"], "u": f[a + "u"], "rk": f[a + "rk"], "rv": f[a + "rv"], "rr": f[a + "rr"],
         "crk": f[a + "crk"], "crr": f[a + "crr"], "g1": f[a + "ln1_g"], "b1": f[a + "ln1_b"], "g2": f[a + "ln2_g"],
         "b2": f[a + "ln2_b"], "bf": f[l + "bf"], "bi": f[l + "bi"], "bc": f[l + "bc"], "in_c": f[l + "in_c"],
         "bq": f[n + "bq"], "bqr": f[n + "bq"][turn], "bk": f[n + "bk"], "bkr": f[n + "bk"][turn]}
    v.update({f"n{k}": np.full(C, k, np.float32) for k in range(8)})
    rows = np.zeros((C, len(ROWS) * C), np.float32)
    for k, b in enumerate((f[l + "bo"], f[n + "bv"], f[n + "bo"])):
        rows[0, k * C:(k + 1) * C] = b
    inv = (1.0 / 10000.0 ** (np.arange(0, D, 2, dtype=np.float32) / np.float32(D))).astype(np.float32)
    ang = np.arange(T, dtype=np.float32)[:, None] * inv[None, :]
    ang = np.concatenate([ang, ang], 1).T
    sign = np.where(np.arange(D) < D // 2, -1.0, 1.0).astype(np.float32)[:, None]
    wd = np.zeros((C, E, NF, C), np.float32)
    down = f["L1_ffn_w_down"]
    for j in range(NF):
        part = down[:, :, j * C:(j + 1) * C]
        wd[:part.shape[2], :, j, :] = part.transpose(2, 0, 1)
    return {
        "x": f["L0_attn_x"],
        "wt": np.concatenate([w[k] for k in BLOCKS], 1),
        "vec": np.stack([v[k] for k in VECS], 1),
        "rows": rows,
        "cos": np.tile(np.cos(ang).astype(np.float32), (H, 1)),
        "sin": np.tile((np.sin(ang) * sign).astype(np.float32), (H, 1)),
        "wg": f["L1_ffn_w_gate"].transpose(2, 0, 1),
        "wu": f["L1_ffn_w_up"].transpose(2, 0, 1),
        "wd": wd,
        "wrt": f["L1_ffn_w_router"].T,
    }


def kernel(**inputs):
    import numpy as np
    import concourse.bacc as bacc
    from concourse.bass_utils import run_bass_kernel_spmd

    nc = bacc.Bacc("TRN2", target_bir_lowering=False, num_devices=1)
    arrays, args = {}, []
    for name, a in _laid_out(inputs).items():
        a = np.ascontiguousarray(a)
        arrays[f"in_{name}"] = a
        args.append(nc.dram_tensor(f"in_{name}", a.shape, mybir.dt.from_np(a.dtype), kind="ExternalInput").ap())
    args.append(nc.dram_tensor("out_x", _N_OUT, F32, kind="ExternalOutput").ap())
    sandwich_kernel(nc, *args)
    r = run_bass_kernel_spmd(nc, [arrays], core_ids=[0])
    return r.results[0]["out_x"]
```

```python
from contextlib import ExitStack

import concourse.bass as bass
from concourse import mybir

ALU = mybir.AluOpType
ACT = mybir.ActivationFunctionType
AXX = mybir.AxisListType.X
F32 = mybir.dt.float32
BF16 = mybir.dt.bfloat16
I32 = mybir.dt.int32
U32 = mybir.dt.uint32

B, T, C = 2, 1024, 128
P = 128
NT = B * T // P
TB = T // P
CH = 512
NCH = B * T // CH
QPB = T // CH
TPC = CH // P
H, D = 16, 8
HG = 4
NG = H // HG
E, FI = 8, 352
FIP = 384
NF = FIP // P
LN_EPS = 1e-5
NEG = -1e38
SCALE = float(D) ** -0.5

BLOCKS = ["wk", "wv", "wr", "wcr", "wck0", "wck1", "wck2", "wck3", "wcv0", "wcv1", "wcv2", "wcv3", "ident",
          "wf", "wi", "wc", "uf", "ui", "uc", "wo", "uo", "aq", "aqr", "ak", "akr", "av", "ao", "row0",
          "ones", "tri", "iota", "slots"]
VECS = ["w", "u", "rk", "rv", "rr", "crk", "crr", "g1", "b1", "g2", "b2", "bf", "bi", "bc", "in_c",
        "bq", "bqr", "bk", "bkr"]
ROWS = ["bo", "bv", "bao"]
Q_PART = (0, 0, 0, 1, 1, 2)
K_PART = (0, 1, 2, 0, 1, 0)
NP6 = len(Q_PART)
STK = D * NP6
NPT = 16
GROUPS = B * NG
ROUNDS = GROUPS * QPB
UNITS = TB * HG
NU = ROUNDS * UNITS
NSIDE = HG * TPC * QPB
AHEAD = NSIDE + 10
NRING = 3
NPAIR = 2 * B * T
NS = (NPAIR + E * (P - 1)) // P
NSP = 40
NX = 8
LAG = 6
MROW = 96


def sandwich_kernel(nc, x_in, wt_in, vec_in, rows_in, cos_in, sin_in, wg_in, wu_in, wd_in, wrt_in, out):
    ctx = ExitStack()
    with ctx:
        def sb(name, shape, dt=F32):
            return ctx.enter_context(nc.sbuf_tensor(name, shape, dt))

        sems = {}

        def S(name):
            if name not in sems:
                sems[name] = ctx.enter_context(nc.semaphore(name))
            return sems[name]

        X = sb("X", [P, NT, C])
        XN = sb("XN", [P, NT, C])
        TM = sb("TM", [P, NT, C])
        CT = sb("CT", [P, B * T])
        XS = sb("XS", [P, B, T + 1])
        WT = sb("WT", [P, len(BLOCKS) * P])
        VEC = sb("VEC", [P, len(VECS)])
        ROW = sb("ROW", [P, len(ROWS) * P])
        OMV = sb("OMV", [P, 8])
        WMA = sb("WMA", [P, 8 * P])
        WMB = sb("WMB", [P, 8 * P])
        COS = sb("COS", [P, T])
        SIN = sb("SIN", [P, T])
        WG = sb("WG", [P, E, FI])
        WU = sb("WU", [P, E, FI])
        WD = sb("WD", [P, E, NF, C])
        WRT = sb("WRT", [P, E])
        ST = sb("ST", [P, NT, 6])
        MV = sb("MV", [P, NT, 2])
        RS = sb("RS", [P, NT])
        RS2 = sb("RS2", [P, NT])
        NV = sb("NV", [P, NT])
        NI = sb("NI", [P, NT], I32)
        ND = sb("ND", [P, NT])
        GB0 = sb("GB0", [P, 4])
        ARENA = sb("ARENA", [P, 96 * 256])

        ps01 = [ctx.enter_context(nc.psum_tensor(f"bank{i}", [P, CH], F32)) for i in range(2)]
        PSP = [ctx.enter_context(nc.psum_tensor(f"banks{2 + 2 * i}", [P, 2 * CH], F32)) for i in range(2)]
        ps67 = [ctx.enter_context(nc.psum_tensor(f"bank{6 + i}", [P, CH], F32)) for i in range(2)]
        PS = [p[:, :] for p in PSP]
        bank = [ps01[0][:, :], ps01[1][:, :], PSP[0][:, 0:CH], PSP[0][:, CH:], PSP[1][:, 0:CH], PSP[1][:, CH:],
                ps67[0][:, :], ps67[1][:, :]]

        def blk(name):
            k = BLOCKS.index(name)
            return WT[:, k * P:(k + 1) * P]

        def vec(name):
            k = VECS.index(name)
            return VEC[:, k:k + 1]

        def row(name):
            k = ROWS.index(name)
            return ROW[:, k * P:(k + 1) * P]

        ident = blk("ident")

        def arena(kib, n, dt=F32):
            v = ARENA[:, kib * 256:kib * 256 + n]
            return v

        Kc = [arena(0 + 4 * b, T) for b in range(B)]
        Vc = [arena(8 + 4 * b, T) for b in range(B)]
        SR = [arena(16 + 4 * b, T) for b in range(B)]
        DD = [arena(24 + 4 * b, T) for b in range(B)]
        EA = [arena(32 + 4 * b, T) for b in range(B)]
        EB = [arena(40 + 4 * b, T) for b in range(B)]
        MM = [arena(48 + 5 * b, T + 1) for b in range(B)]
        SS = [arena(58 + 5 * b, T + 1) for b in range(B)]
        AA = [arena(68 + 5 * b, T + 1) for b in range(B)]
        SG = [arena(78 + 4 * b, T) for b in range(B)]
        RL = [arena(86 + 2 * k, CH) for k in range(4)]
        KC = [arena(2 * k, CH) for k in range(8)]
        SCR = [arena(24 + 2 * k, CH) for k in range(2)]
        OUT1 = arena(32, B * T).rearrange("p (i c) -> p i c", c=C)
        FG = [arena(0 + 2 * k, CH) for k in range(4)]
        IGT = [arena(8 + 2 * k, CH) for k in range(4)]
        GG = [arena(16 + 2 * k, CH) for k in range(4)]
        CST = [arena(24 + 4 * k, T) for k in range(2)]
        HH = arena(40, B * T).rearrange("p (i c) -> p i c", c=C)

        VS = ARENA[:, 0:32 * 256].rearrange("p (i h e) -> p i h e", h=H, e=32)
        PT = [arena(32 + 2 * k, CH) for k in range(NPT)]
        RT1 = [arena(32 + 2 * k, CH) for k in range(4)]
        RT2 = [arena(40 + 2 * k, CH) for k in range(4)]
        PARTS = [ARENA[:, (48 + 3 * k) * 256:(51 + 3 * k) * 256].bitcast(BF16).rearrange("p (s t) -> p s t", s=3)
                 for k in range(4)]
        QS = ARENA[:, 64 * 256:80 * 256].bitcast(BF16).rearrange("p (s q h t) -> p s q h t", s=2, q=QPB, h=HG)
        KS = ARENA[:, 80 * 256:96 * 256].bitcast(BF16).rearrange("p (s h t) -> p s h t", s=2, h=HG)
        OT = XN
        XSF = XS[:, :, :].rearrange("p b t -> p (b t)")
        OE = XSF[:, 0:CH]
        OC = [XSF[:, CH + k * 256:CH + k * 256 + TPC * HG * (D + 1)].rearrange("p (t j e) -> p t j e", j=HG, e=D + 1)
              for k in range(2)]
        PO = XSF[:, 2 * CH:4 * CH].rearrange("p (i c) -> p i c", c=C)
        IDB = sb("IDB", [P, P], BF16)
        NM = HG * TPC
        MX = sb("MX", [P, 2, NM, QPB])
        MQ = sb("MQ", [P, NM])
        MR = sb("MR", [P, NM])
        M3 = sb("M3", [P, 3, NM], BF16)
        M3T = sb("M3T", [3 * NM, P], BF16)
        RDEN = sb("RDEN", [P, 2, TPC, HG])
        QD = nc.dram_tensor("q_stacks", (P, NP6, B * T), BF16, kind="Internal").ap()
        KD = nc.dram_tensor("k_stacks", (P, NP6, B * T), BF16, kind="Internal").ap()
        SL = [arena(0 + 2 * k, FI) for k in range(2)]
        HB = [arena(4 + 2 * k, FIP) for k in range(2)]
        HT = [arena(8 + 2 * k, FIP) for k in range(2)]
        XG = [ARENA[:, (12 * 256 + k * P):(12 * 256 + (k + 1) * P)] for k in range(NX)]
        YG = [ARENA[:, (17 * 256 + k * P):(17 * 256 + (k + 1) * P)] for k in range(NX)]
        XC = [ARENA[:, (16 * 256 + k * P):(16 * 256 + (k + 1) * P)] for k in range(2)]
        LOH = arena(20, 2 * NT * P).rearrange("p (n q) -> p n q", q=P)
        HOH = arena(46, 2 * NT * NSP).rearrange("p (n t) -> p n t", t=NSP)
        HVAL = arena(36, 2 * NT * 2 * NSP).rearrange("p (n t) -> p n t", t=2 * NSP)
        YK = [arena(52 + 8 * k, B * T // 2 * 2).rearrange("p (i c) -> p i c", c=C) for k in range(2)]
        LG = arena(84, NT * E).rearrange("p (i e) -> p i e", e=E)
        TOP = arena(85, NT * 8).rearrange("p (i e) -> p i e", e=8)
        TIX = arena(86, NT * 8).bitcast(U32).rearrange("p (i e) -> p i e", e=8)
        TIF = sb("TIF", [P, 2, NT])
        W12 = sb("W12", [P, 2, NT])
        CHO = arena(72, 2 * NT * E).rearrange("p (k i e) -> p k i e", i=NT, e=E)
        CHS = arena(73, NT * E).rearrange("p (i e) -> p i e", e=E)
        TOT = arena(74, NT * E).rearrange("p (e i) -> p e i", i=NT)
        CUM = arena(75, NT * E).rearrange("p (e i) -> p e i", i=NT)
        BASE = arena(76, NT * E).rearrange("p (i e) -> p i e", e=E)
        PPOS = arena(77, 2 * NT * E).rearrange("p (n e) -> p n e", e=E)
        EXC = arena(78, NSP * E).rearrange("p (t e) -> p t e", e=E)
        NE, TE, TEC, OFF = (ARENA[:, 80 * 256 + k * E:80 * 256 + (k + 1) * E] for k in range(4))
        NEI = ARENA[:, 80 * 256 + 4 * E:80 * 256 + 5 * E].bitcast(I32)
        small = [ARENA[:, 81 * 256 + k * NSP:81 * 256 + (k + 1) * NSP] for k in range(12)]
        POS, LOF, HIF = (v[:, 0:2 * NT] for v in small[0:3])
        POSI, LOI, HII = (v[:, 0:2 * NT].bitcast(I32) for v in small[3:6])
        PAIR, EMPTY, SLOTW = small[6:9]
        EXT = small[9]
        GIX = sb("GIX", [P, NSP], U32)
        SIX = sb("SIX", [P, NSP], U32)
        EXI = sb("EXI", [P, NSP], I32)
        XD = nc.dram_tensor("moe_in", (B * T, C), F32, kind="Internal").ap()
        YD = nc.dram_tensor("moe_out", (NPAIR + NSP * P, C), F32, kind="Internal").ap()

        at_unit = {}
        for n in range(ROUNDS * NSIDE):
            rnd, k = n // NSIDE, n % NSIDE
            at_unit.setdefault(n - AHEAD, []).append(("scores", rnd, k // (TPC * QPB), k // QPB % TPC, k % QPB))
        for rnd in range(ROUNDS):
            at_unit.setdefault((rnd + 1) * NSIDE + 2 - AHEAD, []).append(("maxima", rnd))
            at_unit.setdefault(min((rnd + 1) * UNITS + 9, NU), []).append(("output", rnd))
        free = NU - AHEAD + 6
        for c in range(NCH):
            at_unit.setdefault(free + c if c < QPB else NU, []).append(("turn", c))
        for c in range(NCH):
            at_unit.setdefault(free + 5 + c if c < QPB else NU, []).append(("project", c))
        every = [op for u in sorted(at_unit) for op in at_unit[u]]
        side_at = {op: k for k, op in enumerate(every)}
        BEFORE = [op for u in sorted(at_unit) if u < 0 for op in at_unit[u]]

        def side_bank(op):
            return bank[side_at[op] % NRING]

        def side_used(op):
            n = side_at[op]
            return S(f"side{n % NRING}_used"), n // NRING + 1

        block = ctx.enter_context(nc.Block())

        class Steps:

            def __init__(self, eng, name):
                self.eng, self.sem, self.n = eng, S(name), 0

            def __call__(self, ins):
                ins.then_inc(self.sem, 1)
                self.n += 1

            def sync(self):
                self.eng.wait_ge(self.sem, self.n)

        @block.sync
        def _(sp):
            xv = x_in.rearrange("b (i p) c -> b p i c", p=P)
            n0 = BLOCKS.index("wf") * P
            sp.dma_start(X[:, 0:TB, :], xv[0]).then_inc(S("x_loaded0"), 16)
            sp.dma_start(VEC[:, :], vec_in).then_inc(S("vec_loaded"), 16)
            sp.dma_start(WT[:, 0:n0], wt_in[:, 0:n0]).then_inc(S("w1_loaded"), 16)
            sp.dma_start(X[:, TB:NT, :], xv[1]).then_inc(S("x_loaded1"), 16)
            sp.dma_start(WT[:, n0:], wt_in[:, n0:]).then_inc(S("w2_loaded"), 16)
            sp.dma_start(ROW[:, :], rows_in).then_inc(S("w2_loaded"), 16)
            sp.dma_start(COS[:, :], cos_in).then_inc(S("rope_loaded"), 16)
            sp.dma_start(SIN[:, :], sin_in).then_inc(S("rope_loaded"), 16)
            sp.dma_start(WG[:, :, :], wg_in).then_inc(S("moe_loaded"), 16)
            sp.dma_start(WU[:, :, :], wu_in).then_inc(S("moe_loaded"), 16)
            sp.dma_start(WD[:, :, :, :], wd_in).then_inc(S("moe_loaded"), 16)
            sp.dma_start(WRT[:, :], wrt_in).then_inc(S("moe_loaded"), 16)
            def load_stacks(g):
                b, h0, slot = g // NG, g % NG * HG, g % 2
                if g == 0:
                    sp.wait_ge(S("stacks_cleared"), 1)
                for k in range(4):
                    sp.wait_ge(S(f"parts_stored{k}"), 48 * (b + 1))
                v = KD.rearrange("(h d) s t -> h (d s) t", d=D)[h0:h0 + HG, :, b * T:(b + 1) * T]
                sp.dma_start(KS[0:STK, slot, :, :], v.rearrange("h r t -> r h t")).then_inc(S(f"stacks_loaded{slot}"), 16)
                for half in range(QPB):
                    c = QPB * b + half
                    v = QD.rearrange("(h d) s t -> h (d s) t", d=D)[h0:h0 + HG, :, c * CH:(c + 1) * CH]
                    sp.dma_start(QS[0:STK, slot, half, :, :], v.rearrange("h r t -> r h t"))\
                      .then_inc(S(f"stacks_loaded{slot}"), 16)

            def place_maxima(rnd):
                sp.wait_ge(*side_used(("maxima", rnd)))
                for k in range(3):
                    dst = QS[MROW + k:MROW + k + 1, rnd // QPB % 2, rnd % QPB, :, :].rearrange("p h (t q) -> p (h t) q", q=P)
                    sp.dma_start(dst, M3T[k * NM:(k + 1) * NM, :]).then_inc(S("maxima_placed"), 16)

            for n in range(2 * NCH):
                c, side = n // 2, n % 2
                sp.wait_ge(S("parts_ready"), n + 1)
                ts = slice(c * CH, (c + 1) * CH)
                src, dst = PARTS[n % 4], (QD, KD)[side]
                at = 0
                for k in (3, 2, 1):
                    if side == 0:
                        s1 = src[:, 3 - k:4 - k, :].to_broadcast([P, k, CH])
                    else:
                        s1 = src[:, 0:k, :]
                    sp.dma_start(dst[:, at:at + k, ts], s1).then_inc(S(f"parts_stored{n % 4}"), 16)
                    at += k
                if n == 3:
                    load_stacks(0)

            load_stacks(1)
            place_maxima(0)
            for g in range(GROUPS):
                place_maxima(2 * g + 1)
                if g + 1 < GROUPS:
                    place_maxima(2 * g + 2)
                if g + 2 < GROUPS:
                    sp.wait_ge(S("scores_filled"), QPB * UNITS * (g + 1))
                    load_stacks(g + 2)
            xd = XD.rearrange("(i p) c -> p i c", p=P)
            for b in range(B):
                sp.wait_ge(S(f"m_in_ready{b}"), 1)
                sp.dma_start(xd[:, b * TB:(b + 1) * TB, :], TM[:, b * TB:(b + 1) * TB, :]).then_inc(S("m_stored"), 16)
            for k in range(NX):
                sp.wait_ge(S(f"written{k}"), 16 * len(range(k, NS, NX)))
            yd = YD[0:NPAIR, :].rearrange("(k i p) c -> k p i c", k=2, p=P)
            for b in range(B):
                ts = slice(b * TB, (b + 1) * TB)
                for k in range(2):
                    sp.dma_start(YK[k][:, ts, :], yd[k][:, ts, :]).then_inc(S(f"y_loaded{b}"), 16)
            ov = out.rearrange("b (i p) c -> b p i c", p=P)
            for b in range(B):
                sp.wait_ge(S(f"x_done{b}"), 1)
                sp.dma_start(ov[b], X[:, b * TB:(b + 1) * TB, :]).then_inc(S("out_stored"), 16)
            sp.wait_ge(S("out_stored"), 32)

        @block.gpsimd
        def _(pool):
            st = Steps(pool, "pool_steps")
            st(pool.memset(XS[:, :, 0:1], 0.0))
            for b in range(B):
                st(pool.memset(MM[b][:, 0:1], NEG))
                st(pool.memset(SS[b][:, 0:1], 1.0))
                last = pool.memset(AA[b][:, 0:1], 0.0)
                if b == B - 1:
                    last.then_inc(S("scan_starts_set"), 1)
                else:
                    st(last)
            pool.wait_ge(S("vec_loaded"), 16)
            pool.wait_ge(S("w1_loaded"), 16)
            for k, name in enumerate(("rk", "rv", "rr", "crr", "crk")):
                st(pool.tensor_scalar(OMV[:, k:k + 1], vec(name), -1.0, 1.0, ALU.mult, ALU.add))
            st.sync()
            for k, name in enumerate(("rk", "rv", "rr", "crr")):
                pool.tensor_scalar(WMA[:, k * P:(k + 1) * P], WT[:, k * P:(k + 1) * P], vec(name), None, ALU.mult)
                pool.tensor_scalar(WMB[:, k * P:(k + 1) * P], WT[:, k * P:(k + 1) * P], OMV[:, k:k + 1], None,
                                   ALU.mult).then_inc(S("mix_scaled"), 1)
            pool.tensor_scalar(WMA[:, 4 * P:8 * P], WT[:, 4 * P:8 * P], vec("crk"), None, ALU.mult)
            pool.tensor_scalar(WMB[:, 4 * P:8 * P], WT[:, 4 * P:8 * P], OMV[:, 4:5], None,
                               ALU.mult).then_inc(S("mix_scaled"), 1)
            pool.wait_ge(S("w1_loaded"), 16)
            pool.tensor_copy(IDB[:, :], ident).then_inc(S("ident_bf16"), 1)
            pool.wait_ge(S("kc_ready"), 4 * NCH)
            st(pool.memset(ARENA[:, 64 * 256:96 * 256], 0.0))
            st.sync()
            pool.memset(KS[MROW:MROW + 3, :, :, :], 1.0).then_inc(S("stacks_cleared"), 1)
            pool.wait_ge(S("stacks_cleared"), 1)
            pool.wait_ge(S("h_filled"), NCH)
            st(pool.memset(ARENA[:, 0:32 * 256], 0.0))
            st.sync()
            pool.memset(VS[:, :, :, D:D + 1], 1.0).then_inc(S("v_cleared"), 1)

            for n in range(2 * NCH):
                t1, t2, parts = RT1[n % 4], RT2[n % 4], PARTS[n % 4]
                pool.wait_ge(S("part0_ready"), n + 1)
                pool.tensor_tensor(t2, t1, parts[:, 0, :], ALU.subtract).then_inc(S("rest_ready"), 1)
                pool.wait_ge(S("part1_ready"), n + 1)
                pool.tensor_tensor(parts[:, 2, :], t2, parts[:, 1, :], ALU.subtract).then_inc(S("parts_ready"), 1)

            def split_maxima(rnd):
                pool.wait_ge(S("maxima_found"), rnd + 1)
                st(pool.tensor_scalar(MQ[:, :], MQ[:, :], -1.0, None, ALU.mult))
                if rnd >= 1:
                    pool.wait_ge(S("side_filled"), side_at[("maxima", rnd - 1)] + 1)
                st.sync()
                st(pool.tensor_copy(M3[:, 0, :], MQ[:, :]))
                st.sync()
                st(pool.tensor_tensor(MR[:, :], MQ[:, :], M3[:, 0, :], ALU.subtract))
                st.sync()
                st(pool.tensor_copy(M3[:, 1, :], MR[:, :]))
                st.sync()
                pool.tensor_tensor(M3[:, 2, :], MR[:, :], M3[:, 1, :], ALU.subtract).then_inc(S("maxima_ready"), 1)

            def place_output(rnd):
                pool.wait_ge(S("denominators_ready"), rnd + 1)
                b, h0, i0 = rnd // QPB // NG, rnd // QPB % NG * HG, (rnd // QPB // NG * QPB + rnd % QPB) * TPC
                dst = OT[:, i0:i0 + TPC, h0 * D:(h0 + HG) * D].rearrange("p t (j d) -> p t j d", d=D)
                pool.tensor_tensor(dst, OC[rnd % 2][:, :, :, 0:D],
                                   RDEN[:, rnd % 2, :, :].unsqueeze(3).to_broadcast([P, TPC, HG, D]), ALU.mult)\
                    .then_inc(S("output_placed"), 1)

            split_maxima(0)
            for rnd in range(1, ROUNDS):
                split_maxima(rnd)
                place_output(rnd - 1)
            place_output(ROUNDS - 1)

            pool.wait_ge(S("m_stored"), 32)
            pool.wait_ge(S("slots_ready"), 1)
            for s in range(NS + LAG):
                if s < NS:
                    if s >= NX:
                        pool.wait_ge(S("x_turned"), s - NX + 1)
                    pool.indirect_dma_start(XG[s % NX], None, XD, bass.IndirectOffsetOnAxis(GIX[:, s:s + 1], 0))\
                        .then_inc(S(f"gathered{s % NX}"), 16)
                if s >= LAG:
                    t = s - LAG
                    pool.wait_ge(S("tile_scaled"), t + 1)
                    pool.indirect_dma_start(YD, bass.IndirectOffsetOnAxis(SIX[:, t:t + 1], 0), YG[t % NX], None)\
                        .then_inc(S(f"written{t % NX}"), 16)

        @block.vector
        def _(dve):
            st = Steps(dve, "dve_steps")

            def stats(tiles, src):
                for i in tiles:
                    st(dve.bn_stats(ST[:, i, :], src(i)))
                st.sync()
                for i in tiles:
                    st(dve.bn_aggr(MV[:, i, :], ST[:, i, :]))
                st.sync()

            def rsqrt(dst, var, tiles):
                lo, hi = tiles[0], tiles[-1] + 1
                v, g, d, y = NV[:, lo:hi], NI[:, lo:hi], ND[:, lo:hi], dst[:, lo:hi]
                st(dve.tensor_scalar(v, var, LN_EPS, None, ALU.add))
                st.sync()
                st(dve.tensor_scalar(g, v.bitcast(I32), 1, None, ALU.logical_shift_right))
                st.sync()
                st(dve.tensor_scalar(y.bitcast(I32), g, -1.0, float(0x5F3759DF), ALU.mult, ALU.add))
                st.sync()
                for _ in range(3):
                    st(dve.tensor_tensor(d, y, y, ALU.mult))
                    st.sync()
                    st(dve.scalar_tensor_tensor(out=d, in0=d, scalar=-0.5, in1=v, op0=ALU.mult, op1=ALU.mult))
                    st.sync()
                    st(dve.scalar_tensor_tensor(out=y, in0=d, scalar=1.5, in1=y, op0=ALU.add, op1=ALU.mult))
                    st.sync()

            def var_of(tiles):
                return MV[:, tiles[0]:tiles[-1] + 1, 1]

            def scaled(tiles, dst, src, r, sem=None):
                for i in tiles:
                    ins = dve.tensor_scalar(dst(i), src(i), MV[:, i, 0:1], r[:, i:i + 1], ALU.subtract, ALU.mult)
                    if sem and i == tiles[-1]:
                        ins.then_inc(S(sem), 1)
                    else:
                        st(ins)

            def tm(i):
                return TM[:, i, :]

            def xt(i):
                return X[:, i, :]

            def add_ln(b, src, nxt):
                tiles = range(b * TB, (b + 1) * TB)
                stats(tiles, src)
                rsqrt(RS, var_of(tiles), tiles)
                scaled(tiles, tm, src, RS)
                st.sync()
                ins = dve.tensor_tensor(X[:, tiles[0]:tiles[-1] + 1, :], X[:, tiles[0]:tiles[-1] + 1, :],
                                        TM[:, tiles[0]:tiles[-1] + 1, :], ALU.add)
                if nxt is None:
                    ins.then_inc(S(f"x_done{b}"), 1)
                    return
                st(ins)
                st.sync()
                stats(tiles, xt)
                rsqrt(RS, var_of(tiles), tiles)
                scaled(tiles, tm, xt, RS, nxt)

            for b in range(B):
                tiles = range(b * TB, (b + 1) * TB)
                dve.wait_ge(S(f"x_loaded{b}"), 16)
                stats(tiles, xt)
                rsqrt(RS, var_of(tiles), tiles)
                r1, r2 = RS[:, tiles[0]:tiles[-1] + 1], RS2[:, tiles[0]:tiles[-1] + 1]
                nd = ND[:, tiles[0]:tiles[-1] + 1]
                st(dve.tensor_tensor(nd, r1, r1, ALU.mult))
                st.sync()
                st(dve.tensor_tensor(nd, nd, var_of(tiles), ALU.mult))
                st.sync()
                rsqrt(RS2, nd, tiles)
                st(dve.tensor_tensor(r2, r2, r1, ALU.mult))
                st.sync()
                scaled(tiles, tm, xt, RS2, f"xa_ready{b}")
                scaled(tiles, lambda i: XN[:, i, :], xt, RS)

            dve.wait_ge(S("scan_starts_set"), 1)
            for b in range(B):
                dve.wait_ge(S("kvr_evacuated"), 6 * b + 2)
                st(dve.tensor_tensor_scan(MM[b][:, 1:], Kc[b], VEC[:, 0:1].to_broadcast([P, T]), NEG,
                                          ALU.max, ALU.add))
                st.sync()
                st(dve.tensor_tensor(DD[b], MM[b][:, 0:T], Kc[b], ALU.subtract))
                st.sync()
                st(dve.tensor_scalar(EA[b], DD[b], 0.0, None, ALU.min))
                dve.tensor_scalar(EB[b], DD[b], 0.0, None, ALU.max).then_inc(S(f"d_ready{b}"), 1)
            for b in range(B):
                dve.wait_ge(S(f"ab_exp{b}"), 1)
                dve.tensor_tensor_scan(SS[b][:, 1:], EA[b], EB[b], 1.0, ALU.mult, ALU.add)\
                   .then_inc(S(f"s_ready{b}"), 1)
            for b in range(B):
                dve.wait_ge(S(f"log_s{b}"), 1)
                st(dve.tensor_tensor(DD[b], DD[b], Kc[b], ALU.add))
                st.sync()
                st(dve.tensor_scalar(EA[b], DD[b], 0.0, None, ALU.min))
                dve.tensor_scalar(EB[b], DD[b], 0.0, None, ALU.max).then_inc(S(f"z_ready{b}"), 1)
            for b in range(B):
                dve.wait_ge(S(f"e_exp{b}"), 1)
                dve.wait_ge(S("kvr_evacuated"), 6 * b + 4)
                st(dve.tensor_tensor(EB[b], EB[b], Vc[b], ALU.mult))
                st.sync()
                st(dve.tensor_tensor_scan(AA[b][:, 1:], EA[b], EB[b], 0.0, ALU.mult, ALU.add))
                st.sync()
                st(dve.tensor_tensor(EA[b], AA[b][:, 0:T], Vc[b], ALU.subtract))
            for b in range(B):
                dve.wait_ge(S(f"sig_z{b}"), 1)
                dve.wait_ge(S("kvr_evacuated"), 6 * b + 6)
                st.sync()
                st(dve.tensor_tensor(EA[b], EA[b], SG[b], ALU.mult))
                st.sync()
                st(dve.tensor_tensor(EA[b], EA[b], Vc[b], ALU.add))
                st.sync()
                dve.tensor_tensor(EB[b], EA[b], SR[b], ALU.mult).then_inc(S(f"y_ready{b}"), 1)

            for b in range(B):
                tiles = range(b * TB, (b + 1) * TB)
                for q in range(QPB):
                    c = QPB * b + q
                    dve.wait_ge(S("y_transposed"), c + 1)
                    v = XN[:, c * TPC:(c + 1) * TPC, :]
                    st(dve.tensor_tensor(v, v, bank[c][:, :].rearrange("p (i c) -> p i c", c=C), ALU.add))
                st.sync()
                stats(tiles, lambda i: XN[:, i, :])
                rsqrt(RS, var_of(tiles), tiles)
                scaled(tiles, tm, lambda i: XN[:, i, :], RS, f"xb_ready{b}")

            def mix_out(c):
                dve.wait_ge(S("cr_sigmoid"), c + 1)
                dve.wait_ge(S("vc_ready"), c + 1)
                o = OUT1[:, c * TPC:(c + 1) * TPC, :]
                dve.tensor_tensor(o, SCR[c % 2].rearrange("p (i c) -> p i c", c=C),
                                  bank[4 + c % 2][:, :].rearrange("p (i c) -> p i c", c=C), ALU.mult)\
                   .then_inc(S("vc_used"), 1)
                dve.wait_ge(S("vc_used"), c + 1)
                st(dve.tensor_tensor(o, o, XN[:, c * TPC:(c + 1) * TPC, :], ALU.add))

            for c in range(NCH + 1):
                if c < NCH:
                    for j in range(4):
                        m = 4 * c + j
                        dve.wait_ge(S("relu_done"), m + 1)
                        if m >= 8:
                            dve.wait_ge(S("vc_ready"), c - 1)
                        dve.tensor_tensor(KC[m % 8], RL[m % 4], RL[m % 4], ALU.mult).then_inc(S("kc_ready"), 1)
                if c >= 1:
                    mix_out(c - 1)
                if c in (QPB, 2 * QPB):
                    st.sync()
                    add_ln(c // QPB - 1, lambda i: OUT1[:, i, :], f"l_in_ready{c // QPB - 1}")

            dve.wait_ge(S("uc0_ready"), 1)
            dve.tensor_tensor(GB0[:, 0:3], bank[7][:, 0:3], VEC[:, VECS.index("bf"):VECS.index("bf") + 3],
                              ALU.add).then_inc(S("gate_bias_ready"), 1)
            for t in range(B):
                for q in range(QPB):
                    k = QPB * t + q
                    dve.wait_ge(S("gates_done"), 3 * k + 3)
                    st(dve.tensor_tensor(IGT[k], IGT[k], GG[k], ALU.mult))
                    new = CST[t][:, q * CH:(q + 1) * CH]
                    if t == 0:
                        st.sync()
                        dve.scalar_tensor_tensor(out=new, in0=FG[k], scalar=vec("in_c"), in1=IGT[k], op0=ALU.mult,
                                                 op1=ALU.add).then_inc(S("cell_ready"), 1)
                    else:
                        st(dve.tensor_tensor(FG[k], FG[k], CST[0][:, q * CH:(q + 1) * CH], ALU.mult))
                        st.sync()
                        dve.tensor_tensor(new, FG[k], IGT[k], ALU.add).then_inc(S("cell_ready"), 1)
            for b in range(B):
                dve.wait_ge(S("h_ready"), QPB * (b + 1))
                add_ln(b, lambda i: HH[:, i, :], f"a_in_ready{b}")
            dve.wait_ge(S("rope_loaded"), 32)
            for c in range(NCH):
                cs = slice(c % QPB * CH, (c % QPB + 1) * CH)
                for side in range(2):
                    n = 2 * c + side
                    names = (("bq", "bqr"), ("bk", "bkr"))[side]
                    t1, t2 = RT1[n % 4], RT2[n % 4]
                    if n >= 4:
                        dve.wait_ge(S("parts_ready"), n - 3)
                    for k, (dst, tab) in enumerate(((t1, COS), (t2, SIN))):
                        m = 2 * n + k
                        dve.wait_ge(S("qk_filled"), m + 1)
                        dve.scalar_tensor_tensor(out=dst, in0=bank[m % 7][:, :], scalar=vec(names[k]),
                                                 in1=tab[:, cs], op0=ALU.add, op1=ALU.mult)\
                           .then_inc(S("qk_used"), 1)
                    dve.wait_ge(S("qk_used"), 2 * n + 2)
                    dve.tensor_tensor(t1, t1, t2, ALU.add).then_inc(S("roped"), 1)

            def denominators(rnd):
                dve.wait_ge(*side_used(("output", rnd)))
                if rnd >= 2:
                    dve.wait_ge(S("output_placed"), rnd - 1)
                dve.reciprocal(RDEN[:, rnd % 2, :, :], OC[rnd % 2][:, :, :, D]).then_inc(S("denominators_ready"), 1)

            def whole_maxima(rnd):
                for k in range(NRING):
                    dve.wait_ge(*side_used(("scores", rnd, HG - 1, TPC - 1 - (k + 1) // 2, (k + 1) % 2)))
                if rnd >= 1:
                    dve.wait_ge(S("maxima_ready"), rnd)
                dve.tensor_tensor(MQ[:, :], MX[:, rnd % 2, :, 0], MX[:, rnd % 2, :, 1], ALU.max)\
                   .then_inc(S("maxima_found"), 1)

            def projected(b):
                for c in range(QPB * b, QPB * (b + 1)):
                    dve.wait_ge(*side_used(("project", c)))
                add_ln(b, lambda i: PO[:, i % TB, :], f"m_in_ready{b}")

            for u in range(-AHEAD, NU + 1):
                for op in at_unit.get(u, ()):
                    if op[0] == "scores":
                        _, rnd, j, qt, kk = op
                        dve.wait_ge(S("side_filled"), side_at[op] + 1)
                        if rnd >= 2 and (j, qt, kk) == (0, 0, 0):
                            dve.wait_ge(S("maxima_ready"), rnd - 1)
                        dve.tensor_reduce(MX[:, rnd % 2, j * TPC + qt, kk:kk + 1], side_bank(op)[:, :], AXX, ALU.max)\
                           .then_inc(side_used(op)[0], 1)
                        if rnd >= 1 and (j, qt, kk) == (0, 0, 1):
                            whole_maxima(rnd - 1)
                        elif (rnd, j, qt, kk) == (ROUNDS - 1, HG - 1, TPC - 1, QPB - 1):
                            whole_maxima(rnd)
                    elif op == ("output", ROUNDS - 1):
                        denominators(ROUNDS - 1)
                    elif op[0] == "project" and op[1] % QPB == QPB - 1:
                        projected(op[1] // QPB)
                if u % UNITS == 14 and u >= UNITS:
                    denominators(u // UNITS - 1)

            for b in range(B):
                ts = slice(b * TB, (b + 1) * TB)
                dve.wait_ge(S("router_filled"), b + 1)
                st(dve.tensor_copy(LG[:, ts, :], bank[(7, 3)[b]][:, 0:TB * E].rearrange("p (i e) -> p i e", e=E)))
                st.sync()
                for i in range(b * TB, (b + 1) * TB):
                    st(dve.max(TOP[:, i, :], LG[:, i, :]))
                st.sync()
                for i in range(b * TB, (b + 1) * TB):
                    st(dve.max_index(TIX[:, i, :], TOP[:, i, :], LG[:, i, :]))
                st.sync()
                st(dve.tensor_copy(TIF[:, :, ts], TIX[:, ts, 0:2].rearrange("p i k -> p k i")))
                dve.tensor_tensor(W12[:, 1, ts], TOP[:, ts, 1], TOP[:, ts, 0], ALU.subtract)\
                   .then_inc(S("logit_gap"), 1)
                st.sync()
                for k in range(2):
                    st(dve.tensor_tensor(CHO[:, k, ts, :], blk("iota")[:, 0:E].unsqueeze(1).to_broadcast([P, TB, E]),
                                         TIF[:, k, ts].unsqueeze(2).to_broadcast([P, TB, E]), ALU.is_equal))
                st.sync()
                dve.tensor_tensor(CHS[:, ts, :], CHO[:, 0, ts, :], CHO[:, 1, ts, :], ALU.add)\
                   .then_inc(S("choices_ready"), 1)

            dve.wait_ge(S("counts_filled"), 1)
            st(dve.tensor_copy(TOT, bank[1][:, 0:NT * E].rearrange("p (i e) -> p e i", e=E)))
            for b in range(B):
                ts = slice(b * TB, (b + 1) * TB)
                dve.wait_ge(S("gap_exp"), b + 1)
                st(dve.tensor_scalar(W12[:, 0, ts], W12[:, 1, ts], 1.0, None, ALU.add))
            st.sync()
            st(dve.tensor_tensor_scan(CUM.rearrange("p e i -> p (e i)"), blk("ones"), TOT.rearrange("p e i -> p (e i)"),
                                      0.0, ALU.mult, ALU.add))
            st(dve.tensor_reduce(NE, TOT, AXX, ALU.add))
            st.sync()
            st(dve.tensor_scalar(NEI, NE, float(P - 1), None, ALU.add))
            st(dve.tensor_tensor(CUM, CUM, TOT, ALU.subtract))
            st.sync()
            st(dve.tensor_scalar(NEI, NEI, P.bit_length() - 1, None, ALU.logical_shift_right))
            st(dve.reciprocal(W12[:, 0, :], W12[:, 0, :]))
            st.sync()
            st(dve.tensor_copy(TE, NEI))
            st(dve.tensor_tensor(W12[:, 1, :], W12[:, 1, :], W12[:, 0, :], ALU.mult))
            st.sync()
            st(dve.tensor_tensor_scan(TEC, blk("ones")[:, 0:E], TE, 0.0, ALU.mult, ALU.add))
            st.sync()
            st(dve.tensor_tensor(OFF, TEC, TE, ALU.subtract))
            st.sync()
            st(dve.scalar_tensor_tensor(out=OFF, in0=OFF, scalar=float(P), in1=CUM[:, :, 0], op0=ALU.mult,
                                        op1=ALU.subtract))
            st.sync()
            st(dve.tensor_tensor(CUM, CUM, OFF.unsqueeze(2).to_broadcast([P, E, NT]), ALU.add))
            st(dve.tensor_tensor(EXC, blk("iota")[:, 0:NSP].unsqueeze(2).to_broadcast([P, NSP, E]),
                                 TEC.unsqueeze(1).to_broadcast([P, NSP, E]), ALU.is_ge))
            st.sync()
            st(dve.tensor_tensor(BASE, CUM.rearrange("p e i -> p i e"),
                                 bank[0][:, 0:NT * E].rearrange("p (i e) -> p i e", e=E), ALU.add))
            st(dve.tensor_reduce(EXT, EXC, AXX, ALU.add))
            st.sync()
            st(dve.tensor_tensor(PPOS.rearrange("p (k i) e -> p k i e", k=2), CHO,
                                 BASE.unsqueeze(1).to_broadcast([P, 2, NT, E]), ALU.mult))
            st(dve.tensor_scalar(EXI[:, :], EXT, float(E - 1), None, ALU.min))
            st.sync()
            st(dve.tensor_reduce(POS, PPOS, AXX, ALU.add))
            st.sync()
            st(dve.tensor_copy(POSI, POS))
            st.sync()
            st(dve.tensor_scalar(LOI, POSI, P - 1, None, ALU.bitwise_and))
            st(dve.tensor_scalar(HII, POSI, P.bit_length() - 1, None, ALU.logical_shift_right))
            st.sync()
            st(dve.tensor_copy(HIF, HII))
            st(dve.tensor_copy(LOF, LOI))
            st.sync()
            st(dve.tensor_tensor(HOH, blk("iota")[:, 0:NSP].unsqueeze(1).to_broadcast([P, 2 * NT, NSP]),
                                 HIF.unsqueeze(2).to_broadcast([P, 2 * NT, NSP]), ALU.is_equal))
            st.sync()
            st(dve.tensor_tensor(HVAL[:, :, 0:NSP], HOH,
                                 blk("slots")[:, NSP:NSP + 2 * NT].unsqueeze(2).to_broadcast([P, 2 * NT, NSP]),
                                 ALU.mult))
            st(dve.tensor_tensor(HVAL[:, :, NSP:], HOH,
                                 W12[:, :, :].rearrange("p k i -> p (k i)").unsqueeze(2).to_broadcast([P, 2 * NT, NSP]),
                                 ALU.mult))
            for k in range(4):
                ns = slice(k * NT // 2, (k + 1) * NT // 2)
                if k == 0:
                    st.sync()
                dve.tensor_tensor(LOH[:, ns, :], blk("iota").unsqueeze(1).to_broadcast([P, NT // 2, P]),
                                  LOF[:, ns].unsqueeze(2).to_broadcast([P, NT // 2, P]), ALU.is_equal)\
                   .then_inc(S("onehots_ready"), 1)
            for k in range(2):
                st(dve.memset(HB[k][:, FI:FIP], 0.0))
            dve.wait_ge(S("table_filled"), 1)
            st(dve.tensor_copy(PAIR, bank[2][:, 0:NSP]))
            st(dve.tensor_copy(SLOTW, bank[2][:, NSP:2 * NSP]))
            st.sync()
            st(dve.tensor_scalar(EMPTY, PAIR, 0.0, None, ALU.is_equal))
            st.sync()
            st(dve.tensor_tensor(EXT, EMPTY, PAIR, ALU.add))
            st(dve.tensor_tensor(EMPTY, EMPTY, blk("slots")[:, 0:NSP], ALU.mult))
            st.sync()
            st(dve.tensor_scalar(GIX[:, :].bitcast(I32), EXT, -1.0, None, ALU.add))
            st(dve.scalar_tensor_tensor(out=SIX[:, :].bitcast(I32), in0=PAIR, scalar=-1.0, in1=EMPTY, op0=ALU.add,
                                        op1=ALU.add))
            st.sync()
            dve.tensor_scalar(GIX[:, :].bitcast(I32), GIX[:, :].bitcast(I32), B * T - 1, None, ALU.bitwise_and)\
               .then_inc(S("slots_ready"), 1)

            for s in range(NS + 1):
                if s < NS:
                    dve.wait_ge(S("x_turned"), s + 1)
                    if s >= 2:
                        dve.wait_ge(S("up_filled"), s - 1)
                    dve.tensor_copy(XC[s % 2], bank[s % 2][:, FIP:]).then_inc(S("xc_ready"), 1)
                if s >= 1:
                    t = s - 1
                    dve.wait_ge(S("silu_done"), t + 1)
                    dve.wait_ge(S("up_filled"), t + 1)
                    if t >= 2:
                        dve.wait_ge(S("h_turned"), t - 1)
                    dve.tensor_tensor(HB[t % 2][:, 0:FI], SL[t % 2], bank[2 + t % 2][:, 0:FI], ALU.mult)\
                       .then_inc(S("hidden_ready"), 1)
            for b in range(B):
                ts = slice(b * TB, (b + 1) * TB)
                dve.wait_ge(S(f"y_loaded{b}"), 32)
                st(dve.tensor_tensor(YK[0][:, ts, :], YK[0][:, ts, :], YK[1][:, ts, :], ALU.add))
                st.sync()
                add_ln(b, lambda i: YK[0][:, i, :], None)

        @block.scalar
        def _(act):
            for c in range(NCH):
                b, q = c // QPB, c % QPB
                act.wait_ge(S("xa_transposed"), c + 1)
                if c == 0:
                    act.wait_ge(S("vec_loaded"), 16)
                act.activation(XS[:, b, 1 + q * CH:1 + (q + 1) * CH], bank[c][:, :], ACT.Identity,
                               bias=vec("b1"), scale=vec("g1")).then_inc(S("xa_evacuated"), 1)
            for n in range(12):
                b, kind, q = n // 6, n % 6 // 2, n % 2
                act.wait_ge(S("kvr_filled"), n + 1)
                dst = (Kc, Vc, SR)[kind][b][:, q * CH:(q + 1) * CH]
                act.activation(dst, bank[(4 + n) % 8][:, :], ACT.Sigmoid if kind == 2 else ACT.Identity)\
                   .then_inc(S("kvr_evacuated"), 1)
            for b in range(B):
                act.wait_ge(S(f"d_ready{b}"), 1)
                act.activation(EA[b], EA[b], ACT.Exp)
                act.activation(EB[b], EB[b], ACT.Exp, scale=-1.0).then_inc(S(f"ab_exp{b}"), 1)
            for b in range(B):
                act.wait_ge(S(f"s_ready{b}"), 1)
                act.activation(Kc[b], SS[b][:, 0:T], ACT.Ln).then_inc(S(f"log_s{b}"), 1)
            for b in range(B):
                act.wait_ge(S(f"z_ready{b}"), 1)
                act.activation(EA[b], EA[b], ACT.Exp)
                act.activation(EB[b], EB[b], ACT.Exp, scale=-1.0).then_inc(S(f"e_exp{b}"), 1)
            act.mul(OMV[:, 5:6], vec("u"), -1.0).then_inc(S("minus_u"), 1)
            act.wait_ge(S("minus_u"), 1)
            for b in range(B):
                act.activation(SG[b], DD[b], ACT.Sigmoid, bias=OMV[:, 5:6]).then_inc(S(f"sig_z{b}"), 1)
            for c in range(NCH):
                b, q = c // QPB, c % QPB
                act.wait_ge(S("xb_transposed"), c + 1)
                act.activation(XS[:, b, 1 + q * CH:1 + (q + 1) * CH], bank[4 + c][:, :], ACT.Identity,
                               bias=vec("b2"), scale=vec("g2")).then_inc(S("xb_evacuated"), 1)
            for c in range(NCH):
                for j in range(4):
                    m = 4 * c + j
                    act.wait_ge(S("kc_filled"), m + 1)
                    if m >= 4:
                        act.wait_ge(S("kc_ready"), m - 3)
                    act.activation(RL[m % 4], bank[m % 4][:, :], ACT.Relu).then_inc(S("relu_done"), 1)
                act.wait_ge(S("cr_filled"), c + 1)
                if c >= 2:
                    act.wait_ge(S("vc_used"), c - 1)
                act.activation(SCR[c % 2], bank[6 + c % 2][:, :], ACT.Sigmoid).then_inc(S("cr_sigmoid"), 1)
            act.wait_ge(S("gate_bias_ready"), 1)
            for b in range(B):
                for q in range(QPB):
                    c = QPB * b + q
                    act.wait_ge(S("l_transposed"), c + 1)
                    act.activation(CT[:, c * CH:(c + 1) * CH], bank[c][:, :], ACT.Identity)\
                       .then_inc(S("l_evacuated"), 1)
                for q in range(QPB):
                    for g in range(3):
                        n = 6 * b + 3 * q + g
                        act.wait_ge(S("gates_filled"), n + 1)
                        dst = (FG, IGT, GG)[g][QPB * b + q]
                        bias = GB0[:, g:g + 1] if b == 0 else vec(("bf", "bi", "bc")[g])
                        act.activation(dst, bank[4 + n % 4][:, :], ACT.Tanh if g == 2 else ACT.Sigmoid, bias=bias)\
                           .then_inc(S("gates_done"), 1)
            for c in range(NCH):
                act.wait_ge(S("h_filled"), c + 1)
                act.activation(HH[:, c * TPC:(c + 1) * TPC, :].rearrange("p i c -> p (i c)"), bank[c][:, :],
                               ACT.Tanh).then_inc(S("h_ready"), 1)
            def part(k, n):
                parts = PARTS[n % 4]
                if k == 0:
                    act.wait_ge(S("roped"), n + 1)
                    if n >= 4:
                        act.wait_ge(S(f"parts_stored{n % 4}"), 48 * (n // 4))
                    act.activation(parts[:, 0, :], RT1[n % 4], ACT.Identity).then_inc(S("part0_ready"), 1)
                else:
                    act.wait_ge(S("rest_ready"), n + 1)
                    act.activation(parts[:, 1, :], RT2[n % 4], ACT.Identity).then_inc(S("part1_ready"), 1)

            for c in range(NCH):
                act.wait_ge(S("a_transposed"), c + 1)
                act.activation(CT[:, c * CH:(c + 1) * CH], bank[7][:, :], ACT.Identity).then_inc(S("a_evacuated"), 1)
            for n in range(2 * NCH + 1):
                if n < 2 * NCH:
                    part(0, n)
                if n >= 1:
                    part(1, n - 1)
            act.wait_ge(S("v_cleared"), 1)
            for c in range(NCH):
                act.wait_ge(S("v_filled"), c + 1)
                act.activation(VS[:, c * TPC:(c + 1) * TPC, :, 0:D],
                               bank[(4 * NCH + c) % 7][:, :].rearrange("p (t h d) -> p t h d", h=H, d=D), ACT.Identity)\
                   .then_inc(S("v_ready"), 1)

            def take_side(op):
                if op[0] == "scores":
                    return
                act.wait_ge(S("side_filled"), side_at[op] + 1)
                o = side_bank(op)
                if op[0] == "maxima":
                    if op[1] >= 1:
                        act.wait_ge(S("maxima_placed"), 48 * op[1])
                    ins = act.activation(M3T[:, :], o[:, :].bitcast(BF16)[0:3 * NM, 0:P], ACT.Identity)
                elif op[0] == "output":
                    if op[1] >= 2:
                        act.wait_ge(S("output_placed"), op[1] - 1)
                    v = o[:, :].rearrange("p (t j e) -> p t j e", j=HG, e=32)
                    ins = act.activation(OC[op[1] % 2], v[:, :, :, 0:D + 1], ACT.Identity)
                elif op[0] == "turn":
                    c = op[1]
                    ins = act.activation(CT[:, c * CH:(c + 1) * CH], o[:, :], ACT.Identity)
                else:
                    c = op[1]
                    if c == QPB:
                        act.wait_ge(S("m_in_ready0"), 1)
                    ins = act.activation(PO[:, c % QPB * TPC:(c % QPB + 1) * TPC, :].rearrange("p i c -> p (i c)"),
                                         o[:, :], ACT.Identity)
                ins.then_inc(side_used(op)[0], 1)

            def evacuate(rnd):
                act.wait_ge(S("av_steps"), TB * (rnd + 1))
                if rnd >= 1:
                    act.wait_ge(S("side_filled"), side_at[("output", rnd - 1)] + 1)
                act.activation(OE, bank[6 + rnd % 2][:, :], ACT.Identity).then_inc(S("o_evacuated"), 1)

            for op in BEFORE:
                take_side(op)
            for k in range(4):
                act.wait_ge(S(f"parts_stored{k}"), 96)
            for u in range(NU):
                act.wait_ge(S("scores_filled"), u + 1)
                if u >= NPT:
                    act.wait_ge(S("av_steps"), (u - NPT) // HG + 1)
                act.activation(PT[u % NPT], bank[3 + u % NRING][:, :], ACT.Exp, scale=SCALE)\
                   .then_inc(S("exp_done"), 1)
                for op in at_unit.get(u, ()):
                    take_side(op)
                if u % UNITS == 4 and u >= UNITS:
                    evacuate(u // UNITS - 1)
            evacuate(ROUNDS - 1)
            for op in at_unit[NU]:
                take_side(op)
            for c in range(NCH):
                act.wait_ge(S("m_transposed"), c + 1)
                act.activation(CT[:, c * CH:(c + 1) * CH], bank[3 + c][:, :], ACT.Identity).then_inc(S("m_evacuated"), 1)
            for b in range(B):
                act.wait_ge(S("logit_gap"), b + 1)
                ts = slice(b * TB, (b + 1) * TB)
                act.activation(W12[:, 1, ts], W12[:, 1, ts], ACT.Exp).then_inc(S("gap_exp"), 1)
            for s in range(NS + 2):
                if s < NS:
                    act.wait_ge(S("gate_filled"), s + 1)
                    if s >= 2:
                        act.wait_ge(S("hidden_ready"), s - 1)
                    act.activation(SL[s % 2], bank[s % 2][:, 0:FI], ACT.Silu).then_inc(S("silu_done"), 1)
                if 1 <= s <= NS:
                    t = s - 1
                    act.wait_ge(S("h_turned"), t + 1)
                    if t >= 2:
                        act.wait_ge(S("down_done"), t - 1)
                    act.activation(HT[t % 2], bank[4 + t % 2][:, 0:FIP], ACT.Identity).then_inc(S("ht_ready"), 1)
                if s >= 2:
                    t = s - 2
                    act.wait_ge(S("down_done"), t + 1)
                    if t >= NX:
                        act.wait_ge(S(f"written{t % NX}"), 16 * (t // NX))
                    act.activation(YG[t % NX], bank[6 + t % 2][:, 0:P], ACT.Identity,
                                   scale=SLOTW[:, t:t + 1]).then_inc(S("tile_scaled"), 1)

        @block.tensor
        def _(pe):
            def transposes(src, c, dst, sem):
                for j in range(TPC):
                    ins = pe.transpose(dst[:, j * P:(j + 1) * P], src(c * TPC + j), ident)
                ins.then_inc(S(sem), 1)

            def tm(i):
                return TM[:, i, :]

            pe.wait_ge(S("w1_loaded"), 16)
            n = 0
            for b in range(B):
                pe.wait_ge(S(f"xa_ready{b}"), 1)
                for q in range(QPB):
                    transposes(tm, QPB * b + q, bank[QPB * b + q], "xa_transposed")
                for kind in range(3):
                    pe.wait_ge(S("mix_scaled"), kind + 1)
                    for q in range(QPB):
                        pe.wait_ge(S("xa_evacuated"), QPB * b + q + 1)
                        if n >= 8:
                            pe.wait_ge(S("kvr_evacuated"), n - 7)
                        o = bank[(4 + n) % 8][:, :]
                        pe.matmul(o, WMA[:, kind * P:(kind + 1) * P], XS[:, b, 1 + q * CH:1 + (q + 1) * CH],
                                  start=True, stop=False)
                        pe.matmul(o, WMB[:, kind * P:(kind + 1) * P], XS[:, b, q * CH:(q + 1) * CH],
                                  start=False, stop=True).then_inc(S("kvr_filled"), 1)
                        n += 1
            for b in range(B):
                pe.wait_ge(S(f"y_ready{b}"), 1)
                if b == 0:
                    pe.wait_ge(S("kvr_evacuated"), 12)
                for q in range(QPB):
                    transposes(lambda i: EB[b][:, (i - b * TB) * P:(i - b * TB + 1) * P], QPB * b + q,
                               bank[QPB * b + q], "y_transposed")
            for b in range(B):
                pe.wait_ge(S(f"xb_ready{b}"), 1)
                for q in range(QPB):
                    transposes(tm, QPB * b + q, bank[4 + QPB * b + q], "xb_transposed")

            def kc_in(c):
                b, q = c // QPB, c % QPB
                pe.wait_ge(S("xb_evacuated"), c + 1)
                for j in range(4):
                    m = 4 * c + j
                    if m == 0:
                        pe.wait_ge(S("mix_scaled"), 5)
                    if m >= 4:
                        pe.wait_ge(S("relu_done"), m - 3)
                    k = 4 + j
                    pe.matmul(bank[m % 4][:, :], WMA[:, k * P:(k + 1) * P], XS[:, b, 1 + q * CH:1 + (q + 1) * CH],
                              start=True, stop=False)
                    pe.matmul(bank[m % 4][:, :], WMB[:, k * P:(k + 1) * P], XS[:, b, q * CH:(q + 1) * CH],
                              start=False, stop=True).then_inc(S("kc_filled"), 1)
                if c == 0:
                    pe.wait_ge(S("xb_evacuated"), NCH)
                if c >= 2:
                    pe.wait_ge(S("cr_sigmoid"), c - 1)
                for i in range(TPC):
                    o = bank[6 + c % 2][:, i * P:(i + 1) * P]
                    at = q * CH + i * P
                    pe.matmul(o, XS[:, b, 1 + at:1 + at + P], WMA[:, 3 * P:4 * P], start=True, stop=False)
                    ins = pe.matmul(o, XS[:, b, at:at + P], WMB[:, 3 * P:4 * P], start=False, stop=True)
                ins.then_inc(S("cr_filled"), 1)

            def kc_out(c):
                pe.wait_ge(S("kc_ready"), 4 * c + 4)
                if c >= 2:
                    pe.wait_ge(S("vc_used"), c - 1)
                for i in range(TPC):
                    for j in range(4):
                        ins = pe.matmul(bank[4 + c % 2][:, i * P:(i + 1) * P], KC[(4 * c + j) % 8][:, i * P:(i + 1) * P],
                                        blk(f"wcv{j}"), start=j == 0, stop=j == 3)
                ins.then_inc(S("vc_ready"), 1)

            for c in range(NCH + 1):
                if c < NCH:
                    kc_in(c)
                if c >= 1:
                    kc_out(c - 1)

            pe.wait_ge(S("w2_loaded"), 32)
            pe.wait_ge(S("cr_sigmoid"), NCH)
            for g, name in enumerate(("uf", "ui", "uc")):
                ins = pe.matmul(bank[7][:, g:g + 1], blk(name), vec("in_c"), start=True, stop=True)
            ins.then_inc(S("uc0_ready"), 1)
            pe.wait_ge(S("relu_done"), 4 * NCH)
            pe.wait_ge(S("vc_used"), NCH)
            pe.wait_ge(S("gate_bias_ready"), 1)
            for b in range(B):
                pe.wait_ge(S(f"l_in_ready{b}"), 1)
                for q in range(QPB):
                    transposes(tm, QPB * b + q, bank[QPB * b + q], "l_transposed")
                for q in range(QPB):
                    c = QPB * b + q
                    pe.wait_ge(S("l_evacuated"), c + 1)
                    if b == 1:
                        pe.wait_ge(S("cell_ready"), q + 1)
                    for g, (wn, un) in enumerate((("wf", "uf"), ("wi", "ui"), ("wc", "uc"))):
                        n = 6 * b + 3 * q + g
                        if n >= 4:
                            pe.wait_ge(S("gates_done"), n - 3)
                        o = bank[4 + n % 4][:, :]
                        ins = pe.matmul(o, blk(wn), CT[:, c * CH:(c + 1) * CH], start=True, stop=b == 0)
                        if b == 1:
                            ins = pe.matmul(o, blk(un), CST[0][:, q * CH:(q + 1) * CH], start=False, stop=True)
                        ins.then_inc(S("gates_filled"), 1)
            for c in range(NCH):
                q = c % QPB
                pe.wait_ge(S("cell_ready"), QPB + q + 1)
                for i in range(TPC):
                    o = bank[c][:, i * P:(i + 1) * P]
                    at = q * CH + i * P
                    pe.matmul(o, blk("row0"), row("bo"), start=True, stop=False)
                    pe.matmul(o, CT[:, c * CH + i * P:c * CH + (i + 1) * P], blk("wo"), start=False, stop=False)
                    ins = pe.matmul(o, CST[1][:, at:at + P], blk("uo"), start=False, stop=True)
                ins.then_inc(S("h_filled"), 1)
            def turn_a(c):
                if c >= 1:
                    pe.wait_ge(S("a_evacuated"), c)
                transposes(tm, c, bank[7], "a_transposed")

            def qk_in(c):
                pe.wait_ge(S("a_evacuated"), c + 1)
                for k, name in enumerate(("aq", "aqr", "ak", "akr")):
                    m = 4 * c + k
                    if m >= 7:
                        pe.wait_ge(S("qk_used"), m - 6)
                    pe.matmul(bank[m % 7][:, :], blk(name), CT[:, c * CH:(c + 1) * CH], start=True, stop=True)\
                      .then_inc(S("qk_filled"), 1)

            for b in range(B):
                pe.wait_ge(S(f"a_in_ready{b}"), 1)
                if b == 0:
                    pe.wait_ge(S("h_ready"), NCH)
                for q in range(QPB):
                    turn_a(QPB * b + q)
                for q in range(QPB):
                    qk_in(QPB * b + q)
            for c in range(NCH):
                m = 4 * NCH + c
                pe.wait_ge(S("qk_used"), m - 6)
                for i in range(TPC):
                    o = bank[m % 7][:, i * P:(i + 1) * P]
                    pe.matmul(o, blk("row0"), row("bv"), start=True, stop=False)
                    ins = pe.matmul(o, CT[:, c * CH + i * P:c * CH + (i + 1) * P], blk("av"), start=False, stop=True)
                ins.then_inc(S("v_filled"), 1)
            pe.wait_ge(S("qk_used"), 4 * NCH)
            pe.wait_ge(S("ident_bf16"), 1)

            def side(op):
                n = side_at[op]
                if n >= NRING:
                    pe.wait_ge(*side_used(every[n - NRING]))
                else:
                    pe.wait_ge(S("v_ready"), NCH)
                o = side_bank(op)
                if op[0] == "scores":
                    _, rnd, j, qt, kk = op
                    g, half = rnd // QPB, rnd % QPB
                    if (half, j, qt, kk) == (0, 0, 0, 0):
                        pe.wait_ge(S(f"stacks_loaded{g % 2}"), 48 * (g // 2 + 1))
                    ins = pe.matmul(o[:, :], QS[0:MROW, g % 2, half, j, qt * P:(qt + 1) * P],
                                    KS[0:MROW, g % 2, j, kk * CH:(kk + 1) * CH], start=True, stop=True)
                elif op[0] == "maxima":
                    pe.wait_ge(S("maxima_ready"), op[1] + 1)
                    ins = pe.transpose(o[:, :].bitcast(BF16)[0:3 * NM, 0:P],
                                       M3[:, :, :].rearrange("p s m -> p (s m)"), IDB[:, :])
                elif op[0] == "output":
                    pe.wait_ge(S("o_evacuated"), op[1] + 1)
                    for t in range(TPC):
                        ins = pe.transpose(o[:, t * P:(t + 1) * P], OE[:, t * P:(t + 1) * P], ident)
                elif op[0] == "turn":
                    c = op[1]
                    pe.wait_ge(S("output_placed"), NG * QPB * (c // QPB + 1))
                    for t in range(TPC):
                        ins = pe.transpose(o[:, t * P:(t + 1) * P], OT[:, c * TPC + t, :], ident)
                else:
                    c = op[1]
                    pe.wait_ge(*side_used(("turn", c)))
                    for i in range(TPC):
                        oi = o[:, i * P:(i + 1) * P]
                        pe.matmul(oi, blk("row0"), row("bao"), start=True, stop=False)
                        ins = pe.matmul(oi, CT[:, c * CH + i * P:c * CH + (i + 1) * P], blk("ao"), start=False,
                                        stop=True)
                ins.then_inc(S("side_filled"), 1)

            def scores(u):
                rnd, kt, j = u // UNITS, u % UNITS // HG, u % HG
                g = rnd // QPB
                if u % UNITS == 0:
                    pe.wait_ge(S("maxima_placed"), 48 * (rnd + 1))
                if u >= NRING:
                    pe.wait_ge(S("exp_done"), u - NRING + 1)
                pe.matmul(bank[3 + u % NRING][:, :], KS[:, g % 2, j, kt * P:(kt + 1) * P],
                          QS[:, g % 2, rnd % QPB, j, :], start=True, stop=True).then_inc(S("scores_filled"), 1)

            def weigh(k):
                rnd, kt = k // TB, k % TB
                g = rnd // QPB
                pe.wait_ge(S("exp_done"), HG * (k + 1))
                if kt == 0 and rnd >= 2:
                    pe.wait_ge(S("o_evacuated"), rnd - 1)
                for j in range(HG):
                    ins = pe.matmul(bank[6 + rnd % 2][32 * j:32 * (j + 1), :],
                                    VS[:, g // NG * TB + kt, g % NG * HG + j, :], PT[(HG * k + j) % NPT],
                                    start=kt == 0, stop=kt == TB - 1)
                ins.then_inc(S("av_steps"), 1)

            for op in BEFORE:
                side(op)
            for u in range(NU):
                scores(u)
                for op in at_unit.get(u, ()):
                    side(op)
                if u % HG == 2 and u >= HG:
                    weigh(u // HG - 1)
            weigh(NU // HG - 1)
            for op in at_unit[NU]:
                side(op)

            pe.wait_ge(S("moe_loaded"), 64)
            for b in range(B):
                pe.wait_ge(S(f"m_in_ready{b}"), 1)
                for q in range(QPB):
                    transposes(tm, QPB * b + q, bank[3 + QPB * b + q], "m_transposed")
            for b in range(B):
                pe.wait_ge(S("m_evacuated"), NCH)
                for i in range(b * TB, (b + 1) * TB):
                    ins = pe.matmul(bank[(7, 3)[b]][:, (i % TB) * E:(i % TB + 1) * E], CT[:, i * P:(i + 1) * P], WRT[:, :],
                                    start=True, stop=True)
                ins.then_inc(S("router_filled"), 1)
            pe.wait_ge(S("choices_ready"), B)
            chosen = CHS.rearrange("p i e -> p (i e)")
            pe.matmul(bank[0][:, 0:NT * E], blk("tri"), chosen, start=True, stop=True)
            pe.matmul(bank[1][:, 0:NT * E], blk("ones"), chosen, start=True, stop=True).then_inc(S("counts_filled"), 1)
            for n in range(2 * NT):
                if n % (NT // 2) == 0:
                    pe.wait_ge(S("onehots_ready"), n // (NT // 2) + 1)
                ins = pe.matmul(bank[2][:, 0:2 * NSP], LOH[:, n, :], HVAL[:, n, :], start=n == 0, stop=n == 2 * NT - 1)
            ins.then_inc(S("table_filled"), 1)

            def turn_x(t):
                pe.wait_ge(S(f"gathered{t % NX}"), 16 * (t // NX + 1))
                if t >= 2:
                    pe.wait_ge(S("silu_done"), t - 1)
                pe.transpose(bank[t % 2][:, FIP:], XG[t % NX], ident).then_inc(S("x_turned"), 1)

            turn_x(0)
            for s in range(NS + 2):
                if s < NS:
                    e = pe.value_load(EXI[0:1, s:s + 1], min_val=0, max_val=E - 1)
                    pe.wait_ge(S("xc_ready"), s + 1)
                    pe.matmul(bank[s % 2][:, 0:FI], XC[s % 2], WG[:, :, :].rearrange("p e f -> p (e f)")[:, bass.ds(e * FI, FI)],
                              start=True, stop=True).then_inc(S("gate_filled"), 1)
                    if s >= 2:
                        pe.wait_ge(S("hidden_ready"), s - 1)
                    pe.matmul(bank[2 + s % 2][:, 0:FI], XC[s % 2], WU[:, :, :].rearrange("p e f -> p (e f)")[:, bass.ds(e * FI, FI)],
                              start=True, stop=True).then_inc(S("up_filled"), 1)
                    if s + 1 < NS:
                        turn_x(s + 1)
                if s >= 2:
                    t = s - 2
                    e = pe.value_load(EXI[0:1, t:t + 1], min_val=0, max_val=E - 1)
                    pe.wait_ge(S("ht_ready"), t + 1)
                    if t >= 2:
                        pe.wait_ge(S("tile_scaled"), t - 1)
                    for j in range(NF):
                        ins = pe.matmul(bank[6 + t % 2][:, 0:P], HT[t % 2][:, j * P:(j + 1) * P],
                                        WD[:, :, :, :].rearrange("p e j c -> p (e j c)")[:, bass.ds(e * (NF * C) + j * C, C)],
                                        start=j == 0, stop=j == NF - 1)
                    ins.then_inc(S("down_done"), 1)
                if 1 <= s <= NS:
                    t = s - 1
                    pe.wait_ge(S("hidden_ready"), t + 1)
                    if t >= 2:
                        pe.wait_ge(S("ht_ready"), t - 1)
                    for j in range(NF):
                        ins = pe.transpose(bank[4 + t % 2][:, j * P:(j + 1) * P], HB[t % 2][:, j * P:(j + 1) * P],
                                           ident)
                    ins.then_inc(S("h_turned"), 1)


_N_OUT = (B, T, C)


def _laid_out(f):
    import numpy as np

    f = {k: np.asarray(v, np.float32) for k, v in f.items()}
    a, l, n = "L0_attn_", "L0_ffn_", "L1_attn_"
    turn = (np.arange(C) // D) * D + (np.arange(C) % D + D // 2) % D
    w = {"wk": f[a + "Wk"].T, "wv": f[a + "Wv"].T, "wr": f[a + "Wr"].T, "wcr": f[a + "Wcr"].T,
         "wf": f[l + "wf"].T, "wi": f[l + "wi"].T, "wc": f[l + "wc"].T, "uf": f[l + "uf"].T, "ui": f[l + "ui"].T,
         "uc": f[l + "uc"].T, "wo": f[l + "wo"].T, "uo": f[l + "uo"].T, "aq": f[n + "Wq"].T, "aqr": f[n + "Wq"][turn].T,
         "ak": f[n + "Wk"].T, "akr": f[n + "Wk"][turn].T, "av": f[n + "Wv"].T, "ao": f[n + "Wo"].T,
         "ident": np.eye(C, dtype=np.float32)}
    for j in range(4):
        w[f"wck{j}"] = f[a + "Wck"].T[:, j * C:(j + 1) * C]
        w[f"wcv{j}"] = f[a + "Wcv"].T[j * C:(j + 1) * C]
    w["row0"] = np.zeros((C, C), np.float32)
    w["row0"][0] = 1.0
    w["ones"] = np.ones((C, C), np.float32)
    w["tri"] = np.triu(np.ones((C, C), np.float32), 1)
    w["iota"] = np.tile(np.arange(C, dtype=np.float32), (C, 1))
    part, pair = np.arange(P)[:, None], np.arange(2 * NT)[None]
    w["slots"] = np.zeros((C, C), np.float32)
    w["slots"][:, 0:NSP] = 1 + NPAIR + np.arange(NSP)[None] * P + part
    w["slots"][:, NSP:NSP + 2 * NT] = 1 + pair * P + part
    v = {"w": f[a + "w"], "u": f[a + "u"], "rk": f[a + "rk"], "rv": f[a + "rv"], "rr": f[a + "rr"],
         "crk": f[a + "crk"], "crr": f[a + "crr"], "g1": f[a + "ln1_g"], "b1": f[a + "ln1_b"], "g2": f[a + "ln2_g"],
         "b2": f[a + "ln2_b"], "bf": f[l + "bf"], "bi": f[l + "bi"], "bc": f[l + "bc"], "in_c": f[l + "in_c"],
         "bq": f[n + "bq"], "bqr": f[n + "bq"][turn], "bk": f[n + "bk"], "bkr": f[n + "bk"][turn]}
    rows = np.zeros((C, len(ROWS) * C), np.float32)
    for k, b in enumerate((f[l + "bo"], f[n + "bv"], f[n + "bo"])):
        rows[0, k * C:(k + 1) * C] = b
    inv = (1.0 / 10000.0 ** (np.arange(0, D, 2, dtype=np.float32) / np.float32(D))).astype(np.float32)
    ang = np.arange(T, dtype=np.float32)[:, None] * inv[None, :]
    ang = np.concatenate([ang, ang], 1).T
    sign = np.where(np.arange(D) < D // 2, -1.0, 1.0).astype(np.float32)[:, None]
    wd = np.zeros((C, E, NF, C), np.float32)
    down = f["L1_ffn_w_down"]
    for j in range(NF):
        part = down[:, :, j * C:(j + 1) * C]
        wd[:part.shape[2], :, j, :] = part.transpose(2, 0, 1)
    return {
        "x": f["L0_attn_x"],
        "wt": np.concatenate([w[k] for k in BLOCKS], 1),
        "vec": np.stack([v[k] for k in VECS], 1),
        "rows": rows,
        "cos": np.tile(np.cos(ang).astype(np.float32), (H, 1)),
        "sin": np.tile((np.sin(ang) * sign).astype(np.float32), (H, 1)),
        "wg": f["L1_ffn_w_gate"].transpose(2, 0, 1),
        "wu": f["L1_ffn_w_up"].transpose(2, 0, 1),
        "wd": wd,
        "wrt": f["L1_ffn_w_router"].T,
    }


def kernel(**inputs):
    import numpy as np
    import concourse.bacc as bacc
    from concourse.bass_utils import run_bass_kernel_spmd

    nc = bacc.Bacc("TRN2", target_bir_lowering=False, num_devices=1)
    arrays, args = {}, []
    for name, a in _laid_out(inputs).items():
        a = np.ascontiguousarray(a)
        arrays[f"in_{name}"] = a
        args.append(nc.dram_tensor(f"in_{name}", a.shape, mybir.dt.from_np(a.dtype), kind="ExternalInput").ap())
    args.append(nc.dram_tensor("out_x", _N_OUT, F32, kind="ExternalOutput").ap())
    sandwich_kernel(nc, *args)
    r = run_bass_kernel_spmd(nc, [arrays], core_ids=[0])
    return r.results[0]["out_x"]
```

```python
from contextlib import ExitStack

import concourse.bass as bass
from concourse import mybir

ALU = mybir.AluOpType
ACT = mybir.ActivationFunctionType
AXX = mybir.AxisListType.X
F32 = mybir.dt.float32
BF16 = mybir.dt.bfloat16
I32 = mybir.dt.int32
U32 = mybir.dt.uint32

B, T, C = 2, 1024, 128
P = 128
NT = B * T // P
TB = T // P
CH = 512
NCH = B * T // CH
QPB = T // CH
TPC = CH // P
H, D = 16, 8
HG = 4
NG = H // HG
E, FI = 8, 352
FIP = 384
NF = FIP // P
LN_EPS = 1e-5
NEG = -1e38
SCALE = float(D) ** -0.5

BLOCKS = ["wk", "wv", "wr", "wcr", "wck0", "wck1", "wck2", "wck3", "wcv0", "wcv1", "wcv2", "wcv3", "ident",
          "wf", "wi", "wc", "uf", "ui", "uc", "wo", "uo", "aq", "aqr", "ak", "akr", "av", "ao", "rows3",
          "ones", "tri", "iota", "slots"]
VECS = ["w", "u", "rk", "rv", "rr", "crk", "crr", "g1", "b1", "g2", "b2", "bf", "bi", "bc", "in_c",
        "bq", "bqr", "bk", "bkr", "e0", "e1", "e2"]
ROWS = ["bo", "bv", "bao"]
NPOOL = 2
Q_PART = (0, 0, 0, 1, 1, 2)
K_PART = (0, 1, 2, 0, 1, 0)
NP6 = len(Q_PART)
Q_OR_K = (0, 1, 1, 0)
STK = D * NP6
STORED = tuple(16 * (3 + side) for side in Q_OR_K)
NPT = 16
GROUPS = B * NG
ROUNDS = GROUPS * QPB
UNITS = TB * HG
NU = ROUNDS * UNITS
NSIDE = HG * TPC * QPB
AHEAD = NSIDE + 16
NRING = 3
NPAIR = 2 * B * T
NS = (NPAIR + E * (P - 1)) // P
NSP = 40
NX = 8
LAG = 6
MROW = 96


def sandwich_kernel(nc, x_in, wt_in, vec_in, rows_in, cos_in, sin_in, wg_in, wu_in, wd_in, wrt_in, out):
    ctx = ExitStack()
    with ctx:
        def sb(name, shape, dt=F32):
            return ctx.enter_context(nc.sbuf_tensor(name, shape, dt))

        sems = {}

        def S(name):
            if name not in sems:
                sems[name] = ctx.enter_context(nc.semaphore(name))
            return sems[name]

        X = sb("X", [P, NT, C])
        XN = sb("XN", [P, NT, C])
        TM = sb("TM", [P, NT, C])
        CT = sb("CT", [P, B * T])
        XS = sb("XS", [P, B, T + 1])
        WT = sb("WT", [P, len(BLOCKS) * P])
        VEC = sb("VEC", [P, len(VECS)])
        ROW = sb("ROW", [P, len(ROWS) * P])
        OMV = sb("OMV", [P, 1])
        BP = sb("BP", [P, 3, len(ROWS) * P], BF16)
        BR = sb("BR", [P, len(ROWS) * P])
        BST = sb("BST", [P, len(ROWS) * P], BF16)
        R3 = sb("R3", [P, P], BF16)
        COS = sb("COS", [P, T])
        SIN = sb("SIN", [P, T])
        WG = sb("WG", [P, E, FI])
        WU = sb("WU", [P, E, FI])
        WD = sb("WD", [P, E, NF, C])
        WRT = sb("WRT", [P, E])
        ST = sb("ST", [P, NT, 6])
        MV = sb("MV", [P, NT, 2])
        RS = sb("RS", [P, NT])
        RS2 = sb("RS2", [P, NT])
        SH = sb("SH", [P, NT])
        NV = sb("NV", [P, NT])
        ND = sb("ND", [P, NT])
        GB0 = sb("GB0", [P, 4])
        ARENA = sb("ARENA", [P, 96 * 256])

        ps01 = [ctx.enter_context(nc.psum_tensor(f"bank{i}", [P, CH], F32)) for i in range(2)]
        PSP = [ctx.enter_context(nc.psum_tensor(f"banks{2 + 2 * i}", [P, 2 * CH], F32)) for i in range(2)]
        ps67 = [ctx.enter_context(nc.psum_tensor(f"bank{6 + i}", [P, CH], F32)) for i in range(2)]
        bank = [ps01[0][:, :], ps01[1][:, :], PSP[0][:, 0:CH], PSP[0][:, CH:], PSP[1][:, 0:CH], PSP[1][:, CH:],
                ps67[0][:, :], ps67[1][:, :]]

        def blk(name):
            k = BLOCKS.index(name)
            return WT[:, k * P:(k + 1) * P]

        def vec(name):
            k = VECS.index(name)
            return VEC[:, k:k + 1]

        def bias(name):
            k = ROWS.index(name)
            return BST[:, k * P:(k + 1) * P].unsqueeze(1).to_broadcast([P, TPC, P])

        ident = blk("ident")

        def arena(kib, n, dt=F32):
            v = ARENA[:, kib * 256:kib * 256 + n]
            return v

        Kc = [arena(0 + 4 * b, T) for b in range(B)]
        Vc = [arena(8 + 4 * b, T) for b in range(B)]
        SR = [arena(16 + 4 * b, T) for b in range(B)]
        DD = [arena(24 + 4 * b, T) for b in range(B)]
        EA = [arena(32 + 4 * b, T) for b in range(B)]
        EB = [arena(40 + 4 * b, T) for b in range(B)]
        MM = [arena(48 + 5 * b, T + 1) for b in range(B)]
        SS = [arena(58 + 5 * b, T + 1) for b in range(B)]
        AA = [arena(68 + 5 * b, T + 1) for b in range(B)]
        SG = [arena(78 + 4 * b, T) for b in range(B)]
        VR = [arena(86 + 4 * b, T) for b in range(B)]
        RL = [arena(86 + 2 * k, CH) for k in range(4)]
        XDF = arena(94, CH)
        XM = [arena(78 + 2 * k, CH) for k in range(8)]
        XKR = [arena(68 + 2 * k, CH) for k in range(8)]
        KC = [arena(2 * k, CH) for k in range(8)]
        SCR = [arena(24 + 2 * k, CH) for k in range(2)]
        OUT1 = arena(32, B * T).rearrange("p (i c) -> p i c", c=C)
        FG = [arena(0 + 2 * k, CH) for k in range(4)]
        IGT = [arena(8 + 2 * k, CH) for k in range(4)]
        GG = [arena(16 + 2 * k, CH) for k in range(4)]
        CST = [arena(24 + 4 * k, T) for k in range(2)]
        HH = arena(40, B * T).rearrange("p (i c) -> p i c", c=C)

        VS = ARENA[:, 0:32 * 256].rearrange("p (i h e) -> p i h e", h=H, e=32)
        PT = [arena(32 + 2 * k, CH) for k in range(NPT)]
        PARTS = [ARENA[:, (48 + 3 * k) * 256:(51 + 3 * k) * 256].bitcast(BF16).rearrange("p (s t) -> p s t", s=3)
                 for k in range(4)]
        QS = ARENA[:, 64 * 256:80 * 256].bitcast(BF16).rearrange("p (s q h t) -> p s q h t", s=2, q=QPB, h=HG)
        KS = ARENA[:, 80 * 256:96 * 256].bitcast(BF16).rearrange("p (s h t) -> p s h t", s=2, h=HG)
        OT = XN
        XSF = XS[:, :, :].rearrange("p b t -> p (b t)")
        RT1 = [arena(32 + 2 * k, CH) for k in range(NCH)]
        RT1 += [TM[:, k * TPC:(k + 1) * TPC, :].rearrange("p i c -> p (i c)") for k in range(NCH)]
        RT2 = [arena(40 + 2 * k, CH) for k in range(NCH)] + [XSF[:, k * CH:(k + 1) * CH] for k in range(NCH)]
        OE = XSF[:, 0:CH]
        OC = [XSF[:, CH + k * 256:CH + k * 256 + TPC * HG * (D + 1)].rearrange("p (t j e) -> p t j e", j=HG, e=D + 1)
              for k in range(2)]
        PO = XSF[:, 2 * CH:4 * CH].rearrange("p (i c) -> p i c", c=C)
        IDB = sb("IDB", [P, P], BF16)
        NM = HG * TPC
        MX = sb("MX", [P, 2, NM, QPB])
        MQ = sb("MQ", [P, NM])
        MR = sb("MR", [P, NM])
        M3 = sb("M3", [P, 3, NM], BF16)
        M3T = sb("M3T", [3 * NM, P], BF16)
        RDEN = sb("RDEN", [P, 2, TPC, HG])
        QD = nc.dram_tensor("q_stacks", (P, NP6, B * T), BF16, kind="Internal").ap()
        KD = nc.dram_tensor("k_stacks", (P, NP6, B * T), BF16, kind="Internal").ap()
        SL = [arena(0 + 2 * k, FIP) for k in range(2)]
        HT = [arena(4 + 2 * k, FIP) for k in range(2)]
        EG = [arena(8 + 2 * k, FIP) for k in range(2)]
        EU = [arena(64 + 2 * k, FIP) for k in range(2)]
        XG = [ARENA[:, (12 * 256 + k * P):(12 * 256 + (k + 1) * P)] for k in range(NX)]
        YG = [ARENA[:, (17 * 256 + k * P):(17 * 256 + (k + 1) * P)] for k in range(NX)]
        XC = [ARENA[:, (16 * 256 + k * P):(16 * 256 + (k + 1) * P)] for k in range(2)]
        LOH = ARENA[:, 28 * 256:36 * 256].bitcast(BF16).rearrange("p (n q) -> p n q", q=P)
        HOH = ARENA[:, 49 * 256:49 * 256 + NT * NSP].bitcast(BF16).rearrange("p (n t) -> p n t", t=NSP)
        HVAL = ARENA[:, 36 * 256:36 * 256 + NT * 5 * NSP].bitcast(BF16).rearrange("p (n v t) -> p n v t", v=5, t=NSP)
        YK = [arena(52 + 8 * k, B * T // 2 * 2).rearrange("p (i c) -> p i c", c=C) for k in range(2)]
        LG = arena(84, NT * E).rearrange("p (i e) -> p i e", e=E)
        TOP = arena(85, NT * 8).rearrange("p (i e) -> p i e", e=8)
        TIX = arena(86, NT * 8).bitcast(U32).rearrange("p (i e) -> p i e", e=8)
        TIF = sb("TIF", [P, 2, NT])
        W12 = sb("W12", [P, 2, NT])
        CHO = arena(72, 2 * NT * E).rearrange("p (k i e) -> p k i e", i=NT, e=E)
        CHS = arena(73, NT * E).rearrange("p (i e) -> p i e", e=E)
        TOT = arena(74, NT * E).rearrange("p (e i) -> p e i", i=NT)
        CUM = arena(75, NT * E).rearrange("p (e i) -> p e i", i=NT)
        BASE = arena(76, NT * E).rearrange("p (i e) -> p i e", e=E)
        PPOS = arena(77, 2 * NT * E).rearrange("p (n e) -> p n e", e=E)
        EXC = arena(78, NSP * E).rearrange("p (t e) -> p t e", e=E)
        NE, TEC, OFF = (ARENA[:, 80 * 256 + k * E:80 * 256 + (k + 1) * E] for k in (0, 2, 3))
        NEI = ARENA[:, 80 * 256 + 4 * E:80 * 256 + 5 * E].bitcast(I32)
        small = [ARENA[:, 81 * 256 + k * NSP:81 * 256 + (k + 1) * NSP] for k in range(12)]
        POS = small[0][:, 0:2 * NT]
        POSI, LOI, HII = (v[:, 0:2 * NT].bitcast(I32) for v in small[3:6])
        PAIR, EMPTY, SLOTW = small[6:9]
        EXT = small[9]
        TAB = arena(60, 5 * NSP).rearrange("p (v t) -> p v t", t=NSP)
        WPT = ARENA[:, 62 * 256:62 * 256 + 3 * NT].bitcast(BF16).rearrange("p (v n) -> p v n", v=3)
        WRS = ARENA[:, 63 * 256:63 * 256 + 2 * NT]
        GIX = sb("GIX", [P, NSP], U32)
        SIX = sb("SIX", [P, NSP], U32)
        EXI = sb("EXI", [P, NSP], I32)
        XD = nc.dram_tensor("moe_in", (B * T, C), F32, kind="Internal").ap()
        YD = nc.dram_tensor("moe_out", (NPAIR + NSP * P, C), F32, kind="Internal").ap()

        at_unit = {}
        for n in range(ROUNDS * NSIDE):
            rnd, k = n // NSIDE, n % NSIDE
            at_unit.setdefault(n - AHEAD, []).append(("scores", rnd, k // (TPC * QPB), k // QPB % TPC, k % QPB))
        for rnd in range(ROUNDS):
            at_unit.setdefault((rnd + 1) * NSIDE + 6 - AHEAD, []).append(("maxima", rnd))
            at_unit.setdefault(min((rnd + 1) * UNITS + 9, NU), []).append(("output", rnd))
        free = NU - AHEAD + 10
        for c in range(NCH):
            at_unit.setdefault(free + c if c < QPB else NU, []).append(("turn", c))
        for c in range(NCH):
            at_unit.setdefault(free + 5 + c if c < QPB else NU, []).append(("project", c))
        every = [op for u in sorted(at_unit) for op in at_unit[u]]
        side_at = {op: k for k, op in enumerate(every)}
        BEFORE = [op for u in sorted(at_unit) if u < 0 for op in at_unit[u]]

        def side_bank(op):
            return bank[side_at[op] % NRING]

        def side_used(op):
            n = side_at[op]
            return S(f"side{n % NRING}_used"), n // NRING + 1

        def parts_ready(n):
            return (S("key_parts_ready"), 1) if n == 2 else (S("parts_ready"), n + 1 - (n > 2))

        def roped(n):
            return (S("roped"), n + 1) if n < NCH else (S("roped_late"), n + 1 - NCH)

        block = ctx.enter_context(nc.Block())

        class Steps:

            def __init__(self, eng, name):
                self.eng, self.sem, self.n = eng, S(name), 0

            def __call__(self, ins):
                ins.then_inc(self.sem, 1)
                self.n += 1

            def sync(self):
                self.eng.wait_ge(self.sem, self.n)

        @block.sync
        def _(sp):
            xv = x_in.rearrange("b (i p) c -> b p i c", p=P)
            n0 = BLOCKS.index("wf") * P
            sp.dma_start(X[:, 0:TB, :], xv[0]).then_inc(S("x_loaded0"), 16)
            sp.dma_start(X[:, TB:NT, :], xv[1]).then_inc(S("x_loaded1"), 16)
            sp.dma_start(VEC[:, :], vec_in).then_inc(S("vec_loaded"), 16)
            sp.dma_start(WT[:, 0:n0], wt_in[:, 0:n0]).then_inc(S("w1_loaded"), 16)
            sp.dma_start(WT[:, n0:], wt_in[:, n0:]).then_inc(S("w2_loaded"), 16)
            sp.dma_start(ROW[:, :], rows_in).then_inc(S("w2_loaded"), 16)
            sp.dma_start(COS[:, :], cos_in).then_inc(S("rope_loaded"), 16)
            sp.dma_start(SIN[:, :], sin_in).then_inc(S("rope_loaded"), 16)
            sp.dma_start(WG[:, :, :], wg_in).then_inc(S("moe_loaded"), 16)
            sp.dma_start(WU[:, :, :], wu_in).then_inc(S("moe_loaded"), 16)
            sp.dma_start(WD[:, :, :, :], wd_in).then_inc(S("moe_loaded"), 16)
            sp.dma_start(WRT[:, :], wrt_in).then_inc(S("moe_loaded"), 16)
            def load_q(g, half, name):
                c = g // NG * QPB + half
                v = QD.rearrange("(h d) s t -> h (d s) t", d=D)[g % NG * HG:(g % NG + 1) * HG, :, c * CH:(c + 1) * CH]
                sp.dma_start(QS[0:STK, g % 2, half, :, :], v.rearrange("h r t -> r h t")).then_inc(S(name), 16)

            def load_stacks(g):
                b = g // NG
                if g == 0:
                    sp.wait_ge(S("stacks_cleared"), 1)
                for k in range(3):
                    sp.wait_ge(S(f"parts_stored{k}"), STORED[k] * (b + 1))
                v = KD.rearrange("(h d) s t -> h (d s) t", d=D)[g % NG * HG:(g % NG + 1) * HG, :, b * T:(b + 1) * T]
                sp.dma_start(KS[0:STK, g % 2, :, :], v.rearrange("h r t -> r h t"))\
                  .then_inc(S(f"stacks_loaded{g % 2}"), 16)
                load_q(g, 0, f"stacks_loaded{g % 2}")

            def load_second(g):
                sp.wait_ge(S("parts_stored3"), STORED[3] * (g // NG + 1))
                load_q(g, 1, f"second_loaded{g % 2}")

            def place_maxima(rnd):
                sp.wait_ge(*side_used(("maxima", rnd)))
                dst = QS[MROW:MROW + 3, rnd // QPB % 2, rnd % QPB, :, :].rearrange("p h (t q) -> p (h t) q", q=P)
                sp.dma_start(dst, M3T[:, :]).then_inc(S("maxima_placed"), 16)

            def store_parts(n, part):
                src, ts = PARTS[n % 4], slice(n // 2 * CH, (n // 2 + 1) * CH)
                if Q_OR_K[n % 4] == 0:
                    dst, at, k = QD, (0, 3, 5)[part], 3 - part
                    moves = [(at, k, src[:, part:part + 1, :].to_broadcast([P, k, CH]))]
                else:
                    dst = KD
                    moves = ([(5, 1, src[:, 0:1, :])], [(3, 2, src[:, 0:2, :]), (0, 2, src[:, 0:2, :])],
                             [(2, 1, src[:, 2:3, :])])[part]
                sp.wait_ge(*((S("part0_ready"), n + 1), (S("part1_ready"), n + 1), parts_ready(n))[part])
                for at, k, v in moves:
                    sp.dma_start(dst[:, at:at + k, ts], v).then_inc(S(f"parts_stored{n % 4}"), 16)

            for n in range(2 * NCH + 2):
                if n < 2 * NCH:
                    store_parts(n, 0)
                if 0 <= n - 1 < 2 * NCH:
                    store_parts(n - 1, 1)
                if n >= 2 and n != 4:
                    store_parts(n - 2, 2)
                if n == 3:
                    store_parts(2, 2)
                    load_stacks(0)
                if n == 5:
                    load_second(0)

            load_stacks(1)
            load_second(1)
            place_maxima(0)
            for g in range(GROUPS):
                place_maxima(2 * g + 1)
                if g + 1 < GROUPS:
                    place_maxima(2 * g + 2)
                if g + 2 < GROUPS:
                    sp.wait_ge(S("scores_filled"), QPB * UNITS * (g + 1))
                    load_stacks(g + 2)
                    load_second(g + 2)
            xd = XD.rearrange("(i p) c -> p i c", p=P)
            for b in range(B):
                sp.wait_ge(S(f"m_in_ready{b}"), 2)
                sp.dma_start(xd[:, b * TB:(b + 1) * TB, :], TM[:, b * TB:(b + 1) * TB, :]).then_inc(S("m_stored"), 16)
            for k in range(NX):
                sp.wait_ge(S(f"written{k}"), 16 * len(range(k, NS, NX)))
            yd = YD[0:NPAIR, :].rearrange("(k i p) c -> k p i c", k=2, p=P)
            for c in range(NCH):
                ts = slice(c * TPC, (c + 1) * TPC)
                for k in range(2):
                    sp.dma_start(YK[k][:, ts, :], yd[k][:, ts, :]).then_inc(S(f"y_loaded{c}"), 16)
            ov = out.rearrange("b (i p) c -> b p i c", p=P)
            for b in range(B):
                sp.wait_ge(S(f"x_done{b}"), 2)
                sp.dma_start(ov[b], X[:, b * TB:(b + 1) * TB, :]).then_inc(S("out_stored"), 16)
            sp.wait_ge(S("out_stored"), 32)

        @block.gpsimd
        def _(pool):
            st = Steps(pool, "pool_steps")
            st(pool.memset(XS[:, :, 0:1], 0.0))
            for b in range(B):
                st(pool.memset(MM[b][:, 0:1], NEG))
                st(pool.memset(SS[b][:, 0:1], 1.0))
                last = pool.memset(AA[b][:, 0:1], 0.0)
                if b == B - 1:
                    last.then_inc(S("scan_starts_set"), 1)
                else:
                    st(last)
            pool.wait_ge(S("w1_loaded"), 16)
            pool.tensor_copy(IDB[:, :], ident).then_inc(S("ident_bf16"), 1)

            def scale_tiles(dst, src, lo, hi, r, sem):
                shape = [P, hi - lo, C]
                st(pool.tensor_tensor(dst[:, lo:hi, :], src, MV[:, lo:hi, 0].unsqueeze(2).to_broadcast(shape),
                                      ALU.subtract))
                st.sync()
                pool.tensor_tensor(dst[:, lo:hi, :], dst[:, lo:hi, :], r[:, lo:hi].unsqueeze(2).to_broadcast(shape),
                                   ALU.mult).then_inc(S(sem), 1)

            def theirs(b):
                return (b + 1) * TB - NPOOL, (b + 1) * TB

            norms, halves = [0], [0]

            def normalise_rest(bs, src, sem, r=RS):
                norms[0] += 1
                pool.wait_ge(S("norm_ready"), norms[0])
                for b in bs:
                    lo, hi = theirs(b)
                    at = 0 if src is PO else b * TB
                    scale_tiles(TM, src[:, lo - b * TB + at:hi - b * TB + at, :], lo, hi, r, sem(b))

            def add_ln_rest(bs, src, nxt):
                norms[0] += 1
                pool.wait_ge(S("norm_ready"), norms[0])
                for b in bs:
                    lo, hi = theirs(b)
                    at = 0 if src is PO else b * TB
                    if nxt:
                        st(pool.tensor_tensor(TM[:, lo:hi, :], src[:, lo - b * TB + at:hi - b * TB + at, :],
                                              RS[:, lo:hi].unsqueeze(2).to_broadcast([P, hi - lo, C]), ALU.mult))
                        st.sync()
                    else:
                        halves[0] += 1
                        scale_tiles(TM, src[:, lo:hi, :], lo, hi, RS, "pool_normed")
                        pool.wait_ge(S("pool_normed"), halves[0])
                    pool.tensor_tensor(X[:, lo:hi, :], X[:, lo:hi, :], TM[:, lo:hi, :], ALU.add)\
                        .then_inc(S("pool_added") if nxt else S(f"x_done{b}"), 1)
                if nxt:
                    normalise_rest(bs, X, lambda b: f"{nxt}{b}")

            both = range(B)
            normalise_rest(both, X, lambda b: f"xa_ready{b}", RS2)
            for b in both:
                scale_tiles(XN, X[:, b * TB:(b + 1) * TB, :], b * TB, (b + 1) * TB, RS, f"xn_ready{b}")
            pool.wait_ge(S("w2_loaded"), 32)
            st(pool.tensor_copy(R3[:, :], blk("rows3")))
            st(pool.tensor_copy(BP[:, 0, :], ROW[:, :]))
            st.sync()
            st(pool.tensor_tensor(BR[:, :], ROW[:, :], BP[:, 0, :], ALU.subtract))
            st.sync()
            st(pool.tensor_copy(BP[:, 1, :], BR[:, :]))
            st.sync()
            st(pool.tensor_tensor(BP[:, 2, :], BR[:, :], BP[:, 1, :], ALU.subtract))
            st.sync()
            for k in range(3):
                st(pool.tensor_scalar(BP[:, k, :], BP[:, k, :], vec(f"e{k}"), None, ALU.mult))
            st.sync()
            st(pool.tensor_tensor(BST[:, :], BP[:, 0, :], BP[:, 1, :], ALU.add))
            st.sync()
            pool.tensor_tensor(BST[:, :], BST[:, :], BP[:, 2, :], ALU.add).then_inc(S("biases_ready"), 1)
            pool.wait_ge(S("kvr_evacuated"), 6 * B)
            for b in both:
                pool.tensor_tensor(VR[b], Vc[b], SR[b], ALU.mult).then_inc(S("vr_ready"), 1)
            for b in both:
                pool.wait_ge(S(f"sig_z{b}"), 1)
                pool.tensor_tensor(SG[b], SG[b], SR[b], ALU.mult).then_inc(S(f"past_weight{b}"), 1)
            normalise_rest(both, XN, lambda b: f"xb_ready{b}")
            for b in both:
                add_ln_rest([b], OUT1, "l_in_ready")
            pool.wait_ge(S("kc_ready"), 4 * NCH)
            st(pool.memset(ARENA[:, 64 * 256:96 * 256], 0.0))
            st.sync()
            pool.memset(KS[MROW:MROW + 3, :, :, :], 1.0).then_inc(S("stacks_cleared"), 1)
            pool.wait_ge(S("stacks_cleared"), 1)
            pool.wait_ge(S("h_filled"), NCH)
            st(pool.memset(ARENA[:, 0:32 * 256], 0.0))
            st.sync()
            pool.memset(VS[:, :, :, D:D + 1], 1.0).then_inc(S("v_cleared"), 1)

            add_ln_rest(both, HH, "a_in_ready")

            for n in range(2 * NCH + 1):
                if NCH <= n + 1 < 2 * NCH:
                    t1, t2 = RT1[n + 1], RT2[n + 1]
                    pool.wait_ge(S("qk_used"), 2 * n + 4)
                    pool.tensor_tensor(t1, t1, t2, ALU.add).then_inc(roped(n + 1)[0], 1)
                if n < 2 * NCH:
                    pool.wait_ge(S("part0_ready"), n + 1)
                    pool.tensor_tensor(RT2[n], RT1[n], PARTS[n % 4][:, 0, :], ALU.subtract)\
                        .then_inc(S("rest_ready"), 1)
                if n >= 1 and n - 1 != 2:
                    k = n - 1
                    pool.wait_ge(S("part1_ready"), k + 1)
                    pool.tensor_tensor(PARTS[k % 4][:, 2, :], RT2[k], PARTS[k % 4][:, 1, :], ALU.subtract)\
                        .then_inc(parts_ready(k)[0], 1)

            def split_maxima(rnd):
                pool.wait_ge(S("maxima_found"), rnd + 1)
                st(pool.tensor_scalar(MQ[:, :], MQ[:, :], -1.0, None, ALU.mult))
                if rnd >= 1:
                    pool.wait_ge(S("side_filled"), side_at[("maxima", rnd - 1)] + 1)
                st.sync()
                st(pool.tensor_copy(M3[:, 0, :], MQ[:, :]))
                st.sync()
                st(pool.tensor_tensor(MR[:, :], MQ[:, :], M3[:, 0, :], ALU.subtract))
                st.sync()
                st(pool.tensor_copy(M3[:, 1, :], MR[:, :]))
                st.sync()
                pool.tensor_tensor(M3[:, 2, :], MR[:, :], M3[:, 1, :], ALU.subtract).then_inc(S("maxima_ready"), 1)

            def place_output(rnd):
                pool.wait_ge(S("denominators_ready"), rnd + 1)
                b, h0, i0 = rnd // QPB // NG, rnd // QPB % NG * HG, (rnd // QPB // NG * QPB + rnd % QPB) * TPC
                dst = OT[:, i0:i0 + TPC, h0 * D:(h0 + HG) * D].rearrange("p t (j d) -> p t j d", d=D)
                pool.tensor_tensor(dst, OC[rnd % 2][:, :, :, 0:D],
                                   RDEN[:, rnd % 2, :, :].unsqueeze(3).to_broadcast([P, TPC, HG, D]), ALU.mult)\
                    .then_inc(S("output_placed"), 1)

            split_maxima(0)
            for rnd in range(1, ROUNDS):
                split_maxima(rnd)
                if rnd == ROUNDS - 1:
                    add_ln_rest([0], PO, "m_in_ready")
                place_output(rnd - 1)
            place_output(ROUNDS - 1)
            add_ln_rest([1], PO, "m_in_ready")

            pool.wait_ge(S("choice_weights"), 1)
            w12 = W12[:, :, :].rearrange("p k i -> p (k i)")
            st(pool.tensor_copy(WPT[:, 0, :], w12))
            st.sync()
            st(pool.tensor_tensor(WRS, w12, WPT[:, 0, :], ALU.subtract))
            st.sync()
            st(pool.tensor_copy(WPT[:, 1, :], WRS))
            st.sync()
            pool.tensor_tensor(WPT[:, 2, :], WRS, WPT[:, 1, :], ALU.subtract).then_inc(S("weight_parts"), 1)
            pool.wait_ge(S("tile_onehots"), 1)
            for v in range(2):
                num = blk("slots")[:, NSP + v * 2 * NT:NSP + (v + 1) * 2 * NT]
                pool.tensor_tensor(HVAL[:, :, v, :], HOH, num.unsqueeze(2).to_broadcast([P, 2 * NT, NSP]), ALU.mult)\
                    .then_inc(S("pair_numbers"), 1)

            pool.wait_ge(S("m_stored"), 32)
            pool.wait_ge(S("slots_ready"), 1)
            for s in range(NS + LAG):
                if s < NS:
                    if s >= NX:
                        pool.wait_ge(S("x_turned"), s - NX + 1)
                    pool.indirect_dma_start(XG[s % NX], None, XD, bass.IndirectOffsetOnAxis(GIX[:, s:s + 1], 0))\
                        .then_inc(S(f"gathered{s % NX}"), 16)
                if s >= LAG:
                    t = s - LAG
                    pool.wait_ge(S("tile_scaled"), t + 1)
                    pool.indirect_dma_start(YD, bass.IndirectOffsetOnAxis(SIX[:, t:t + 1], 0), YG[t % NX], None)\
                        .then_inc(S(f"written{t % NX}"), 16)
            add_ln_rest(both, YK[0], None)

        @block.vector
        def _(dve):
            st = Steps(dve, "dve_steps")

            def stats(tiles, src):
                for i in tiles:
                    st(dve.bn_stats(ST[:, i, :], src(i)))
                st.sync()
                for i in tiles:
                    st(dve.bn_aggr(MV[:, i, :], ST[:, i, :]))
                st.sync()

            def rsqrt(dst, var, tiles, sem=None):
                lo, hi = tiles[0], tiles[-1] + 1
                v, d, y = NV[:, lo:hi], ND[:, lo:hi], dst[:, lo:hi]
                st(dve.tensor_scalar(v, var, LN_EPS, None, ALU.add))
                st.sync()
                st(dve.tensor_scalar(y.bitcast(I32), v.bitcast(I32), -0.5, float(0x5F3759DF), ALU.mult, ALU.add))
                st.sync()
                for k in range(3):
                    st(dve.tensor_tensor(d, y, y, ALU.mult))
                    st.sync()
                    st(dve.scalar_tensor_tensor(out=d, in0=d, scalar=-0.5, in1=v, op0=ALU.mult, op1=ALU.mult))
                    st.sync()
                    ins = dve.scalar_tensor_tensor(out=y, in0=d, scalar=1.5, in1=y, op0=ALU.add, op1=ALU.mult)
                    if sem and k == 2:
                        ins.then_inc(S(sem), 1)
                    else:
                        st(ins)
                        st.sync()

            def var_of(tiles):
                return MV[:, tiles[0]:tiles[-1] + 1, 1]

            norms = [0]

            def await_norms():
                norms[0] += 1
                dve.wait_ge(S("norm_ready"), norms[0])

            def normalise(bs, src, r, sem=None):
                for b in bs:
                    for i in own(b):
                        ins = dve.tensor_scalar(TM[:, i, :], src(i), MV[:, i, 0:1], r[:, i:i + 1], ALU.subtract,
                                                ALU.mult)
                        if sem and i == own(b)[-1]:
                            ins.then_inc(S(f"{sem}{b}"), 1)
                        else:
                            st(ins)

            def own(b):
                return range(b * TB, (b + 1) * TB - NPOOL)

            def rest(b):
                return range((b + 1) * TB - NPOOL, (b + 1) * TB)

            def tm(i):
                return TM[:, i, :]

            def xt(i):
                return X[:, i, :]

            added = [0]

            def add_ln(bs, src, nxt, first=False):
                tiles = range(bs[0] * TB, (bs[-1] + 1) * TB)
                if nxt:
                    for i in tiles:
                        st(dve.bn_stats(ST[:, i, :], src(i)))
                    st.sync()
                for i in tiles:
                    st(dve.bn_aggr(MV[:, i, :], ST[:, i, :]))
                st.sync()
                rsqrt(RS, var_of(tiles), tiles, "norm_ready")
                await_norms()
                lo, hi = tiles[0], tiles[-1] + 1
                if nxt:
                    new = SH if first else ND
                    st(dve.tensor_tensor(new[:, lo:hi], MV[:, lo:hi, 0], RS[:, lo:hi], ALU.mult))
                    for b in bs:
                        for i in own(b):
                            st(dve.scalar_tensor_tensor(out=X[:, i, :], in0=src(i), scalar=RS[:, i:i + 1],
                                                        in1=X[:, i, :], op0=ALU.mult, op1=ALU.add))
                    if not first:
                        st.sync()
                        st(dve.tensor_tensor(SH[:, lo:hi], SH[:, lo:hi], ND[:, lo:hi], ALU.add))
                for b in bs:
                    if nxt is None:
                        normalise([b], src, RS)
                        st.sync()
                        xs = X[:, own(b)[0]:own(b)[-1] + 1, :]
                        dve.tensor_tensor(xs, xs, TM[:, own(b)[0]:own(b)[-1] + 1, :], ALU.add)\
                           .then_inc(S(f"x_done{b}"), 1)
                if nxt is None:
                    return
                st.sync()
                for b in bs:
                    for i in own(b):
                        st(dve.bn_stats(ST[:, i, :], xt(i)))
                for b in bs:
                    added[0] += 1
                    dve.wait_ge(S("pool_added"), added[0])
                    for i in rest(b):
                        st(dve.bn_stats(ST[:, i, :], xt(i)))
                st.sync()
                for i in tiles:
                    st(dve.bn_aggr(MV[:, i, :], ST[:, i, :]))
                st.sync()
                rsqrt(RS, var_of(tiles), tiles, "norm_ready")
                await_norms()
                normalise(bs, xt, RS, nxt)

            def difference(c):
                b, q = c // QPB, c % QPB
                st.sync()
                st(dve.tensor_tensor(XDF, XS[:, b, 1 + q * CH:1 + (q + 1) * CH], XS[:, b, q * CH:(q + 1) * CH],
                                     ALU.subtract))
                st.sync()

            def mixed(dst, c, name, sem):
                b, q = c // QPB, c % QPB
                dve.scalar_tensor_tensor(out=dst, in0=XDF, scalar=vec(name), in1=XS[:, b, q * CH:(q + 1) * CH],
                                         op0=ALU.mult, op1=ALU.add).then_inc(S(sem), 1)

            both, tiles = range(B), range(NT)
            for b in both:
                dve.wait_ge(S(f"x_loaded{b}"), 16)
                for i in range(b * TB, (b + 1) * TB):
                    st(dve.bn_stats(ST[:, i, :], xt(i)))
            st.sync()
            for i in tiles:
                st(dve.bn_aggr(MV[:, i, :], ST[:, i, :]))
            st.sync()
            rsqrt(RS, var_of(tiles), tiles)
            st(dve.tensor_tensor(ND[:, :], RS[:, :], RS[:, :], ALU.mult))
            st.sync()
            st(dve.tensor_tensor(ND[:, :], ND[:, :], var_of(tiles), ALU.mult))
            st.sync()
            rsqrt(RS2, ND[:, :], tiles)
            dve.tensor_tensor(RS2[:, :], RS2[:, :], RS[:, :], ALU.mult).then_inc(S("norm_ready"), 1)
            await_norms()
            normalise(both, xt, RS2, "xa_ready")
            dve.wait_ge(S("vec_loaded"), 16)
            for c in range(NCH):
                dve.wait_ge(S("xa_evacuated"), c + 1)
                if c >= 1:
                    dve.wait_ge(S("mixed_kvr"), 3 * c)
                difference(c)
                for kind, name in enumerate(("rk", "rv", "rr")):
                    n = 3 * c + kind
                    if n >= 8:
                        dve.wait_ge(S("kvr_filled"), n - 7)
                    mixed(XM[n % 8], c, name, "mixed_kvr")

            dve.wait_ge(S("scan_starts_set"), 1)
            for b in range(B):
                dve.wait_ge(S("kvr_evacuated"), 6 * b + 4)
                st(dve.tensor_tensor_scan(MM[b][:, 1:], Kc[b], VEC[:, 0:1].to_broadcast([P, T]), NEG,
                                          ALU.max, ALU.add))
                st.sync()
                st(dve.tensor_tensor(DD[b], MM[b][:, 0:T], Kc[b], ALU.subtract))
                st.sync()
                st(dve.tensor_scalar(EA[b], DD[b], 0.0, None, ALU.min))
                dve.tensor_scalar(EB[b], DD[b], 0.0, None, ALU.max).then_inc(S(f"d_ready{b}"), 1)
            for b in range(B):
                dve.wait_ge(S(f"ab_exp{b}"), 1)
                dve.tensor_tensor_scan(SS[b][:, 1:], EA[b], EB[b], 1.0, ALU.mult, ALU.add)\
                   .then_inc(S(f"s_ready{b}"), 1)
            for b in range(B):
                dve.wait_ge(S(f"log_s{b}"), 1)
                st(dve.tensor_tensor(DD[b], DD[b], Kc[b], ALU.add))
                st.sync()
                st(dve.tensor_scalar(EA[b], DD[b], 0.0, None, ALU.min))
                dve.tensor_scalar(EB[b], DD[b], 0.0, None, ALU.max).then_inc(S(f"z_ready{b}"), 1)
            for b in range(B):
                dve.wait_ge(S(f"e_exp{b}"), 1)
                dve.wait_ge(S("kvr_evacuated"), 6 * b + 5)
                st(dve.tensor_tensor(EB[b], EB[b], Vc[b], ALU.mult))
                st.sync()
                st(dve.tensor_tensor_scan(AA[b][:, 1:], EA[b], EB[b], 0.0, ALU.mult, ALU.add))
                st.sync()
                st(dve.tensor_tensor(EA[b], AA[b][:, 0:T], Vc[b], ALU.subtract))
            for b in range(B):
                dve.wait_ge(S(f"past_weight{b}"), 1)
                dve.wait_ge(S("vr_ready"), b + 1)
                st.sync()
                st(dve.tensor_tensor(EA[b], EA[b], SG[b], ALU.mult))
                st.sync()
                dve.tensor_tensor(EB[b], EA[b], VR[b], ALU.add).then_inc(S(f"y_ready{b}"), 1)

            dve.wait_ge(S("uc0_ready"), 1)
            dve.tensor_tensor(GB0[:, 0:3], bank[4][:, 0:3], VEC[:, VECS.index("bf"):VECS.index("bf") + 3],
                              ALU.add).then_inc(S("gate_bias_ready"), 1)
            for c in range(NCH):
                if c % QPB == 0:
                    dve.wait_ge(S(f"xn_ready{c // QPB}"), 1)
                dve.wait_ge(S("y_transposed"), c + 1)
                v = XN[:, c * TPC:(c + 1) * TPC, :]
                st(dve.tensor_tensor(v, v, bank[c][:, :].rearrange("p (i c) -> p i c", c=C), ALU.add))
            st.sync()
            stats(tiles, lambda i: XN[:, i, :])
            rsqrt(RS, var_of(tiles), tiles, "norm_ready")
            await_norms()
            normalise(both, lambda i: XN[:, i, :], RS, "xb_ready")

            def channel_input(c):
                dve.wait_ge(S("xb_evacuated"), c + 1)
                if c >= 1:
                    dve.wait_ge(S("mixed_cm"), 2 * c)
                difference(c)
                for kind, name in enumerate(("crk", "crr")):
                    mixed(XKR[2 * c + kind], c, name, "mixed_cm")

            for c in range(NCH):
                channel_input(c)

            def mix_out(c):
                dve.wait_ge(S("cr_sigmoid"), c + 1)
                dve.wait_ge(S("vc_ready"), c + 1)
                o = OUT1[:, c * TPC:(c + 1) * TPC, :]
                dve.tensor_tensor(o, SCR[c % 2].rearrange("p (i c) -> p i c", c=C),
                                  bank[4 + c % 2][:, :].rearrange("p (i c) -> p i c", c=C), ALU.mult)\
                   .then_inc(S("vc_used"), 1)
                dve.wait_ge(S("vc_used"), c + 1)
                st(dve.tensor_tensor(o, o, XN[:, c * TPC:(c + 1) * TPC, :], ALU.add))

            for c in range(NCH + 1):
                if c >= 1:
                    mix_out(c - 1)
                if c in (QPB, 2 * QPB):
                    st.sync()
                    add_ln([c // QPB - 1], lambda i: OUT1[:, i, :], "l_in_ready", first=True)

            for t in range(B):
                for q in range(QPB):
                    k = QPB * t + q
                    dve.wait_ge(S("gates_done"), 3 * k + 3)
                    st(dve.tensor_tensor(IGT[k], IGT[k], GG[k], ALU.mult))
                    new = CST[t][:, q * CH:(q + 1) * CH]
                    if t == 0:
                        st.sync()
                        dve.scalar_tensor_tensor(out=new, in0=FG[k], scalar=vec("in_c"), in1=IGT[k], op0=ALU.mult,
                                                 op1=ALU.add).then_inc(S("cell_ready"), 1)
                    else:
                        st(dve.tensor_tensor(FG[k], FG[k], CST[0][:, q * CH:(q + 1) * CH], ALU.mult))
                        st.sync()
                        dve.tensor_tensor(new, FG[k], IGT[k], ALU.add).then_inc(S("cell_ready"), 1)
            dve.wait_ge(S("h_ready"), NCH)
            add_ln(both, lambda i: HH[:, i, :], "a_in_ready")
            dve.wait_ge(S("rope_loaded"), 32)
            for c in range(NCH):
                cs = slice(c % QPB * CH, (c % QPB + 1) * CH)
                for side in Q_OR_K[c % 2 * 2:c % 2 * 2 + 2]:
                    n = 2 * c + (side != Q_OR_K[c % 2 * 2])
                    names = (("bq", "bqr"), ("bk", "bkr"))[side]
                    t1, t2 = RT1[n], RT2[n]
                    for k, (dst, tab) in enumerate(((t1, COS), (t2, SIN))):
                        m = 2 * n + k
                        dve.wait_ge(S("qk_filled"), m + 1)
                        dve.scalar_tensor_tensor(out=dst, in0=bank[m % 7][:, :], scalar=vec(names[k]),
                                                 in1=tab[:, cs], op0=ALU.add, op1=ALU.mult)\
                           .then_inc(S("qk_used"), 1)
                    if n < NCH:
                        dve.wait_ge(S("qk_used"), 2 * n + 2)
                        dve.tensor_tensor(t1, t1, t2, ALU.add).then_inc(roped(n)[0], 1)
                    if n == 3:
                        dve.wait_ge(S("part1_ready"), 3)
                        dve.tensor_tensor(PARTS[2][:, 2, :], RT2[2], PARTS[2][:, 1, :], ALU.subtract)\
                           .then_inc(parts_ready(2)[0], 1)

            def denominators(rnd):
                dve.wait_ge(*side_used(("output", rnd)))
                if rnd >= 2:
                    dve.wait_ge(S("output_placed"), rnd - 1)
                dve.reciprocal(RDEN[:, rnd % 2, :, :], OC[rnd % 2][:, :, :, D]).then_inc(S("denominators_ready"), 1)

            def whole_maxima(rnd):
                for k in range(NRING):
                    dve.wait_ge(*side_used(("scores", rnd, HG - 1, TPC - 1 - (k + 1) // 2, (k + 1) % 2)))
                if rnd >= 1:
                    dve.wait_ge(S("maxima_ready"), rnd)
                dve.tensor_tensor(MQ[:, :], MX[:, rnd % 2, :, 0], MX[:, rnd % 2, :, 1], ALU.max)\
                   .then_inc(S("maxima_found"), 1)

            def projected(b):
                for c in range(QPB * b, QPB * (b + 1)):
                    dve.wait_ge(*side_used(("project", c)))
                add_ln([b], lambda i: PO[:, i % TB, :], "m_in_ready")

            def choose(b):
                ts = slice(b * TB, (b + 1) * TB)
                dve.wait_ge(S("router_filled"), b + 1)
                st(dve.tensor_copy(LG[:, ts, :], bank[(5, 3)[b]][:, 0:TB * E].rearrange("p (i e) -> p i e", e=E)))
                st.sync()
                for i in range(b * TB, (b + 1) * TB):
                    st(dve.max(TOP[:, i, :], LG[:, i, :]))
                st.sync()
                for i in range(b * TB, (b + 1) * TB):
                    st(dve.max_index(TIX[:, i, :], TOP[:, i, :], LG[:, i, :]))
                st.sync()
                st(dve.tensor_copy(TIF[:, :, ts], TIX[:, ts, 0:2].rearrange("p i k -> p k i")))
                dve.tensor_tensor(W12[:, 1, ts], TOP[:, ts, 1], TOP[:, ts, 0], ALU.subtract)\
                   .then_inc(S("logit_gap"), 1)
                st.sync()
                for k in range(2):
                    st(dve.tensor_tensor(CHO[:, k, ts, :], blk("iota")[:, 0:E].unsqueeze(1).to_broadcast([P, TB, E]),
                                         TIF[:, k, ts].unsqueeze(2).to_broadcast([P, TB, E]), ALU.is_equal))
                st.sync()
                dve.tensor_tensor(CHS[:, ts, :], CHO[:, 0, ts, :], CHO[:, 1, ts, :], ALU.add)\
                   .then_inc(S("choices_ready"), 1)

            for u in range(-AHEAD, NU + 1):
                for op in at_unit.get(u, ()):
                    if op[0] == "scores":
                        _, rnd, j, qt, kk = op
                        dve.wait_ge(S("side_filled"), side_at[op] + 1)
                        if rnd >= 2 and (j, qt, kk) == (0, 0, 0):
                            dve.wait_ge(S("maxima_ready"), rnd - 1)
                        dve.tensor_reduce(MX[:, rnd % 2, j * TPC + qt, kk:kk + 1], side_bank(op)[:, :], AXX, ALU.max)\
                           .then_inc(side_used(op)[0], 1)
                        if rnd >= 1 and (j, qt, kk) == (0, 0, 1):
                            whole_maxima(rnd - 1)
                        elif (rnd, j, qt, kk) == (ROUNDS - 1, HG - 1, TPC - 1, QPB - 1):
                            whole_maxima(rnd)
                    elif op == ("output", ROUNDS - 1):
                        denominators(ROUNDS - 1)
                        choose(0)
                    elif op[0] == "project" and op[1] % QPB == QPB - 1:
                        projected(op[1] // QPB)
                if u % UNITS == 14 and u >= UNITS:
                    denominators(u // UNITS - 1)

            choose(1)

            dve.wait_ge(S("counts_filled"), 1)
            st(dve.tensor_copy(TOT, bank[1][:, 0:NT * E].rearrange("p (i e) -> p e i", e=E)))
            for b in range(B):
                ts = slice(b * TB, (b + 1) * TB)
                dve.wait_ge(S("gap_exp"), b + 1)
                st(dve.tensor_scalar(W12[:, 0, ts], W12[:, 1, ts], 1.0, None, ALU.add))
            st.sync()
            st(dve.tensor_tensor_scan(CUM.rearrange("p e i -> p (e i)"), blk("ones"), TOT.rearrange("p e i -> p (e i)"),
                                      0.0, ALU.mult, ALU.add))
            st(dve.tensor_reduce(NE, TOT, AXX, ALU.add))
            st.sync()
            st(dve.tensor_scalar(NEI, NE, float(P - 1), None, ALU.add))
            st(dve.tensor_tensor(CUM, CUM, TOT, ALU.subtract))
            st.sync()
            st(dve.tensor_scalar(NEI, NEI, P.bit_length() - 1, None, ALU.logical_shift_right))
            st(dve.reciprocal(W12[:, 0, :], W12[:, 0, :]))
            st.sync()
            dve.tensor_tensor(W12[:, 1, :], W12[:, 1, :], W12[:, 0, :], ALU.mult).then_inc(S("choice_weights"), 1)
            st.sync()
            st(dve.tensor_tensor_scan(TEC, blk("ones")[:, 0:E], NEI, 0.0, ALU.mult, ALU.add))
            st.sync()
            st(dve.tensor_tensor(OFF, TEC, NEI, ALU.subtract))
            st.sync()
            st(dve.scalar_tensor_tensor(out=OFF, in0=OFF, scalar=float(P), in1=CUM[:, :, 0], op0=ALU.mult,
                                        op1=ALU.subtract))
            st.sync()
            st(dve.tensor_tensor(CUM, CUM, OFF.unsqueeze(2).to_broadcast([P, E, NT]), ALU.add))
            st(dve.tensor_tensor(EXC, blk("iota")[:, 0:NSP].unsqueeze(2).to_broadcast([P, NSP, E]),
                                 TEC.unsqueeze(1).to_broadcast([P, NSP, E]), ALU.is_ge))
            st.sync()
            st(dve.tensor_tensor(BASE, CUM.rearrange("p e i -> p i e"),
                                 bank[0][:, 0:NT * E].rearrange("p (i e) -> p i e", e=E), ALU.add))
            st(dve.tensor_reduce(EXT, EXC, AXX, ALU.add))
            st.sync()
            st(dve.tensor_tensor(PPOS.rearrange("p (k i) e -> p k i e", k=2), CHO,
                                 BASE.unsqueeze(1).to_broadcast([P, 2, NT, E]), ALU.mult))
            st(dve.tensor_scalar(EXI[:, :], EXT, float(E - 1), None, ALU.min))
            st.sync()
            st(dve.tensor_reduce(POS, PPOS, AXX, ALU.add))
            st.sync()
            st(dve.tensor_copy(POSI, POS))
            st.sync()
            st(dve.tensor_scalar(LOI, POSI, P - 1, None, ALU.bitwise_and))
            st(dve.tensor_scalar(HII, POSI, P.bit_length() - 1, None, ALU.logical_shift_right))
            st.sync()
            dve.tensor_tensor(HOH, blk("iota")[:, 0:NSP].unsqueeze(1).to_broadcast([P, 2 * NT, NSP]),
                              HII.unsqueeze(2).to_broadcast([P, 2 * NT, NSP]), ALU.is_equal)\
               .then_inc(S("tile_onehots"), 1)
            dve.wait_ge(S("tile_onehots"), 1)
            dve.wait_ge(S("weight_parts"), 1)
            for v in range(3):
                dve.tensor_tensor(HVAL[:, :, 2 + v, :], HOH, WPT[:, v, :].unsqueeze(2).to_broadcast([P, 2 * NT, NSP]),
                                  ALU.mult).then_inc(S("pair_weights"), 1)
            for k in range(4):
                ns = slice(k * NT // 2, (k + 1) * NT // 2)
                dve.tensor_tensor(LOH[:, ns, :], blk("iota").unsqueeze(1).to_broadcast([P, NT // 2, P]),
                                  LOI[:, ns].unsqueeze(2).to_broadcast([P, NT // 2, P]), ALU.is_equal)\
                   .then_inc(S("onehots_ready"), 1)
            for k in range(2):
                st(dve.memset(EG[k][:, FI:FIP], 0.0))
                st(dve.memset(EU[k][:, FI:FIP], 0.0))
            dve.wait_ge(S("table_filled"), 1)
            st(dve.tensor_copy(TAB, bank[2][:, 0:5 * NSP].rearrange("p (v t) -> p v t", t=NSP)))
            st.sync()
            st(dve.scalar_tensor_tensor(out=PAIR, in0=TAB[:, 0, :], scalar=float(P), in1=TAB[:, 1, :], op0=ALU.mult,
                                        op1=ALU.add))
            st(dve.tensor_tensor(SLOTW, TAB[:, 2, :], TAB[:, 3, :], ALU.add))
            st.sync()
            dve.tensor_tensor(SLOTW, SLOTW, TAB[:, 4, :], ALU.add).then_inc(S("slot_weights"), 1)
            st(dve.tensor_scalar(EMPTY, PAIR, 0.0, None, ALU.is_equal))
            st.sync()
            st(dve.tensor_tensor(EXT, EMPTY, PAIR, ALU.add))
            st(dve.tensor_tensor(EMPTY, EMPTY, blk("slots")[:, 0:NSP], ALU.mult))
            st.sync()
            st(dve.tensor_scalar(GIX[:, :].bitcast(I32), EXT, -1.0, None, ALU.add))
            st(dve.scalar_tensor_tensor(out=SIX[:, :].bitcast(I32), in0=PAIR, scalar=-1.0, in1=EMPTY, op0=ALU.add,
                                        op1=ALU.add))
            st.sync()
            dve.tensor_scalar(GIX[:, :].bitcast(I32), GIX[:, :].bitcast(I32), B * T - 1, None, ALU.bitwise_and)\
               .then_inc(S("slots_ready"), 1)

            st(dve.tensor_tensor(X[:, :, :], X[:, :, :], SH[:, :].unsqueeze(2).to_broadcast([P, NT, C]), ALU.subtract))

            def load_expert(t):
                e = dve.value_load(EXI[0:1, t:t + 1], min_val=0, max_val=E - 1)
                if t >= 2:
                    dve.wait_ge(S("up_filled"), t - 1)
                for src, dst in ((WG, EG), (WU, EU)):
                    dve.tensor_copy(dst[t % 2][:, 0:FI], src[:, :, :].rearrange("p e f -> p (e f)")[:, bass.ds(e * FI, FI)])\
                       .then_inc(S("expert_loaded"), 1)

            load_expert(0)
            for s in range(NS + 1):
                if s < NS:
                    dve.wait_ge(S("x_turned"), s + 1)
                    if s >= 2:
                        dve.wait_ge(S("up_filled"), s - 1)
                    dve.tensor_copy(XC[s % 2], bank[s % 2][:, FIP:]).then_inc(S("xc_ready"), 1)
                if s >= 1:
                    t = s - 1
                    dve.wait_ge(S("silu_done"), t + 1)
                    dve.wait_ge(S("up_filled"), t + 1)
                    if t >= 2:
                        dve.wait_ge(S("down_done"), t - 1)
                    dve.tensor_tensor(HT[t % 2], SL[t % 2], bank[2 + t % 2][:, 0:FIP], ALU.mult)\
                       .then_inc(S("hidden_ready"), 1)
                if s + 1 < NS:
                    load_expert(s + 1)
            for c in range(NCH):
                ts = slice(c * TPC, (c + 1) * TPC)
                dve.wait_ge(S(f"y_loaded{c}"), 32)
                st(dve.tensor_tensor(YK[0][:, ts, :], YK[0][:, ts, :], YK[1][:, ts, :], ALU.add))
                st.sync()
                for i in range(c * TPC, (c + 1) * TPC):
                    st(dve.bn_stats(ST[:, i, :], YK[0][:, i, :]))
            st.sync()
            add_ln(both, lambda i: YK[0][:, i, :], None)

        @block.scalar
        def _(act):
            for c in range(NCH):
                b, q = c // QPB, c % QPB
                act.wait_ge(S("xa_transposed"), c + 1)
                if c == 0:
                    act.wait_ge(S("vec_loaded"), 16)
                act.activation(XS[:, b, 1 + q * CH:1 + (q + 1) * CH], bank[c][:, :], ACT.Identity,
                               bias=vec("b1"), scale=vec("g1")).then_inc(S("xa_evacuated"), 1)
            for n in range(12):
                b, q, kind = n // 6, n % 6 // 3, n % 3
                act.wait_ge(S("kvr_filled"), n + 1)
                dst = (Kc, Vc, SR)[kind][b][:, q * CH:(q + 1) * CH]
                act.activation(dst, bank[(4 + n) % 8][:, :], ACT.Sigmoid if kind == 2 else ACT.Identity)\
                   .then_inc(S("kvr_evacuated"), 1)
            for b in range(B):
                act.wait_ge(S(f"d_ready{b}"), 1)
                act.activation(EA[b], EA[b], ACT.Exp)
                act.activation(EB[b], EB[b], ACT.Exp, scale=-1.0).then_inc(S(f"ab_exp{b}"), 1)
            for b in range(B):
                act.wait_ge(S(f"s_ready{b}"), 1)
                act.activation(Kc[b], SS[b][:, 0:T], ACT.Ln).then_inc(S(f"log_s{b}"), 1)
            for b in range(B):
                act.wait_ge(S(f"z_ready{b}"), 1)
                act.activation(EA[b], EA[b], ACT.Exp)
                act.activation(EB[b], EB[b], ACT.Exp, scale=-1.0).then_inc(S(f"e_exp{b}"), 1)
            act.mul(OMV[:, 0:1], vec("u"), -1.0).then_inc(S("minus_u"), 1)
            act.wait_ge(S("minus_u"), 1)
            for b in range(B):
                act.activation(SG[b], DD[b], ACT.Sigmoid, bias=OMV[:, 0:1]).then_inc(S(f"sig_z{b}"), 1)
            for c in range(NCH):
                b, q = c // QPB, c % QPB
                act.wait_ge(S("xb_transposed"), c + 1)
                act.activation(XS[:, b, 1 + q * CH:1 + (q + 1) * CH], bank[4 + c][:, :], ACT.Identity,
                               bias=vec("b2"), scale=vec("g2")).then_inc(S("xb_evacuated"), 1)
            for c in range(NCH):
                for j in range(4):
                    m = 4 * c + j
                    act.wait_ge(S("kc_filled"), m + 1)
                    if m >= 4:
                        act.wait_ge(S("kc_ready"), m - 3)
                    act.activation(RL[m % 4], bank[m % 4][:, :], ACT.Relu).then_inc(S("relu_done"), 1)
                    if m >= 8:
                        act.wait_ge(S("vc_ready"), c - 1)
                    act.wait_ge(S("relu_done"), m + 1)
                    act.activation(KC[m % 8], RL[m % 4], ACT.Square).then_inc(S("kc_ready"), 1)
                act.wait_ge(S("cr_filled"), c + 1)
                if c >= 2:
                    act.wait_ge(S("vc_used"), c - 1)
                act.activation(SCR[c % 2], bank[6 + c % 2][:, :], ACT.Sigmoid).then_inc(S("cr_sigmoid"), 1)
            act.wait_ge(S("gate_bias_ready"), 1)
            for b in range(B):
                for q in range(QPB):
                    c = QPB * b + q
                    act.wait_ge(S("l_transposed"), c + 1)
                    act.activation(CT[:, c * CH:(c + 1) * CH], bank[c][:, :], ACT.Identity)\
                       .then_inc(S("l_evacuated"), 1)
                for q in range(QPB):
                    for g in range(3):
                        n = 6 * b + 3 * q + g
                        act.wait_ge(S("gates_filled"), n + 1)
                        dst = (FG, IGT, GG)[g][QPB * b + q]
                        bias = GB0[:, g:g + 1] if b == 0 else vec(("bf", "bi", "bc")[g])
                        act.activation(dst, bank[4 + n % 4][:, :], ACT.Tanh if g == 2 else ACT.Sigmoid, bias=bias)\
                           .then_inc(S("gates_done"), 1)
            for c in range(NCH):
                act.wait_ge(S("h_filled"), c + 1)
                act.activation(HH[:, c * TPC:(c + 1) * TPC, :].rearrange("p i c -> p (i c)"), bank[c][:, :],
                               ACT.Tanh).then_inc(S("h_ready"), 1)
            def part(k, n):
                parts = PARTS[n % 4]
                if k == 0:
                    act.wait_ge(*roped(n))
                    if n >= 4:
                        act.wait_ge(S(f"parts_stored{n % 4}"), STORED[n % 4] * (n // 4))
                    act.activation(parts[:, 0, :], RT1[n], ACT.Identity).then_inc(S("part0_ready"), 1)
                else:
                    act.wait_ge(S("rest_ready"), n + 1)
                    act.activation(parts[:, 1, :], RT2[n], ACT.Identity).then_inc(S("part1_ready"), 1)

            for c in range(NCH):
                act.wait_ge(S("a_transposed"), c + 1)
                act.activation(CT[:, c * CH:(c + 1) * CH], bank[4 + c][:, :], ACT.Identity)\
                   .then_inc(S("a_evacuated"), 1)
            def take_v(c):
                if c == 0:
                    act.wait_ge(S("v_cleared"), 1)
                act.wait_ge(S("v_filled"), c + 1)
                act.activation(VS[:, c * TPC:(c + 1) * TPC, :, 0:D],
                               bank[(4 * NCH + c) % 7][:, :].rearrange("p (t h d) -> p t h d", h=H, d=D), ACT.Identity)\
                   .then_inc(S("v_ready"), 1)

            for n in range(2 * NCH + 1):
                if n < 2 * NCH:
                    part(0, n)
                if n >= 1:
                    part(1, n - 1)
                if n >= 2 * NCH - 3:
                    take_v(n - (2 * NCH - 3))

            def take_side(op):
                if op[0] == "scores":
                    return
                act.wait_ge(S("side_filled"), side_at[op] + 1)
                o = side_bank(op)
                if op[0] == "maxima":
                    if op[1] >= 1:
                        act.wait_ge(S("maxima_placed"), 16 * op[1])
                    ins = act.activation(M3T[:, :], o[:, :].bitcast(BF16)[0:3 * NM, 0:P], ACT.Identity)
                elif op[0] == "output":
                    if op[1] >= 2:
                        act.wait_ge(S("output_placed"), op[1] - 1)
                    v = o[:, :].rearrange("p (t j e) -> p t j e", j=HG, e=32)
                    ins = act.activation(OC[op[1] % 2], v[:, :, :, 0:D + 1], ACT.Identity)
                elif op[0] == "turn":
                    c = op[1]
                    ins = act.activation(CT[:, c * CH:(c + 1) * CH], o[:, :], ACT.Identity)
                else:
                    c = op[1]
                    if c == QPB:
                        act.wait_ge(S("m_in_ready0"), 2)
                    ins = act.activation(PO[:, c % QPB * TPC:(c % QPB + 1) * TPC, :].rearrange("p i c -> p (i c)"),
                                         o[:, :], ACT.Identity)
                ins.then_inc(side_used(op)[0], 1)

            def evacuate(rnd):
                act.wait_ge(S("av_steps"), TB * (rnd + 1))
                if rnd >= 1:
                    act.wait_ge(S("side_filled"), side_at[("output", rnd - 1)] + 1)
                act.activation(OE, bank[6 + rnd % 2][:, :], ACT.Identity).then_inc(S("o_evacuated"), 1)

            for op in BEFORE:
                take_side(op)
            for k in range(4):
                act.wait_ge(S(f"parts_stored{k}"), 2 * STORED[k])
            for u in range(NU):
                act.wait_ge(S("scores_filled"), u + 1)
                if u >= NPT:
                    act.wait_ge(S("av_steps"), (u - NPT) // HG + 1)
                act.activation(PT[u % NPT], bank[3 + u % NRING][:, :], ACT.Exp, scale=SCALE)\
                   .then_inc(S("exp_done"), 1)
                for op in at_unit.get(u, ()):
                    take_side(op)
                if u % UNITS == 4 and u >= UNITS:
                    evacuate(u // UNITS - 1)
            evacuate(ROUNDS - 1)

            def take_m(b):
                for c in range(QPB * b, QPB * (b + 1)):
                    act.wait_ge(S("m_transposed"), c + 1)
                    act.activation(CT[:, c * CH:(c + 1) * CH], bank[(3, 4, 6, 7)[c]][:, :], ACT.Identity)\
                       .then_inc(S("m_evacuated"), 1)

            take_m(0)
            for op in at_unit[NU]:
                take_side(op)
            take_m(1)
            for b in range(B):
                act.wait_ge(S("logit_gap"), b + 1)
                ts = slice(b * TB, (b + 1) * TB)
                act.activation(W12[:, 1, ts], W12[:, 1, ts], ACT.Exp).then_inc(S("gap_exp"), 1)
            for s in range(NS + 1):
                if s < NS:
                    act.wait_ge(S("gate_filled"), s + 1)
                    if s >= 2:
                        act.wait_ge(S("hidden_ready"), s - 1)
                    act.activation(SL[s % 2], bank[s % 2][:, 0:FIP], ACT.Silu).then_inc(S("silu_done"), 1)
                if s >= 1:
                    t = s - 1
                    act.wait_ge(S("down_done"), t + 1)
                    if t >= NX:
                        act.wait_ge(S(f"written{t % NX}"), 16 * (t // NX))
                    if t == 0:
                        act.wait_ge(S("slot_weights"), 1)
                    act.activation(YG[t % NX], bank[6 + t % 2][:, 0:P], ACT.Identity,
                                   scale=SLOTW[:, t:t + 1]).then_inc(S("tile_scaled"), 1)

        @block.tensor
        def _(pe):
            def transposes(src, c, dst, sem):
                for j in range(TPC):
                    ins = pe.transpose(dst[:, j * P:(j + 1) * P], src(c * TPC + j), ident)
                ins.then_inc(S(sem), 1)

            def tm(i):
                return TM[:, i, :]

            pe.wait_ge(S("w1_loaded"), 16)
            for b in range(B):
                pe.wait_ge(S(f"xa_ready{b}"), 2)
                for q in range(QPB):
                    transposes(tm, QPB * b + q, bank[QPB * b + q], "xa_transposed")
            for n in range(3 * NCH):
                pe.wait_ge(S("mixed_kvr"), n + 1)
                if n >= 8:
                    pe.wait_ge(S("kvr_evacuated"), n - 7)
                elif n >= 4:
                    pe.wait_ge(S("xa_evacuated"), n - 3)
                pe.matmul(bank[(4 + n) % 8][:, :], blk(("wk", "wv", "wr")[n % 3]), XM[n % 8], start=True, stop=True)\
                  .then_inc(S("kvr_filled"), 1)
            pe.wait_ge(S("w2_loaded"), 32)
            pe.wait_ge(S("kvr_evacuated"), 12)
            for g, name in enumerate(("uf", "ui", "uc")):
                ins = pe.matmul(bank[4][:, g:g + 1], blk(name), vec("in_c"), start=True, stop=True)
            ins.then_inc(S("uc0_ready"), 1)
            for b in range(B):
                pe.wait_ge(S(f"y_ready{b}"), 1)
                for q in range(QPB):
                    transposes(lambda i: EB[b][:, (i - b * TB) * P:(i - b * TB + 1) * P], QPB * b + q,
                               bank[QPB * b + q], "y_transposed")
            for b in range(B):
                pe.wait_ge(S(f"xb_ready{b}"), 2)
                for q in range(QPB):
                    transposes(tm, QPB * b + q, bank[4 + QPB * b + q], "xb_transposed")

            def kc_in(c):
                pe.wait_ge(S("mixed_cm"), 2 * c + 2)
                for j in range(4):
                    m = 4 * c + j
                    if m >= 4:
                        pe.wait_ge(S("relu_done"), m - 3)
                    pe.matmul(bank[m % 4][:, :], blk(f"wck{j}"), XKR[2 * c], start=True, stop=True)\
                      .then_inc(S("kc_filled"), 1)
                if c == 0:
                    pe.wait_ge(S("xb_evacuated"), NCH)
                if c >= 2:
                    pe.wait_ge(S("cr_sigmoid"), c - 1)
                for i in range(TPC):
                    ins = pe.matmul(bank[6 + c % 2][:, i * P:(i + 1) * P], XKR[2 * c + 1][:, i * P:(i + 1) * P],
                                    blk("wcr"), start=True, stop=True)
                ins.then_inc(S("cr_filled"), 1)

            def kc_out(c):
                pe.wait_ge(S("kc_ready"), 4 * c + 4)
                if c >= 2:
                    pe.wait_ge(S("vc_used"), c - 1)
                for i in range(TPC):
                    for j in range(4):
                        ins = pe.matmul(bank[4 + c % 2][:, i * P:(i + 1) * P], KC[(4 * c + j) % 8][:, i * P:(i + 1) * P],
                                        blk(f"wcv{j}"), start=j == 0, stop=j == 3)
                ins.then_inc(S("vc_ready"), 1)

            for c in range(NCH + 1):
                if c < NCH:
                    kc_in(c)
                if c >= 1:
                    kc_out(c - 1)

            pe.wait_ge(S("biases_ready"), 1)
            pe.wait_ge(S("cr_sigmoid"), NCH)
            pe.wait_ge(S("relu_done"), 4 * NCH)
            pe.wait_ge(S("vc_used"), NCH)
            pe.wait_ge(S("gate_bias_ready"), 1)
            def h_input(c):
                pe.matmul(bank[c][:, :], R3[:, :], bias("bo"), start=True, stop=False)
                for i in range(TPC):
                    pe.matmul(bank[c][:, i * P:(i + 1) * P], CT[:, c * CH + i * P:c * CH + (i + 1) * P], blk("wo"),
                              start=False, stop=False)

            for b in range(B):
                pe.wait_ge(S(f"l_in_ready{b}"), 2)
                for q in range(QPB):
                    transposes(tm, QPB * b + q, bank[QPB * b + q], "l_transposed")
                for q in range(QPB):
                    c = QPB * b + q
                    pe.wait_ge(S("l_evacuated"), c + 1)
                    if b == 1:
                        pe.wait_ge(S("cell_ready"), q + 1)
                    for g, (wn, un) in enumerate((("wf", "uf"), ("wi", "ui"), ("wc", "uc"))):
                        n = 6 * b + 3 * q + g
                        if n >= 4:
                            pe.wait_ge(S("gates_done"), n - 3)
                        o = bank[4 + n % 4][:, :]
                        ins = pe.matmul(o, blk(wn), CT[:, c * CH:(c + 1) * CH], start=True, stop=b == 0)
                        if b == 1:
                            ins = pe.matmul(o, blk(un), CST[0][:, q * CH:(q + 1) * CH], start=False, stop=True)
                        ins.then_inc(S("gates_filled"), 1)
                for q in range(QPB):
                    h_input(QPB * b + q)
            for c in range(NCH):
                q = c % QPB
                pe.wait_ge(S("cell_ready"), QPB + q + 1)
                for i in range(TPC):
                    at = q * CH + i * P
                    ins = pe.matmul(bank[c][:, i * P:(i + 1) * P], CST[1][:, at:at + P], blk("uo"), start=False,
                                    stop=i == TPC - 1)
                ins.then_inc(S("h_filled"), 1)

            def qk_in(c):
                pe.wait_ge(S("a_evacuated"), c + 1)
                names = ("aq", "aqr", "ak", "akr") if c % 2 == 0 else ("ak", "akr", "aq", "aqr")
                for k, name in enumerate(names):
                    m = 4 * c + k
                    if m >= 7:
                        pe.wait_ge(S("qk_used"), m - 6)
                    elif m >= 4:
                        pe.wait_ge(S("a_evacuated"), m - 3)
                    pe.matmul(bank[m % 7][:, :], blk(name), CT[:, c * CH:(c + 1) * CH], start=True, stop=True)\
                      .then_inc(S("qk_filled"), 1)

            for c in range(NCH):
                if c % QPB == 0:
                    pe.wait_ge(S(f"a_in_ready{c // QPB}"), 2)
                transposes(tm, c, bank[4 + c], "a_transposed")
            for c in range(NCH):
                qk_in(c)
            for c in range(NCH):
                m = 4 * NCH + c
                pe.wait_ge(S("qk_used"), m - 6)
                pe.matmul(bank[m % 7][:, :], R3[:, :], bias("bv"), start=True, stop=False)
                for i in range(TPC):
                    o = bank[m % 7][:, i * P:(i + 1) * P]
                    ins = pe.matmul(o, CT[:, c * CH + i * P:c * CH + (i + 1) * P], blk("av"), start=False,
                                    stop=i == TPC - 1)
                ins.then_inc(S("v_filled"), 1)
            pe.wait_ge(S("qk_used"), 4 * NCH)
            pe.wait_ge(S("ident_bf16"), 1)

            def side(op):
                n = side_at[op]
                if n >= NRING:
                    pe.wait_ge(*side_used(every[n - NRING]))
                elif n == 2:
                    pe.wait_ge(S("v_ready"), 1)
                o = side_bank(op)
                if op[0] == "scores":
                    _, rnd, j, qt, kk = op
                    g, half = rnd // QPB, rnd % QPB
                    if (j, qt, kk) == (0, 0, 0):
                        if half == 0:
                            pe.wait_ge(S(f"stacks_loaded{g % 2}"), 32 * (g // 2 + 1))
                        else:
                            pe.wait_ge(S(f"second_loaded{g % 2}"), 16 * (g // 2 + 1))
                    ins = pe.matmul(o[:, :], QS[0:MROW, g % 2, half, j, qt * P:(qt + 1) * P],
                                    KS[0:MROW, g % 2, j, kk * CH:(kk + 1) * CH], start=True, stop=True)
                elif op[0] == "maxima":
                    pe.wait_ge(S("maxima_ready"), op[1] + 1)
                    ins = pe.transpose(o[:, :].bitcast(BF16)[0:3 * NM, 0:P],
                                       M3[:, :, :].rearrange("p s m -> p (s m)"), IDB[:, :])
                elif op[0] == "output":
                    pe.wait_ge(S("o_evacuated"), op[1] + 1)
                    for t in range(TPC):
                        ins = pe.transpose(o[:, t * P:(t + 1) * P], OE[:, t * P:(t + 1) * P], ident)
                elif op[0] == "turn":
                    c = op[1]
                    pe.wait_ge(S("output_placed"), NG * QPB * (c // QPB + 1))
                    for t in range(TPC):
                        ins = pe.transpose(o[:, t * P:(t + 1) * P], OT[:, c * TPC + t, :], ident)
                else:
                    c = op[1]
                    pe.wait_ge(*side_used(("turn", c)))
                    pe.matmul(o[:, :], R3[:, :], bias("bao"), start=True, stop=False)
                    for i in range(TPC):
                        oi = o[:, i * P:(i + 1) * P]
                        ins = pe.matmul(oi, CT[:, c * CH + i * P:c * CH + (i + 1) * P], blk("ao"), start=False,
                                        stop=i == TPC - 1)
                ins.then_inc(S("side_filled"), 1)

            def scores(u):
                rnd, kt, j = u // UNITS, u % UNITS // HG, u % HG
                g = rnd // QPB
                if u % UNITS == 0:
                    pe.wait_ge(S("maxima_placed"), 16 * (rnd + 1))
                if u >= NRING:
                    pe.wait_ge(S("exp_done"), u - NRING + 1)
                elif u == 0:
                    pe.wait_ge(S("v_ready"), NCH)
                pe.matmul(bank[3 + u % NRING][:, :], KS[:, g % 2, j, kt * P:(kt + 1) * P],
                          QS[:, g % 2, rnd % QPB, j, :], start=True, stop=True).then_inc(S("scores_filled"), 1)

            def weigh(k):
                rnd, kt = k // TB, k % TB
                g = rnd // QPB
                pe.wait_ge(S("exp_done"), HG * (k + 1))
                if kt == 0 and rnd >= 2:
                    pe.wait_ge(S("o_evacuated"), rnd - 1)
                for j in range(HG):
                    ins = pe.matmul(bank[6 + rnd % 2][32 * j:32 * (j + 1), :],
                                    VS[:, g // NG * TB + kt, g % NG * HG + j, :], PT[(HG * k + j) % NPT],
                                    start=kt == 0, stop=kt == TB - 1)
                ins.then_inc(S("av_steps"), 1)

            for op in BEFORE:
                side(op)
            for u in range(NU):
                scores(u)
                for op in at_unit.get(u, ()):
                    side(op)
                if u % HG == 2 and u >= HG:
                    weigh(u // HG - 1)
            weigh(NU // HG - 1)

            def router(b):
                pe.wait_ge(S(f"m_in_ready{b}"), 2)
                if b == 0:
                    pe.wait_ge(S("exp_done"), NU)
                    pe.wait_ge(S("moe_loaded"), 64)
                else:
                    pe.wait_ge(S("o_evacuated"), ROUNDS)
                for c in range(QPB * b, QPB * (b + 1)):
                    transposes(tm, c, bank[(3, 4, 6, 7)[c]], "m_transposed")
                for i in range(b * TB, (b + 1) * TB):
                    if i % TPC == 0:
                        pe.wait_ge(S("m_evacuated"), i // TPC + 1)
                    ins = pe.matmul(bank[(5, 3)[b]][:, (i % TB) * E:(i % TB + 1) * E], CT[:, i * P:(i + 1) * P],
                                    WRT[:, :], start=True, stop=True)
                ins.then_inc(S("router_filled"), 1)

            router(0)
            for op in at_unit[NU]:
                side(op)

            router(1)
            pe.wait_ge(S("choices_ready"), B)
            chosen = CHS.rearrange("p i e -> p (i e)")
            pe.matmul(bank[0][:, 0:NT * E], blk("tri"), chosen, start=True, stop=True)
            pe.matmul(bank[1][:, 0:NT * E], blk("ones"), chosen, start=True, stop=True).then_inc(S("counts_filled"), 1)
            for n in range(2 * NT):
                if n % (NT // 2) == 0:
                    pe.wait_ge(S("onehots_ready"), n // (NT // 2) + 1)
                if n == 0:
                    pe.wait_ge(S("pair_numbers"), 2)
                    pe.wait_ge(S("pair_weights"), 3)
                ins = pe.matmul(bank[2][:, 0:5 * NSP], LOH[:, n, :], HVAL[:, n, :, :].rearrange("p v t -> p (v t)"),
                                start=n == 0, stop=n == 2 * NT - 1)
            ins.then_inc(S("table_filled"), 1)

            def turn_x(t):
                pe.wait_ge(S(f"gathered{t % NX}"), 16 * (t // NX + 1))
                if t >= 2:
                    pe.wait_ge(S("silu_done"), t - 1)
                pe.transpose(bank[t % 2][:, FIP:], XG[t % NX], ident).then_inc(S("x_turned"), 1)

            turn_x(0)
            for s in range(NS + 1):
                if s < NS:
                    pe.wait_ge(S("xc_ready"), s + 1)
                    pe.wait_ge(S("expert_loaded"), 2 * s + 2)
                    for j in range(NF):
                        js = slice(j * P, (j + 1) * P)
                        ins = pe.matmul(bank[s % 2][:, js], EG[s % 2][:, js], XC[s % 2], start=True, stop=True)
                    ins.then_inc(S("gate_filled"), 1)
                    if s >= 2:
                        pe.wait_ge(S("hidden_ready"), s - 1)
                    for j in range(NF):
                        js = slice(j * P, (j + 1) * P)
                        ins = pe.matmul(bank[2 + s % 2][:, js], EU[s % 2][:, js], XC[s % 2], start=True, stop=True)
                    ins.then_inc(S("up_filled"), 1)
                    if s + 1 < NS:
                        turn_x(s + 1)
                if s >= 1:
                    t = s - 1
                    e = pe.value_load(EXI[0:1, t:t + 1], min_val=0, max_val=E - 1)
                    pe.wait_ge(S("hidden_ready"), t + 1)
                    if t >= 2:
                        pe.wait_ge(S("tile_scaled"), t - 1)
                    for j in range(NF):
                        ins = pe.matmul(bank[6 + t % 2][:, 0:P], HT[t % 2][:, j * P:(j + 1) * P],
                                        WD[:, :, :, :].rearrange("p e j c -> p (e j c)")[:, bass.ds(e * (NF * C) + j * C, C)],
                                        start=j == 0, stop=j == NF - 1)
                    ins.then_inc(S("down_done"), 1)


_N_OUT = (B, T, C)


def _laid_out(f):
    import numpy as np

    f = {k: np.asarray(v, np.float32) for k, v in f.items()}
    a, l, n = "L0_attn_", "L0_ffn_", "L1_attn_"
    turn = (np.arange(C) // D) * D + (np.arange(C) % D + D // 2) % D
    w = {"wk": f[a + "Wk"].T, "wv": f[a + "Wv"].T, "wr": f[a + "Wr"].T, "wcr": f[a + "Wcr"].T,
         "wf": f[l + "wf"].T, "wi": f[l + "wi"].T, "wc": f[l + "wc"].T, "uf": f[l + "uf"].T, "ui": f[l + "ui"].T,
         "uc": f[l + "uc"].T, "wo": f[l + "wo"].T, "uo": f[l + "uo"].T, "aq": f[n + "Wq"].T, "aqr": f[n + "Wq"][turn].T,
         "ak": f[n + "Wk"].T, "akr": f[n + "Wk"][turn].T, "av": f[n + "Wv"].T, "ao": f[n + "Wo"].T,
         "ident": np.eye(C, dtype=np.float32)}
    for j in range(4):
        w[f"wck{j}"] = f[a + "Wck"].T[:, j * C:(j + 1) * C]
        w[f"wcv{j}"] = f[a + "Wcv"].T[j * C:(j + 1) * C]
    w["rows3"] = np.zeros((C, C), np.float32)
    w["rows3"][0:3] = 1.0
    w["ones"] = np.ones((C, C), np.float32)
    w["tri"] = np.triu(np.ones((C, C), np.float32), 1)
    w["iota"] = np.tile(np.arange(C, dtype=np.float32), (C, 1))
    part, pair = np.arange(P)[:, None], np.arange(2 * NT)[None]
    w["slots"] = np.zeros((C, C), np.float32)
    w["slots"][:, 0:NSP] = 1 + NPAIR + np.arange(NSP)[None] * P + part
    w["slots"][:, NSP:NSP + 2 * NT] = pair
    w["slots"][:, NSP + 2 * NT:] = 0
    w["slots"][:, NSP + 2 * NT:NSP + 4 * NT] = 1 + part
    v = {"w": f[a + "w"], "u": f[a + "u"], "rk": f[a + "rk"], "rv": f[a + "rv"], "rr": f[a + "rr"],
         "crk": f[a + "crk"], "crr": f[a + "crr"], "g1": f[a + "ln1_g"], "b1": f[a + "ln1_b"], "g2": f[a + "ln2_g"],
         "b2": f[a + "ln2_b"], "bf": f[l + "bf"], "bi": f[l + "bi"], "bc": f[l + "bc"], "in_c": f[l + "in_c"],
         "bq": f[n + "bq"], "bqr": f[n + "bq"][turn], "bk": f[n + "bk"], "bkr": f[n + "bk"][turn]}
    v.update({f"e{k}": np.eye(C, dtype=np.float32)[k] for k in range(3)})
    rows = np.zeros((C, len(ROWS) * C), np.float32)
    for k, b in enumerate((f[l + "bo"], f[n + "bv"], f[n + "bo"])):
        rows[0:3, k * C:(k + 1) * C] = b
    inv = (1.0 / 10000.0 ** (np.arange(0, D, 2, dtype=np.float32) / np.float32(D))).astype(np.float32)
    ang = np.arange(T, dtype=np.float32)[:, None] * inv[None, :]
    ang = np.concatenate([ang, ang], 1).T
    sign = np.where(np.arange(D) < D // 2, -1.0, 1.0).astype(np.float32)[:, None]
    wd = np.zeros((C, E, NF, C), np.float32)
    down = f["L1_ffn_w_down"]
    for j in range(NF):
        part = down[:, :, j * C:(j + 1) * C]
        wd[:part.shape[2], :, j, :] = part.transpose(2, 0, 1)
    return {
        "x": f["L0_attn_x"],
        "wt": np.concatenate([w[k] for k in BLOCKS], 1),
        "vec": np.stack([v[k] for k in VECS], 1),
        "rows": rows,
        "cos": np.tile(np.cos(ang).astype(np.float32), (H, 1)),
        "sin": np.tile((np.sin(ang) * sign).astype(np.float32), (H, 1)),
        "wg": f["L1_ffn_w_gate"].transpose(2, 0, 1),
        "wu": f["L1_ffn_w_up"].transpose(2, 0, 1),
        "wd": wd,
        "wrt": f["L1_ffn_w_router"].T,
    }


def kernel(**inputs):
    import numpy as np
    import concourse.bacc as bacc
    from concourse.bass_utils import run_bass_kernel_spmd

    nc = bacc.Bacc("TRN2", target_bir_lowering=False, num_devices=1)
    arrays, args = {}, []
    for name, a in _laid_out(inputs).items():
        a = np.ascontiguousarray(a)
        arrays[f"in_{name}"] = a
        args.append(nc.dram_tensor(f"in_{name}", a.shape, mybir.dt.from_np(a.dtype), kind="ExternalInput").ap())
    args.append(nc.dram_tensor("out_x", _N_OUT, F32, kind="ExternalOutput").ap())
    sandwich_kernel(nc, *args)
    r = run_bass_kernel_spmd(nc, [arrays], core_ids=[0])
    return r.results[0]["out_x"]
```
